# Optimizing a Trainium2 kernel written in Bass

```python
import numpy as np
import jax
import jax.numpy as jnp

def _softmax(x, axis=-1):
    return jax.nn.softmax(x, axis=axis)

def _gelu(x):
    return jax.nn.gelu(x, approximate=True)

def _silu(x):
    return jax.nn.silu(x)

def _sigmoid(x):
    return jax.nn.sigmoid(x)

def _layernorm(x, axis=-1, eps=1e-05):
    m = jnp.mean(x, axis=axis, keepdims=True)
    v = jnp.var(x, axis=axis, keepdims=True)
    return (x - m) / jnp.sqrt(v + eps)

def _scatter_add(tgt, idx, src, axis=0):
    return tgt.at[idx].add(src)

def _segment_sum(src, seg, n):
    return jax.ops.segment_sum(src, seg, n)
kernel_name = 'mk_decoder_preln_d2_seqx_r8_9c5384'

def setup_inputs(seed: int=0):
    np.random.seed(seed)
    _w = jnp.asarray

    def _rec_inputs():
        import jax
        import jax.numpy as jnp
        _rk = jax.random.key(seed)
        x = -0.0003929 + 0.9999 * jax.random.normal(jax.random.fold_in(_rk, 1), (16, 56, 256), jnp.float32)
        _lenS = 56 - jax.random.randint(jax.random.fold_in(_rk, 7), (16,), 0, max(1, 56 // 4) + 1, jnp.int32)
        _lenS2 = 1500 - jax.random.randint(jax.random.fold_in(_rk, 8), (16,), 0, max(1, 1500 // 4) + 1, jnp.int32)
        _ctx_1024P = jax.random.normal(jax.random.fold_in(_rk, 11), (16, 16, 128), jnp.float32)
        _ctx_1024c = jax.random.dirichlet(jax.random.fold_in(_rk, 511), 0.3 * jnp.ones((16,), jnp.float32), (16, 1500))
        _ctx_1024t = jnp.einsum('bsk,bkd->bsd', _ctx_1024c, _ctx_1024P)
        _ctx_1024t = _ctx_1024t * jax.lax.rsqrt(jnp.mean(jnp.square(_ctx_1024t)) + 1e-12) * 0.953939
        ctx_1024 = 0.000227908 + 0.99994 * (_ctx_1024t + 0.3 * jax.random.normal(jax.random.fold_in(_rk, 611), (16, 1500, 128), jnp.float32))
        return (x, ctx_1024)
    x, ctx_1024 = _rec_inputs()

    def _L0_attn_setup():
        import jax, jax.numpy as jnp
        import numpy as np
        import math
        B, S, D, H = (4, 256, 256, 16)
        HD = D // H

        def _alibi_slopes(n_heads):
            return jnp.asarray([2.0 ** (-8.0 / n_heads * (h + 1)) for h in range(n_heads)], dtype=jnp.float32)
        key = jax.random.key(seed)
        ks = jax.random.split(key, 10)
        w = lambda k: jax.random.normal(k, (D, D), dtype=jnp.float32) * 0.02
        b = lambda k: jax.random.normal(k, (D,), dtype=jnp.float32) * 0.01
        return {'hidden_states': jax.random.normal(ks[0], (B, S, D), dtype=jnp.float32), 'Wq': w(ks[1]), 'bq': b(ks[2]), 'Wk': w(ks[3]), 'bk': b(ks[4]), 'Wv': w(ks[5]), 'bv': b(ks[6]), 'Wo': w(ks[7]), 'bo': b(ks[8]), 'alibi_slopes': _alibi_slopes(H)}
    _L0_attn_all = _L0_attn_setup()
    _L0_attn_in = {k: v for k, v in _L0_attn_all.items() if k in ('Wq', 'bq', 'Wk', 'bk', 'Wv', 'bv', 'Wo', 'bo', 'alibi_slopes')}
    del _L0_attn_all

    def _L0_xattn_setup():
        import jax, jax.numpy as jnp
        import numpy as np
        EPS = 1e-05

        def rmsnorm(x, g, eps=EPS):
            var = jnp.mean(jnp.square(x), axis=-1, keepdims=True)
            return x * jax.lax.rsqrt(var + eps) * g
        key = jax.random.key(seed)
        ks = jax.random.split(key, 8)
        B, Sq, Skv = (2, 512, 64)
        dim, cdim, H, D = (256, 128, 16, 128)
        inner = H * D
        s = lambda f: 1.0 / np.sqrt(f)
        return {'hidden_states': jax.random.normal(ks[0], (B, Sq, dim), jnp.float32), 'encoder_hidden_states': jax.random.normal(ks[1], (B, Skv, cdim), jnp.float32), 'Wq': jax.random.normal(ks[2], (dim, inner), jnp.float32) * s(dim), 'Wk': jax.random.normal(ks[3], (cdim, inner), jnp.float32) * s(cdim), 'Wv': jax.random.normal(ks[4], (cdim, inner), jnp.float32) * s(cdim), 'Wo': jax.random.normal(ks[5], (inner, dim), jnp.float32) * s(inner), 'gq': jnp.ones((D,), jnp.float32), 'gk': jnp.ones((D,), jnp.float32)}
    _L0_xattn_all = _L0_xattn_setup()
    _L0_xattn_in = {k: v for k, v in _L0_xattn_all.items() if k in ('Wq', 'Wk', 'Wv', 'Wo', 'gq', 'gk')}
    del _L0_xattn_all

    def _L0_ffn_setup():
        import math
        import jax, jax.numpy as jnp
        import numpy as np
        DIM = 256
        RANK = 8
        B, T = (4, 512)

        def _orthogonal(key, n):
            a = jax.random.normal(key, (n, n), dtype=jnp.float32)
            q, r = jnp.linalg.qr(a)
            q = q * jnp.sign(jnp.diagonal(r))[None, :]
            return q
        key = jax.random.key(seed)
        kx, kf = jax.random.split(key)
        x = jax.random.normal(kx, (B, T, DIM), dtype=jnp.float32)
        fkeys = jax.random.split(kf, RANK)
        factors = jnp.stack([_orthogonal(fkeys[r], DIM) * (r + 1) ** (-0.5) for r in range(RANK)])
        bias = jnp.zeros((DIM,), dtype=jnp.float32)
        return {'x': x, 'factors': factors, 'bias': bias}
    _L0_ffn_all = _L0_ffn_setup()
    _L0_ffn_in = {k: v for k, v in _L0_ffn_all.items() if k in ('factors', 'bias')}
    del _L0_ffn_all

    def _L1_attn_setup():
        import jax, jax.numpy as jnp
        import numpy as np
        EMB = 256
        HEADS = 16
        G = 2
        HEAD_DIM = EMB // HEADS
        KV = HEADS // G
        B = 2
        S = 256

        def compute_rope(x):
            D = x.shape[2]
            half = D // 2
            inv_freq = 1.0 / 10000.0 ** (jnp.arange(0, half, dtype=jnp.float32) * 2.0 / D)
            pos = jnp.arange(x.shape[1], dtype=jnp.float32)
            ang = pos[:, None] * inv_freq[None, :]
            cos = jnp.concatenate([jnp.cos(ang), jnp.cos(ang)], axis=-1)[None, :, :, None]
            sin = jnp.concatenate([jnp.sin(ang), jnp.sin(ang)], axis=-1)[None, :, :, None]
            x1, x2 = (x[:, :, :half], x[:, :, half:])
            rot = jnp.concatenate([-x2, x1], axis=2)
            return x * cos + rot * sin
        key = jax.random.key(seed)
        ks = jax.random.split(key, 5)
        sc = 0.02
        return {'x': jax.random.normal(ks[0], (B, S, EMB), dtype=jnp.float32), 'W_Q': jax.random.normal(ks[1], (EMB, EMB), dtype=jnp.float32) * sc, 'W_K': jax.random.normal(ks[2], (EMB // G, EMB), dtype=jnp.float32) * sc, 'W_V': jax.random.normal(ks[3], (EMB // G, EMB), dtype=jnp.float32) * sc, 'W_O': jax.random.normal(ks[4], (EMB, EMB), dtype=jnp.float32) * sc}
    _L1_attn_all = _L1_attn_setup()
    _L1_attn_in = {k: v for k, v in _L1_attn_all.items() if k in ('W_Q', 'W_K', 'W_V', 'W_O')}
    del _L1_attn_all

    def _L1_xattn_setup():
        import jax, jax.numpy as jnp
        import numpy as np
        B, S1, S2, DCA = (2, 256, 128, 16)
        QDIM, KDIM, H = (256, 128, 16)
        HD = QDIM // H
        SCALE = HD ** (-0.5)
        EPS = 1e-06
        DCA_WEIGHT = 1.0

        def _ln(t, w, b):
            m = jnp.mean(t, axis=-1, keepdims=True)
            v = jnp.var(t, axis=-1, keepdims=True)
            return (t - m) * jax.lax.rsqrt(v + EPS) * w + b

        def _attn(q, k, v):
            s = jnp.einsum('bhqd,bhkd->bhqk', q, k) * SCALE
            p = jax.nn.softmax(s, axis=-1)
            return jnp.einsum('bhqk,bhkd->bhqd', p, v)
        key = jax.random.key(seed)
        ks = jax.random.split(key, 8)
        w = lambda k, shape: jax.random.normal(k, shape, jnp.float32) * 0.02
        return {'x': jax.random.normal(ks[0], (B, S1, QDIM), jnp.float32), 'y': jax.random.normal(ks[1], (B, S2 + DCA, KDIM), jnp.float32), 'Wq': w(ks[2], (QDIM, QDIM)), 'bq': jnp.zeros((QDIM,), jnp.float32), 'Wk': w(ks[3], (KDIM, QDIM)), 'bk': jnp.zeros((QDIM,), jnp.float32), 'Wv': w(ks[4], (KDIM, QDIM)), 'bv': jnp.zeros((QDIM,), jnp.float32), 'Wkv_dca': w(ks[5], (KDIM, 2 * QDIM)), 'bkv_dca': jnp.zeros((2 * QDIM,), jnp.float32), 'qn_w': jnp.ones((HD,), jnp.float32), 'qn_b': jnp.zeros((HD,), jnp.float32), 'kn_w': jnp.ones((HD,), jnp.float32), 'kn_b': jnp.zeros((HD,), jnp.float32), 'kn_dca_w': jnp.ones((HD,), jnp.float32), 'kn_dca_b': jnp.zeros((HD,), jnp.float32), 'Wo': w(ks[6], (QDIM, QDIM)), 'bo': jnp.zeros((QDIM,), jnp.float32)}
    _L1_xattn_all = _L1_xattn_setup()
    _L1_xattn_in = {k: v for k, v in _L1_xattn_all.items() if k in ('Wq', 'bq', 'Wk', 'bk', 'Wv', 'bv', 'Wkv_dca', 'bkv_dca', 'qn_w', 'qn_b', 'kn_w', 'kn_b', 'kn_dca_w', 'kn_dca_b', 'Wo', 'bo')}
    del _L1_xattn_all

    def _L1_ffn_setup():
        import jax, jax.numpy as jnp
        import numpy as np
        H = 256
        E = 16
        I = 64
        IS = 256
        TOP_K = 2
        B, S = (1, 256)
        key = jax.random.key(seed)
        ks = jax.random.split(key, 9)
        std = 0.02
        return {'hidden_states': jax.random.normal(ks[0], (B, S, H), dtype=jnp.float32), 'gate_w': jax.random.normal(ks[1], (E, H), dtype=jnp.float32) * std, 'w1': jax.random.normal(ks[2], (E, I, H), dtype=jnp.float32) * std, 'w2': jax.random.normal(ks[3], (E, H, I), dtype=jnp.float32) * std, 'w3': jax.random.normal(ks[4], (E, I, H), dtype=jnp.float32) * std, 'ws_gate': jax.random.normal(ks[5], (IS, H), dtype=jnp.float32) * std, 'ws_up': jax.random.normal(ks[6], (IS, H), dtype=jnp.float32) * std, 'ws_down': jax.random.normal(ks[7], (H, IS), dtype=jnp.float32) * std, 'shared_gate_w': jax.random.normal(ks[8], (1, H), dtype=jnp.float32) * std}
    _L1_ffn_all = _L1_ffn_setup()
    _L1_ffn_in = {k: v for k, v in _L1_ffn_all.items() if k in ('gate_w', 'w1', 'w2', 'w3', 'ws_gate', 'ws_up', 'ws_down', 'shared_gate_w')}
    del _L1_ffn_all
    return {'x': x, 'ctx_1024': ctx_1024, 'L0_attn_Wq': _L0_attn_in['Wq'], 'L0_attn_bq': _L0_attn_in['bq'], 'L0_attn_Wk': _L0_attn_in['Wk'], 'L0_attn_bk': _L0_attn_in['bk'], 'L0_attn_Wv': _L0_attn_in['Wv'], 'L0_attn_bv': _L0_attn_in['bv'], 'L0_attn_Wo': _L0_attn_in['Wo'], 'L0_attn_bo': _L0_attn_in['bo'], 'L0_attn_alibi_slopes': _L0_attn_in['alibi_slopes'], 'L0_xattn_Wq': _L0_xattn_in['Wq'], 'L0_xattn_Wk': _L0_xattn_in['Wk'], 'L0_xattn_Wv': _L0_xattn_in['Wv'], 'L0_xattn_Wo': _L0_xattn_in['Wo'], 'L0_xattn_gq': _L0_xattn_in['gq'], 'L0_xattn_gk': _L0_xattn_in['gk'], 'L0_ffn_factors': _L0_ffn_in['factors'], 'L0_ffn_bias': _L0_ffn_in['bias'], 'L1_attn_W_Q': _L1_attn_in['W_Q'], 'L1_attn_W_K': _L1_attn_in['W_K'], 'L1_attn_W_V': _L1_attn_in['W_V'], 'L1_attn_W_O': _L1_attn_in['W_O'], 'L1_xattn_Wq': _L1_xattn_in['Wq'], 'L1_xattn_bq': _L1_xattn_in['bq'], 'L1_xattn_Wk': _L1_xattn_in['Wk'], 'L1_xattn_bk': _L1_xattn_in['bk'], 'L1_xattn_Wv': _L1_xattn_in['Wv'], 'L1_xattn_bv': _L1_xattn_in['bv'], 'L1_xattn_Wkv_dca': _L1_xattn_in['Wkv_dca'], 'L1_xattn_bkv_dca': _L1_xattn_in['bkv_dca'], 'L1_xattn_qn_w': _L1_xattn_in['qn_w'], 'L1_xattn_qn_b': _L1_xattn_in['qn_b'], 'L1_xattn_kn_w': _L1_xattn_in['kn_w'], 'L1_xattn_kn_b': _L1_xattn_in['kn_b'], 'L1_xattn_kn_dca_w': _L1_xattn_in['kn_dca_w'], 'L1_xattn_kn_dca_b': _L1_xattn_in['kn_dca_b'], 'L1_xattn_Wo': _L1_xattn_in['Wo'], 'L1_xattn_bo': _L1_xattn_in['bo'], 'L1_ffn_gate_w': _L1_ffn_in['gate_w'], 'L1_ffn_w1': _L1_ffn_in['w1'], 'L1_ffn_w2': _L1_ffn_in['w2'], 'L1_ffn_w3': _L1_ffn_in['w3'], 'L1_ffn_ws_gate': _L1_ffn_in['ws_gate'], 'L1_ffn_ws_up': _L1_ffn_in['ws_up'], 'L1_ffn_ws_down': _L1_ffn_in['ws_down'], 'L1_ffn_shared_gate_w': _L1_ffn_in['shared_gate_w']}

def reference(x, ctx_1024, L0_attn_Wq, L0_attn_bq, L0_attn_Wk, L0_attn_bk, L0_attn_Wv, L0_attn_bv, L0_attn_Wo, L0_attn_bo, L0_attn_alibi_slopes, L0_xattn_Wq, L0_xattn_Wk, L0_xattn_Wv, L0_xattn_Wo, L0_xattn_gq, L0_xattn_gk, L0_ffn_factors, L0_ffn_bias, L1_attn_W_Q, L1_attn_W_K, L1_attn_W_V, L1_attn_W_O, L1_xattn_Wq, L1_xattn_bq, L1_xattn_Wk, L1_xattn_bk, L1_xattn_Wv, L1_xattn_bv, L1_xattn_Wkv_dca, L1_xattn_bkv_dca, L1_xattn_qn_w, L1_xattn_qn_b, L1_xattn_kn_w, L1_xattn_kn_b, L1_xattn_kn_dca_w, L1_xattn_kn_dca_b, L1_xattn_Wo, L1_xattn_bo, L1_ffn_gate_w, L1_ffn_w1, L1_ffn_w2, L1_ffn_w3, L1_ffn_ws_gate, L1_ffn_ws_up, L1_ffn_ws_down, L1_ffn_shared_gate_w):
    import jax
    import jax.numpy as jnp

    def _L0_attn_ref(hidden_states, Wq, bq, Wk, bk, Wv, bv, Wo, bo, alibi_slopes):
        import jax, jax.numpy as jnp
        import numpy as np
        import math
        B, S, D, H = (4, 256, 256, 16)
        HD = D // H

        def _alibi_slopes(n_heads):
            return jnp.asarray([2.0 ** (-8.0 / n_heads * (h + 1)) for h in range(n_heads)], dtype=jnp.float32)
        Bn, t, _ = hidden_states.shape
        split = lambda x: x.reshape(Bn, t, H, HD).transpose(0, 2, 1, 3)
        q = split(hidden_states @ Wq.T + bq)
        k = split(hidden_states @ Wk.T + bk)
        v = split(hidden_states @ Wv.T + bv)
        scores = jnp.einsum('bhsd,bhtd->bhst', q, k)
        pos = jnp.arange(t)
        rel = (pos[None, :] - pos[:, None]).astype(scores.dtype)
        bias = alibi_slopes[:, None, None] * rel
        scores = (scores + bias[None]) / math.sqrt(HD)
        scores = 30.0 * jnp.tanh(scores / 30.0)
        causal = pos[:, None] >= pos[None, :]
        scores = jnp.where(causal[None, None], scores, -jnp.inf)
        probs = jax.nn.softmax(scores, axis=-1)
        ctx = jnp.einsum('bhst,bhtd->bhsd', probs, v)
        ctx = ctx.transpose(0, 2, 1, 3).reshape(Bn, t, D)
        return ctx @ Wo.T + bo

    def _L0_xattn_ref(hidden_states, encoder_hidden_states, Wq, Wk, Wv, Wo, gq, gk):
        import jax, jax.numpy as jnp
        import numpy as np
        EPS = 1e-05

        def rmsnorm(x, g, eps=EPS):
            var = jnp.mean(jnp.square(x), axis=-1, keepdims=True)
            return x * jax.lax.rsqrt(var + eps) * g
        B, Sq, _ = hidden_states.shape
        Skv = encoder_hidden_states.shape[1]
        D = gq.shape[0]
        H = Wq.shape[1] // D
        scale = 1.0 / np.sqrt(D)
        q = (hidden_states @ Wq).reshape(B, Sq, H, D)
        k = (encoder_hidden_states @ Wk).reshape(B, Skv, H, D)
        v = (encoder_hidden_states @ Wv).reshape(B, Skv, H, D)
        q = rmsnorm(q, gq)
        k = rmsnorm(k, gk)
        scores = jnp.einsum('bqhd,bkhd->bhqk', q, k) * scale
        attn = jax.nn.softmax(scores, axis=-1)
        out = jnp.einsum('bhqk,bkhd->bqhd', attn, v)
        out = out.reshape(B, Sq, H * D)
        return out @ Wo

    def _L0_ffn_ref(x, factors, bias):
        import math
        import jax, jax.numpy as jnp
        import numpy as np
        DIM = 256
        RANK = 8
        B, T = (4, 512)

        def _orthogonal(key, n):
            a = jax.random.normal(key, (n, n), dtype=jnp.float32)
            q, r = jnp.linalg.qr(a)
            q = q * jnp.sign(jnp.diagonal(r))[None, :]
            return q
        rank = factors.shape[0]
        mixed = jnp.einsum('btd,rde->bte', x, factors)
        mixed = mixed / math.sqrt(rank) + bias
        return mixed

    def _L1_attn_ref(x, W_Q, W_K, W_V, W_O):
        import jax, jax.numpy as jnp
        import numpy as np
        EMB = 256
        HEADS = 16
        G = 2
        HEAD_DIM = EMB // HEADS
        KV = HEADS // G
        B = 2
        S = 256

        def compute_rope(x):
            D = x.shape[2]
            half = D // 2
            inv_freq = 1.0 / 10000.0 ** (jnp.arange(0, half, dtype=jnp.float32) * 2.0 / D)
            pos = jnp.arange(x.shape[1], dtype=jnp.float32)
            ang = pos[:, None] * inv_freq[None, :]
            cos = jnp.concatenate([jnp.cos(ang), jnp.cos(ang)], axis=-1)[None, :, :, None]
            sin = jnp.concatenate([jnp.sin(ang), jnp.sin(ang)], axis=-1)[None, :, :, None]
            x1, x2 = (x[:, :, :half], x[:, :, half:])
            rot = jnp.concatenate([-x2, x1], axis=2)
            return x * cos + rot * sin
        Bsz, Sl, E = x.shape
        q = (x @ W_Q.T).reshape(Bsz, Sl, HEAD_DIM, HEADS)
        k = (x @ W_K.T).reshape(Bsz, Sl, HEAD_DIM, KV)
        v = (x @ W_V.T).reshape(Bsz, Sl, HEAD_DIM, KV)
        q = compute_rope(q)
        k = compute_rope(k)
        q = q.reshape(Bsz, Sl, HEAD_DIM, KV, G)
        scores = jnp.einsum('bsdkg,btdk->bkgst', q, k) / jnp.sqrt(jnp.float32(E))
        w = jax.nn.softmax(scores, axis=-1)
        ctx = jnp.einsum('bkgst,btdk->bkgsd', w, v)
        ctx = ctx.reshape(Bsz, HEADS, Sl, HEAD_DIM).transpose(0, 2, 1, 3).reshape(Bsz, Sl, E)
        return ctx @ W_O.T

    def _L1_xattn_ref(x, y, Wq, bq, Wk, bk, Wv, bv, Wkv_dca, bkv_dca, qn_w, qn_b, kn_w, kn_b, kn_dca_w, kn_dca_b, Wo, bo):
        import jax, jax.numpy as jnp
        import numpy as np
        B, S1, S2, DCA = (2, 256, 128, 16)
        QDIM, KDIM, H = (256, 128, 16)
        HD = QDIM // H
        SCALE = HD ** (-0.5)
        EPS = 1e-06
        DCA_WEIGHT = 1.0

        def _ln(t, w, b):
            m = jnp.mean(t, axis=-1, keepdims=True)
            v = jnp.var(t, axis=-1, keepdims=True)
            return (t - m) * jax.lax.rsqrt(v + EPS) * w + b

        def _attn(q, k, v):
            s = jnp.einsum('bhqd,bhkd->bhqk', q, k) * SCALE
            p = jax.nn.softmax(s, axis=-1)
            return jnp.einsum('bhqk,bhkd->bhqd', p, v)
        b, s1, _ = x.shape
        y_dca = y[:, -DCA:, :]
        y_main = y[:, :-DCA, :]
        kv_dca = (y_dca @ Wkv_dca + bkv_dca).reshape(b, DCA, 2, H, HD)
        k_dca = _ln(kv_dca[:, :, 0], kn_dca_w, kn_dca_b)
        v_dca = kv_dca[:, :, 1]
        s2 = y_main.shape[1]
        q = _ln((x @ Wq + bq).reshape(b, s1, H, HD), qn_w, qn_b)
        kv = jnp.concatenate([y_main @ Wk + bk, y_main @ Wv + bv], axis=-1)
        kv = kv.reshape(b, s2, H, 2 * HD)
        k = _ln(kv[..., :HD], kn_w, kn_b)
        v = kv[..., HD:]
        qT = q.transpose(0, 2, 1, 3)
        ctx = _attn(qT, k.transpose(0, 2, 1, 3), v.transpose(0, 2, 1, 3))
        ctx = ctx.transpose(0, 2, 1, 3).reshape(b, s1, QDIM)
        ctx_dca = _attn(qT, k_dca.transpose(0, 2, 1, 3), v_dca.transpose(0, 2, 1, 3))
        ctx_dca = ctx_dca.transpose(0, 2, 1, 3).reshape(b, s1, QDIM)
        ctx = ctx + DCA_WEIGHT * ctx_dca
        return ctx @ Wo + bo

    def _L1_ffn_ref(hidden_states, gate_w, w1, w2, w3, ws_gate, ws_up, ws_down, shared_gate_w):
        import jax, jax.numpy as jnp
        import numpy as np
        H = 256
        E = 16
        I = 64
        IS = 256
        TOP_K = 2
        B, S = (1, 256)
        b, s, h = hidden_states.shape
        x = hidden_states.reshape(-1, h)
        T = x.shape[0]
        router_logits = x @ gate_w.T
        routing = jax.nn.softmax(router_logits.astype(jnp.float32), axis=-1)
        topw, sel = jax.lax.top_k(routing, TOP_K)
        topw = topw / jnp.sum(topw, axis=-1, keepdims=True)
        topw = topw.astype(x.dtype)
        combine = jnp.zeros((T, E), dtype=x.dtype).at[jnp.arange(T)[:, None], sel].set(topw)
        hmid = jax.nn.silu(jnp.einsum('th,eih->tei', x, w1)) * jnp.einsum('th,eih->tei', x, w3)
        hmid = hmid * combine[:, :, None]
        moe_out = jnp.einsum('tei,ehi->th', hmid, w2)
        shared = jax.nn.silu(x @ ws_gate.T) * (x @ ws_up.T) @ ws_down.T
        shared = jax.nn.sigmoid(x @ shared_gate_w.T) * shared
        return (moe_out + shared).reshape(b, s, h)
    x = x + _L0_attn_ref(_layernorm(x, axis=-1), L0_attn_Wq, L0_attn_bq, L0_attn_Wk, L0_attn_bk, L0_attn_Wv, L0_attn_bv, L0_attn_Wo, L0_attn_bo, L0_attn_alibi_slopes)
    x = x + _L0_xattn_ref(_layernorm(x, axis=-1), ctx_1024, L0_xattn_Wq, L0_xattn_Wk, L0_xattn_Wv, L0_xattn_Wo, L0_xattn_gq, L0_xattn_gk)
    x = x + _L0_ffn_ref(_layernorm(x, axis=-1), L0_ffn_factors, L0_ffn_bias)
    x = x + _L1_attn_ref(_layernorm(x, axis=-1), L1_attn_W_Q, L1_attn_W_K, L1_attn_W_V, L1_attn_W_O)
    x = x + _L1_xattn_ref(_layernorm(x, axis=-1), ctx_1024, L1_xattn_Wq, L1_xattn_bq, L1_xattn_Wk, L1_xattn_bk, L1_xattn_Wv, L1_xattn_bv, L1_xattn_Wkv_dca, L1_xattn_bkv_dca, L1_xattn_qn_w, L1_xattn_qn_b, L1_xattn_kn_w, L1_xattn_kn_b, L1_xattn_kn_dca_w, L1_xattn_kn_dca_b, L1_xattn_Wo, L1_xattn_bo)
    x = x + _L1_ffn_ref(_layernorm(x, axis=-1), L1_ffn_gate_w, L1_ffn_w1, L1_ffn_w2, L1_ffn_w3, L1_ffn_ws_gate, L1_ffn_ws_up, L1_ffn_ws_down, L1_ffn_shared_gate_w)
    return x

_drawn_inputs = setup_inputs


def setup_inputs(seed=0):
    import zlib

    import numpy as np

    out = dict(_drawn_inputs(seed))
    spreads = {'L0_xattn_gq': (1.0, 0.2),
     'L0_xattn_gk': (1.0, 0.2),
     'L0_ffn_bias': (0.0, 0.1),
     'L1_xattn_bq': (0.0, 0.8),
     'L1_xattn_bk': (0.0, 0.436),
     'L1_xattn_bv': (0.0, 0.47),
     'L1_xattn_bkv_dca': (0.0, 0.295),
     'L1_xattn_qn_w': (1.0, 0.6),
     'L1_xattn_qn_b': (0.0, 0.8),
     'L1_xattn_kn_w': (1.0, 0.6),
     'L1_xattn_kn_b': (0.0, 2.0),
     'L1_xattn_kn_dca_w': (1.0, 0.6),
     'L1_xattn_kn_dca_b': (0.0, 2.0),
     'L1_xattn_bo': (0.0, 0.1)}
    factors = {'L0_attn_Wq': 8.0,
     'L0_attn_bq': 25.85,
     'L0_attn_Wk': 8.0,
     'L0_attn_bk': 64.0,
     'L0_attn_bv': 8.0,
     'L0_attn_bo': 6.518,
     'L0_attn_alibi_slopes': 8.0,
     'L1_attn_W_Q': 8.0,
     'L1_attn_W_K': 8.0,
     'L1_xattn_Wq': 3.183,
     'L1_xattn_Wk': 2.745,
     'L1_xattn_Wv': 2.774,
     'L1_ffn_gate_w': 8.0,
     'L1_ffn_w1': 8.0,
     'L1_ffn_w2': 8.0,
     'L1_ffn_w3': 8.0,
     'L1_ffn_ws_gate': 8.0,
     'L1_ffn_ws_up': 8.0,
     'L1_ffn_ws_down': 8.0,
     'L1_ffn_shared_gate_w': 8.0}
    for name, (base, spread) in spreads.items():
        noise = np.random.default_rng([zlib.crc32(name.encode()), seed]).standard_normal(out[name].shape)
        drawn = base * np.exp(spread * noise) if base else spread * noise
        out[name] = jnp.asarray(drawn.astype(out[name].dtype))
    for name, factor in factors.items():
        out[name] = (out[name] * factor).astype(out[name].dtype)
    return out
```

```python
from contextlib import ExitStack

import numpy as np

import concourse.bass as bass
from concourse import mybir
from concourse.alu_op_type import AluOpType as ALU

ACT = mybir.ActivationFunctionType
AX = mybir.AxisListType
F32 = mybir.dt.float32
U32 = mybir.dt.uint32

P = 128
B, S, D = 16, 56, 256
R = 2 * S
NT = B // 2
G = 2
SL = 64
H, HD = 16, 16
HM = 8
KC = D // P
W = HM * S
C = 1500
CD = 128
CR = 125
CT = C // CR
NDCA = 16
XD = 128
E, FI = 16, 64
FA = E * FI + D
EW = FA // FI
CHUNK = 3
CREDIT = 2


class Step:

    def __init__(self, sem, n=1):
        self.sem, self.n = sem, n

    def credit(self, eng):
        eng.sem_inc(self.sem, CREDIT * self.n)

    def done(self, index):
        return (index + 1 + CREDIT) * self.n


def wait(eng, step, index):
    eng.wait_ge(step.sem, step.done(index))


def rows_in(layer, t):
    return CR if layer == 0 else min(CR, C - NDCA - t * CR)


class Buffers:

    def __init__(self, T, PT, va, Km, qT, Z, mx, rc, cx, cT):
        self.T, self.PT, self.va, self.Km, self.qT = T, PT, va, Km, qT
        self.Z, self.mx, self.rc, self.cx, self.cT = Z, mx, rc, cx, cT


def build(nc, a, out):
    ctx = ExitStack()
    with ctx:
        def sb(name, shape, dt=F32):
            return ctx.enter_context(nc.sbuf_tensor(name, shape, dt))

        def sem(name):
            return ctx.enter_context(nc.semaphore(name))

        by_engine = {"pe": [], "act": [], "dve": [], "pool": [], "sp": []}

        def step(name, n=1):
            s = Step(sem(name), n)
            by_engine[name.split("_")[0]].append(s)
            return s

        PS = ctx.enter_context(nc.psum_tensor("PS", [P, 8, 512], F32))

        x = sb("x", [P, NT, D])
        ident = sb("ident", [P, P])
        ones = sb("ones", [P, P])
        hmask = sb("hmask", [P, HM])
        cosT = sb("cosT", [P, R])
        sinT = sb("sinT", [P, R])
        causal = sb("causal", [P, S])
        rel = sb("rel", [P, S])
        slopes = sb("slopes", [P, H])
        eidx = sb("eidx", [P, E])
        wq0, wk0, wv0, wo0 = (sb(n, [P, KC, D]) for n in ("wq0", "wk0", "wv0", "wo0"))
        bqk0 = sb("bqk0", [P, 2, KC])
        bv0 = sb("bv0", [P, D])
        rows = sb("rows", [P, D])
        wk_x0 = sb("wk_x0", [P, H * XD])
        gqk = sb("gqk", [P, 2])
        fmix = sb("fmix", [P, KC, D])
        vo = sb("vo", [P, H, D])

        lnst = sb("lnst", [P, G, 6])
        lnmv = sb("lnmv", [P, G, 2])
        lnve = sb("lnve", [P, G])
        lnrs = sb("lnrs", [P, G])
        xn = sb("xn", [P, G, D])
        xT = sb("xT", [P, G, KC, R])
        nhalf = sb("nhalf", [P, 64])

        QREG = B * H * S
        SREG = CT * H * S
        MREG = 7 * H * S
        CREG = 4 * H * S + 1024 + C + CT * CD
        big = sb("big", [P, QREG + SREG + MREG + CREG])
        used = {}

        def region(start, size):
            used[start] = 0

            def take(*shape, dt=None):
                n = int(np.prod(shape))
                at = start + used[start]
                used[start] += n
                assert used[start] <= size, (start, used[start], size)
                v = big[:, at:at + n]
                names = "abcde"[:len(shape)]
                if len(shape) > 1:
                    v = v.rearrange(f"p ({' '.join(names)}) -> p {' '.join(names)}",
                                    **{names[i]: shape[i] for i in range(1, len(shape))})
                return v
            return take

        Q0, S0, M0, C0 = 0, QREG, QREG + SREG, QREG + SREG + MREG

        def attention_buffers(takes, T):
            shapes = dict(PT=(G, H, P), va=(G, 2, H, HD + 1), Km=(G, 2, KC, HM * T), qT=(G, KC, S + SL), Z=(G, H * T),
                          mx=(G, H), rc=(G, H), cx=(G, D), cT=(G, KC, R))
            return Buffers(T=T, **{n: takes[0 if n in ("PT", "va", "Km") else -1](*sh) for n, sh in shapes.items()})

        take = region(Q0, QREG)
        SA = attention_buffers([take], S)
        rope = take(3, KC, R)
        abias = take(H, S)
        take = region(Q0, QREG)
        th = take(G, FA)
        hm = take(G, FA)
        hT = take(G, FA // P, R)
        lg = take(G, H + 1)
        le = take(G, H)
        lm = take(G, 1)
        top = take(G, 8)
        topi = sb("topi", [P, G, 8], U32)
        topf = take(G, 8)
        tw = take(G, 4)
        hot = take(G, 2, E)
        comb = take(G, EW)
        take = region(S0, SREG)
        factors = take(KC * D, 8)
        take = region(S0, SREG)
        w13 = take(KC, 2, FA)
        w2 = take(FA // P, D)
        wr = take(KC, E + 1)
        take = region(S0, SREG)
        wq_x1 = take(KC, D)
        wkv_d = take(2 * D)
        wvT_x1 = take(H, CD)
        woh_x1 = take(H, D)
        wo_x1 = take(KC, D)
        ydT = take(B * NDCA)
        kTd = take(KC, B * NDCA)
        bq_x1 = take(D)
        bkv_d = take(2 * D)
        qs = take(G, D)
        sq1a = take(G, D)
        mean = take(2 * D // HD)
        take = region(M0, MREG)
        take_c = region(C0, CREG)
        DCA = attention_buffers([take, take_c], NDCA)
        kd = take_c(2, D)
        yds = take_c(G, 2 * NDCA)
        ss1a = take_c(G, H)
        rs1a = take_c(G, H)

        take = region(S0, SREG)
        wq_x0 = take(KC, H * XD)
        wkT_x0 = take(H, CD)
        wvT_x0 = take(H, CD)
        take = region(M0, MREG)
        wo_x0 = take(H, D)
        take = region(C0, CREG)
        sq_a = take(H * XD)
        qhT = take(H, R)
        ss_a = take(G, H)
        rq_a = take(G, H)
        qn_a = take(H, XD)
        take = region(Q0 + 0, QREG)
        Qall = take(B, 2, W)
        take = region(S0, SREG)
        Sall = take(CT, 2 * W)
        take = region(M0, MREG)
        Mx = take(2 * W)
        Mb = take(2 * W)
        Zs = take(2 * W)
        Pr = take(3, 2 * W)
        rz = take(2 * W)
        take = region(C0, CREG)
        Dr = take(2, 2 * W)
        sqr = take(2, 512)
        cxT = take(C)
        cxn = take(CT, CD)
        ssr = sb("ssr", [P, 2, H])
        vek = sb("vek", [P, 2, H])
        rkr = sb("rkr", [P, 2, H])
        mcol = sb("mcol", [P, 8])
        mdiag = sb("mdiag", [P, 7, P])
        take = region(M0, MREG)
        OTs = take(G, H, R)
        flat = vo[:, :, :].rearrange("p h d -> p (h d)")
        wq1 = flat[:, 0:2 * KC * D].rearrange("p (k n) -> p k n", k=KC)
        wk1 = flat[:, 2 * KC * D:3 * KC * D].rearrange("p (k n) -> p k n", k=KC)
        wv1 = flat[:, 3 * KC * D:3 * KC * D + KC * P].rearrange("p (k n) -> p k n", k=KC)
        wo1 = flat[:, 3 * KC * D + KC * P:4 * KC * D + KC * P].rearrange("p (k n) -> p k n", k=KC)
        wk_x1 = wk_x0[:, 0:D]
        bk_x1 = wk_x0[:, D:2 * D]
        KT = wk_x0[:, 2 * D:2 * D + 4 * CR].rearrange("p (n m r) -> p n m r", n=2, m=KC)
        lncol = wk_x0[:, 3 * D + 256:3 * D + 262]
        bvcol = wk_x0[:, 3 * D + 264:3 * D + 266]

        sp_const = sem("sp_const")
        sp_x = sem("sp_x")
        sp_w0 = sem("sp_w0")
        sp_wx0 = sem("sp_wx0")
        sp_fac = sem("sp_fac")
        sp_w1 = sem("sp_w1")
        sp_out = sem("sp_out")
        pool_init = sem("pool_init")
        pe_beat, dve_beat, pool_beat = sem("pe_beat"), sem("dve_beat"), sem("pool_beat")
        dve_setup = sem("dve_setup")
        dve_x = step("dve_x")
        dve_stats, dve_aggr, dve_xn = step("dve_stats"), step("dve_aggr"), step("dve_xn")
        pool_ve, pool_rs = step("pool_ve"), step("pool_rs")
        pe_xT, act_xT = step("pe_xT"), step("act_xT")
        pe_y = step("pe_y")
        pe_q, pe_k, pe_v = step("pe_q"), step("pe_k"), step("pe_v")
        act_q = step("act_q", KC)
        dve_km0, dve_km1 = step("dve_km0", 4), step("dve_km1", 2)
        dve_va = step("dve_va")
        dve_rope, dve_qk1 = step("dve_rope", 4), step("dve_qk1", 2)
        pe_s, dve_mx, dve_z = step("pe_s"), step("dve_mx"), step("dve_z")
        act_tanh, act_e, dve_p = step("act_tanh"), step("act_e"), step("dve_p")
        pe_pT, act_pT, dve_pT = step("pe_pT"), step("act_pT"), step("dve_pT")
        pe_o, dve_rc, dve_cx = step("pe_o"), step("dve_rc"), step("dve_cx")
        pe_cT, act_cT = step("pe_cT"), step("act_cT")
        pe_qx, act_sqa, dve_ssa = step("pe_qx"), step("act_sqa"), step("dve_ssa")
        pool_vea, pool_rqa = step("pool_vea"), step("pool_rqa")
        dve_qh = step("dve_qh")
        pe_qhT, act_qhT, pe_qt, dve_qt = step("pe_qhT"), step("act_qhT"), step("pe_qt"), step("dve_qt")
        pe_vo, dve_vo = step("pe_vo"), step("dve_vo")
        sp_cxT = [step(f"sp_cxT{c}", 16) for c in range(CT // CHUNK)]
        sp_cxn = [step(f"sp_cxn{c}", 16) for c in range(CT // CHUNK)]
        pe_kp, act_sq, dve_ss = step("pe_kp"), step("act_sq"), step("dve_ss")
        pool_vek, pool_rk = step("pool_vek"), step("pool_rk")
        pe_sx, dve_t, dve_mxr = step("pe_sx"), step("dve_t"), step("dve_mxr")
        pool_d, act_p, dve_sum, pe_pv = step("pool_d"), step("act_p"), step("dve_sum"), step("pe_pv")
        pe_mT, dve_mcol, dve_diag, pe_mb, act_mb = (
            step("pe_mT"), step("dve_mcol", 2), step("dve_diag"), step("pe_mb"), step("act_mb"))
        pe_den, dve_rz, dve_ot = step("pe_den"), step("dve_rz"), step("dve_ot")
        act_ots, pool_ots = step("act_ots"), step("pool_ots")
        sp_wx1, pe_kd, dve_kd, act_kd, pool_kd, pe_kdT = (
            sem("sp_wx1"), sem("pe_kd"), sem("dve_kd"), sem("act_kd"), sem("pool_kd"), sem("pe_kdT"))
        pe_q1, dve_qs, act_q1s, dve_q1ss = step("pe_q1"), step("dve_qs"), step("act_q1s"), step("dve_q1ss")
        pool_q1v, pool_q1r, dve_q1n, pe_q1T = step("pool_q1v"), step("pool_q1r"), step("dve_q1n"), step("pe_q1T")
        act_q1, dve_q1m, dve_kmd, pool_yd = step("act_q1"), step("dve_q1m", 4), step("dve_kmd", 4), step("pool_yd")
        pe_k1, dve_k1c, act_k1s, dve_k1ss = step("pe_k1"), step("dve_k1c"), step("act_k1s"), step("dve_k1ss")
        pool_k1v, pool_k1r, dve_k1n, pe_k1T, act_k1T = (
            step("pool_k1v"), step("pool_k1r"), step("dve_k1n"), step("pe_k1T"), step("act_k1T"))
        act_t = step("act_t")
        sp_moe = sem("sp_moe")
        pe_lg, dve_lg, dve_lm, dve_le, act_le = step("pe_lg"), step("dve_lg"), step("dve_lm"), step("dve_le"), step("act_le", 2)
        dve_top, dve_topi, dve_topf, dve_tw, dve_hot, dve_comb = (
            step("dve_top"), step("dve_topi"), step("dve_topf"), step("dve_tw", 3), step("dve_hot", 2), step("dve_comb", 2))
        pe_h, act_th, dve_h, pe_hT, act_hT, dve_hT = (
            step("pe_h"), step("act_th"), step("dve_h", 3), step("pe_hT"), step("act_hT"), step("dve_hT"))

        block = ctx.enter_context(nc.Block())

        @block.sync
        def _(sp):
            for s in by_engine["sp"]:
                s.credit(sp)
            sp.dma_start(x[0:R, :, :], a["x"].rearrange("(j r) c -> r j c", r=R)).then_inc(sp_x, 16)
            for dst, name in ((ident, "ident"), (wq0, "wq0"), (wk0, "wk0"), (wv0, "wv0"), (bqk0, "bqk0")):
                sp.dma_start(dst[:], a[name]).then_inc(sp_w0, 16)
            sp.dma_start(bv0[:, :], a["bv0"].partition_broadcast(P)).then_inc(sp_w0, 16)
            for dst, name in ((hmask, "hmask"), (causal, "causal"), (rel, "rel"), (wo0, "wo0"), (cosT, "cosT"), (sinT, "sinT"), (eidx, "eidx")):
                sp.dma_start(dst[:], a[name]).then_inc(sp_w0, 16)
            sp.dma_start(rows[0:P:32, :], a["rows"]).then_inc(sp_w0, 16)
            sp.dma_start(slopes[:, :], a["slopes"].partition_broadcast(P)).then_inc(sp_w0, 16)
            for dst, name in ((wq_x0, "wq_x0"), (wkT_x0, "wkT_x0"), (wvT_x0, "wvT_x0"), (wo_x0, "wo_x0"),
                              (wk_x0, "wk_x0"), (gqk, "gqk")):
                sp.dma_start(dst[:], a[name]).then_inc(sp_wx0, 16)

            def context(X):
                def part(b, c):
                    span = slice(c * CHUNK * CR, (c + 1) * CHUNK * CR)
                    sp.dma_start(cxT[:, span], a["ctxT"][b, :, span]).then_inc(sp_cxT[c].sem, 16)

                def part_rows(b, c):
                    span = slice(c * CHUNK * CR, (c + 1) * CHUNK * CR)
                    sp.dma_start(cxn[0:CR, c * CHUNK:(c + 1) * CHUNK, :],
                                 a["ctx"][b, span, :].rearrange("(t r) c -> r t c", r=CR)).then_inc(sp_cxn[c].sem, 16)

                for c in range(CT // CHUNK):
                    part(0, c)
                    part_rows(0, c)
                with sp.Fori(1, B) as b:
                    for c in range(CT // CHUNK):
                        used = (X * B + b - 1) * CT + CHUNK * c + CHUNK - 1
                        wait(sp, pe_sx, used)
                        part(b, c)
                    for c in range(CT // CHUNK):
                        used = (X * B + b - 1) * CT + CHUNK * c + CHUNK - 1
                        wait(sp, pe_pv, used)
                        part_rows(b, c)

            wait(sp, pe_qt, 4 * NT - 1)
            context(0)
            wait(sp, dve_ot, B - 1)
            sp.dma_start(factors, a["factors"]).then_inc(sp_fac, 16)
            wait(sp, pe_y, 2 * NT - 1)
            for dst, name in ((wq1, "wq1"), (wk1, "wk1"), (wv1, "wv1"), (wo1, "wo1")):
                sp.dma_start(dst, a[name]).then_inc(sp_w1, 16)
            sp.wait_ge(dve_setup, 4)
            for dst, name in ((wq_x1, "wq_x1"), (wkv_d, "wkv_d"), (wo_x1, "wo_x1"), (ydT, "ydT"),
                              (wk_x1, "wk_x1"), (lncol, "lncol"), (bvcol, "bvcol")):
                sp.dma_start(dst, a[name]).then_inc(sp_wx1, 16)
            sp.dma_start(wvT_x1[0:HD], a["wvT_x1"]).then_inc(sp_wx1, 16)
            sp.dma_start(woh_x1[0:HD], a["woh_x1"]).then_inc(sp_wx1, 16)
            for dst, name in ((bq_x1, "bq_x1"), (bkv_d, "bkv_d"), (bk_x1, "bk_x1")):
                sp.dma_start(dst, a[name].partition_broadcast(P)).then_inc(sp_wx1, 16)
            wait(sp, dve_x, 5 * NT - 1)
            context(1)
            wait(sp, dve_ot, 2 * B - 1)
            for dst, name in ((w13, "w13"), (w2, "w2"), (wr, "wr")):
                sp.dma_start(dst, a[name]).then_inc(sp_moe, 16)

            wait(sp, dve_x, 7 * NT - 1)
            sp.dma_start(out.rearrange("(j r) c -> r j c", r=R), x[0:R, :, :]).then_inc(sp_out, 16)
            sp.wait_ge(sp_out, 16)

        @block.tensor
        def _(pe):
            for s in by_engine["pe"]:
                s.credit(pe)

            def norm_T(js, L):
                for g, j in enumerate(js):
                    wait(pe, dve_xn, L + j)
                    wait(pe, act_xT, L + j - 1)
                    for k in range(KC):
                        ins = pe.transpose(PS[:, 0, k * R:(k + 1) * R], xn[0:R, g, k * P:(k + 1) * P],
                                           ident[0:R, 0:R])
                    ins.then_inc(pe_xT.sem, 1)

            def attention(js, U, V, J, ready, wout, row):
                T = V.T
                for g, j in enumerate(js):
                    for s, n in ready:
                        wait(pe, s, n + j)
                    wait(pe, dve_z, U + j - 1)
                    for b in range(2):
                        for m in range(KC):
                            ins = pe.matmul(PS[SL * b:SL * b + SL, 3 + m, 0:HM * T], V.qT[:, g, m, S * b:S * b + SL],
                                            V.Km[:, g, b, 0 if U == NT else m],
                                            start=True, stop=True)
                    ins.then_inc(pe_s.sem, 1)
                for g, j in enumerate(js):
                    if U == 0:
                        wait(pe, dve_p, j)
                    else:
                        wait(pe, act_e, U + j)
                    for n in range(4):
                        wait(pe, (act_pT, dve_pT)[n % 2], (U + j) * 2 + n // 2 - 1)
                        pe.sem_inc(pe_beat, 1)
                        for h in range(4):
                            s0 = (4 * n + h) * T
                            ins = pe.transpose(PS[0:T, 5 + n % 2, h * P:(h + 1) * P], V.Z[:, g, s0:s0 + T],
                                               ident[:, :])
                        ins.then_inc(pe_pT.sem, 1)
                for g, j in enumerate(js):
                    wait(pe, act_pT, (U + j) * 2 + 1)
                    wait(pe, dve_pT, (U + j) * 2 + 1)
                    wait(pe, dve_va, U + j)
                    wait(pe, dve_cx, U + j - 1)
                    pe.sem_inc(pe_beat, 1)
                    for b in range(2):
                        for h in range(H):
                            vh = h % HM if U == NT else h
                            ins = pe.matmul(PS[SL * b:SL * b + SL, 7, h * (HD + 1):(h + 1) * (HD + 1)],
                                            V.PT[0:T, g, h, SL * b:SL * b + SL], V.va[0:T, g, b, vh, :],
                                            start=True, stop=True, skip_group_check=True)
                    ins.then_inc(pe_o.sem, 1)
                for g, j in enumerate(js):
                    wait(pe, dve_cx, U + j)
                    wait(pe, act_cT, U + j - 1)
                    for k in range(KC):
                        ins = pe.transpose(PS[:, 0, k * P:(k + 1) * P], V.cx[:, g, k * P:(k + 1) * P], ident[:, :])
                    ins.then_inc(pe_cT.sem, 1)
                for g, j in enumerate(js):
                    wait(pe, act_cT, U + j)
                    project(j, J, [V.cT[:, g, k] for k in range(KC)], [wout[:, k, :] for k in range(KC)], row)

            def project(j, J, left, right, row):
                wait(pe, dve_x, J + j - 1)
                for n, (le, ri) in enumerate(zip(left, right)):
                    ins = pe.matmul(PS[0:R, 2, 0:D], le, ri, start=(n == 0), stop=(row is None and n == len(left) - 1))
                if row is not None:
                    ins = pe.matmul(PS[0:R, 2, 0:D], ones[32 * row:32 * row + 1, 0:R], rows[32 * row:32 * row + 1, :], start=False, stop=True)
                ins.then_inc(pe_y.sem, 1)

            pe.wait_ge(sp_w0, 15 * 16)
            pe.wait_ge(pool_init, 4)
            with pe.Fori(0, NT // G) as i:
                js = [i * G + g for g in range(G)]
                norm_T(js, 0)
                for g, j in enumerate(js):
                    wait(pe, act_xT, j)
                    wait(pe, act_q, j - 1)
                    for m in range(KC):
                        for k in range(KC):
                            ins = pe.matmul(PS[:, 1, m * R:(m + 1) * R], wq0[:, k, m * P:(m + 1) * P],
                                            xT[:, g, k], start=(k == 0), stop=(k == KC - 1))
                    ins.then_inc(pe_q.sem, 1)
                    wait(pe, dve_km0, j - 1)
                    wait(pe, dve_cx, i * G - 1)
                    for m in range(KC):
                        for k in range(KC):
                            ins = pe.matmul(PS[:, 7, m * R:(m + 1) * R], wk0[:, k, m * P:(m + 1) * P],
                                            xT[:, g, k], start=(k == 0), stop=(k == KC - 1))
                    ins.then_inc(pe_k.sem, 1)
                    wait(pe, dve_va, j - 1)
                    wait(pe, dve_x, i * G - 1)
                    for b in range(2):
                        for k in range(KC):
                            ins = pe.matmul(PS[0:S, 2, b * D:(b + 1) * D], xT[:, g, k, b * S:(b + 1) * S], wv0[:, k, :],
                                            start=(k == 0), stop=(k == KC - 1))
                    ins.then_inc(pe_v.sem, 1)
                attention(js, 0, SA, 0, [(act_q, 0), (dve_km0, 0)], wo0, 0)

            def value_output(pairs, wvT, wo, V):
                for n in range(H // 2):
                    wait(pe, dve_vo, V + n - 1)
                    for h in range(2):
                        ins = pe.matmul(PS[:, 7, h * D:(h + 1) * D], wvT[0:pairs, 2 * n + h, :], wo[0:pairs, 2 * n + h, :],
                                        start=True, stop=True, skip_group_check=True)
                    ins.then_inc(pe_vo.sem, 1)

            def context_scores(b, t):
                X = 0
                K = (X * B + b) * CT + t
                n_rows = rows_in(X, t)
                tile = cxT[:, t * CR:t * CR + n_rows]
                if t % CHUNK == 0:
                    wait(pe, sp_cxT[t // CHUNK], X * B + b)
                for n in range(4):
                    wait(pe, act_sq, K * 4 + n - 2)
                    pe.matmul(PS[0:n_rows, n % 2, :], tile, wk_x0[:, n * 512:(n + 1) * 512],
                              start=True, stop=True).then_inc(pe_kp.sem, 1)
                wait(pe, dve_t, K - 1)
                for m in range(2):
                    ins = pe.matmul(PS[0:n_rows, 2 + m, 0:W], tile, Qall[:, b, m, :], start=True, stop=True)
                ins.then_inc(pe_sx.sem, 1)

            def weighted_context(X, b, t):
                K = (X * B + b) * CT + t
                n_rows = rows_in(X, t)
                if t % CHUNK == 0:
                    wait(pe, sp_cxn[t // CHUNK], X * B + b)
                if t == 0:
                    wait(pe, dve_ot, X * B + b - 1)
                wait(pe, act_p, K)
                for m in range(2):
                    ins = pe.matmul(PS[:, 4 + m, 0:W], cxn[0:n_rows, t, :], Pr[0:n_rows, t % 3, m * W:(m + 1) * W],
                                    start=(t == 0), stop=(t == CT - 1))
                ins.then_inc(pe_pv.sem, 1)

            def maximum(X, b):
                u = X * B + b
                wait(pe, dve_mxr, u * CT + CT - 1)
                wait(pe, dve_rz, u - 2)
                for q in range(7):
                    ins = pe.transpose(PS[:, 6 + q // 4, (q % 4) * CR:(q % 4 + 1) * CR], Mx[0:CR, q * P:(q + 1) * P],
                                       ident[0:CR, 0:CR])
                ins.then_inc(pe_mT.sem, 1)
                wait(pe, dve_diag, u)
                for m in range(2):
                    ins = pe.matmul(PS[0:CR, 6 + m, 0:W], ones[:, 0:CR],
                                    mdiag[:, :, :].rearrange("p a q -> p (a q)")[:, m * W:(m + 1) * W], start=True, stop=True)
                ins.then_inc(pe_mb.sem, 1)

            def denominators(X, b):
                u = X * B + b
                wait(pe, dve_sum, u * CT + CT - 1)
                wait(pe, act_mb, u + 1 if not isinstance(b, int) else min(u + 1, X * B + B - 1))
                for m in range(2):
                    ins = pe.matmul(PS[:, 6 + m, 0:W], ones[0:CR, :], Zs[0:CR, m * W:(m + 1) * W], start=True, stop=True)
                ins.then_inc(pe_den.sem, 1)

            def context_keys(b, t):
                k = b * CT + t
                if t % CHUNK == 0:
                    wait(pe, sp_cxT[t // CHUNK], B + b)
                wait(pe, act_k1T, k - 2)
                n_rows = rows_in(1, t)
                pe.matmul(PS[0:n_rows, t % 2, 0:D], cxT[:, t * CR:t * CR + n_rows], wk_x1, start=True, stop=True)\
                    .then_inc(pe_k1.sem, 1)

            def context_keys_T(b, t):
                n_rows = rows_in(1, t)
                wait(pe, dve_k1n, b * CT + t)
                for m in range(KC):
                    ins = pe.transpose(PS[:, t % 2, D + m * CR:D + m * CR + n_rows],
                                       sqr[0:n_rows, t % 2, D + m * P:D + (m + 1) * P], ident[0:n_rows, 0:n_rows])
                ins.then_inc(pe_k1T.sem, 1)

            def context_scores_1(b, t):
                n_rows = rows_in(1, t)
                wait(pe, act_k1T, b * CT + t)
                wait(pe, act_t, b * CT + t - 1)
                for m in range(2):
                    ins = pe.matmul(PS[0:n_rows, 2 + m, 0:W], KT[:, t % 2, m, 0:n_rows], Qall[:, b, m, :],
                                    start=True, stop=True)
                ins.then_inc(pe_sx.sem, 1)

            def cross_attention_0():
                for t in range(CT):
                    context_scores(0, t)
                maximum(0, 0)
                with pe.Fori(1, B) as b:
                    for t in range(CT):
                        context_scores(b, t)
                        weighted_context(0, b - 1, t)
                    maximum(0, b)
                    denominators(0, b - 1)
                for t in range(CT):
                    weighted_context(0, B - 1, t)
                denominators(0, B - 1)

            def cross_attention_1():
                def batch(b, before):
                    for u in range(CT + 2):
                        if u < CT:
                            context_keys(b, u)
                        if 1 <= u <= CT:
                            context_keys_T(b, u - 1)
                        if u >= 2:
                            context_scores_1(b, u - 2)
                        if before is not None and u < CT:
                            weighted_context(1, before, u)
                    maximum(1, b)
                batch(0, None)
                with pe.Fori(1, B) as b:
                    batch(b, b - 1)
                    denominators(1, b - 1)
                for t in range(CT):
                    weighted_context(1, B - 1, t)
                denominators(1, B - 1)

            def output_rows(X, J, row):
                with pe.Fori(0, NT // G) as i:
                    for g in range(G):
                        j = i * G + g
                        wait(pe, act_ots, X * NT + j)
                        wait(pe, pool_ots, X * NT + j)
                        project(j, J, [OTs[:, g, h, :] for h in range(H)], [vo[:, h, :] for h in range(H)], row)

            pe.wait_ge(sp_wx0, 6 * 16)
            wait(pe, dve_x, NT - 1)
            value_output(P, wvT_x0, wo_x0, 0)
            pe.wait_ge(dve_setup, 2)
            with pe.Fori(0, NT // G) as i:
                js = [i * G + g for g in range(G)]
                norm_T(js, NT)
                for g, j in enumerate(js):
                    wait(pe, act_xT, NT + j)
                    wait(pe, dve_qh, j - 1)
                    for n in range(4):
                        for k in range(KC):
                            ins = pe.matmul(PS[0:R, 1 + n, :], xT[:, g, k], wq_x0[:, k, n * 512:(n + 1) * 512],
                                            start=(k == 0), stop=(k == KC - 1))
                    ins.then_inc(pe_qx.sem, 1)
                    wait(pe, dve_qh, j)
                    for n in range(4):
                        wait(pe, act_qhT, j * 4 + n - 2)
                        for h in range(4):
                            ins = pe.transpose(PS[:, 5 + n % 2, h * R:(h + 1) * R], qn_a[0:R, 4 * n + h, :],
                                               ident[0:R, 0:R])
                        ins.then_inc(pe_qhT.sem, 1)
                    for n in range(4):
                        wait(pe, act_qhT, j * 4 + n)
                        wait(pe, dve_qt, j * 4 + n - 1)
                        for h in range(4 * n, 4 * n + 4):
                            ins = pe.matmul(PS[:, 7, (h % 4) * R:(h % 4 + 1) * R], wkT_x0[:, h, :], qhT[:, h, :],
                                            start=True, stop=True, skip_group_check=True)
                        ins.then_inc(pe_qt.sem, 1)
            wait(pe, dve_qt, 4 * NT - 1)
            cross_attention_0()
            output_rows(0, NT, None)

            pe.wait_ge(dve_setup, 4)
            with pe.Fori(0, NT // G) as i:
                js = [i * G + g for g in range(G)]
                norm_T(js, 2 * NT)
                for g, j in enumerate(js):
                    wait(pe, act_xT, 2 * NT + j)
                    project(j, 2 * NT, [xT[:, g, k] for k in range(KC)], [fmix[:, k, :] for k in range(KC)], 1)

            pe.wait_ge(sp_w1, 4 * 16)
            pe.wait_ge(pool_init, 6)
            wait(pe, dve_x, 3 * NT - 1)
            with pe.Fori(0, NT // G) as i:
                js = [i * G + g for g in range(G)]
                norm_T(js, 3 * NT)
                for g, j in enumerate(js):
                    wait(pe, act_xT, 3 * NT + j)
                    wait(pe, dve_rope, j - 1)
                    for m in range(2 * KC):
                        for k in range(KC):
                            ins = pe.matmul(PS[:, 1, m * R:(m + 1) * R], wq1[:, k, m * P:(m + 1) * P], xT[:, g, k],
                                            start=(k == 0), stop=(k == KC - 1))
                    ins.then_inc(pe_q.sem, 1)
                    wait(pe, dve_cx, NT + i * G - 1)
                    for m in range(KC):
                        for k in range(KC):
                            ins = pe.matmul(PS[:, 7, m * R:(m + 1) * R], wk1[:, k, m * P:(m + 1) * P], xT[:, g, k],
                                            start=(k == 0), stop=(k == KC - 1))
                    ins.then_inc(pe_k.sem, 1)
                    wait(pe, dve_va, NT + j - 1)
                    wait(pe, dve_x, 3 * NT + i * G - 1)
                    for b in range(2):
                        for k in range(KC):
                            ins = pe.matmul(PS[0:S, 2, b * P:(b + 1) * P], xT[:, g, k, b * S:(b + 1) * S], wv1[:, k, :],
                                            start=(k == 0), stop=(k == KC - 1))
                    ins.then_inc(pe_v.sem, 1)
                attention(js, NT, SA, 3 * NT, [(dve_km1, 0)], wo1, None)

            pe.wait_ge(sp_wx1, 12 * 16)
            wait(pe, dve_x, 4 * NT - 1)
            value_output(HD, wvT_x1, woh_x1, H // 2)
            pe.wait_ge(dve_setup, 13)
            for n in range(2):
                if n:
                    pe.wait_ge(dve_kd, 3 * n - 2)
                pe.matmul(PS[:, 1, 0:D], ydT[:, n * P:(n + 1) * P], wkv_d[:, 0:D], start=True, stop=True)\
                    .then_inc(pe_kd, 1)
            for n in range(2):
                pe.wait_ge(dve_kd, 2 + 2 + n + 1)
                if n:
                    pe.wait_ge(act_kd, 2 + n)
                for m in range(KC):
                    ins = pe.transpose(PS[:, 5, m * P:(m + 1) * P], kd[:, n, m * P:(m + 1) * P], ident[:, :])
                ins.then_inc(pe_kdT, 1)
            pe.wait_ge(act_kd, 4)
            with pe.Fori(0, NT // G) as i:
                js = [i * G + g for g in range(G)]
                norm_T(js, 4 * NT)
                for g, j in enumerate(js):
                    wait(pe, act_xT, 4 * NT + j)
                    wait(pe, dve_qs, j - 1)
                    for k in range(KC):
                        ins = pe.matmul(PS[0:R, 1, 0:D], xT[:, g, k], wq_x1[:, k, :], start=(k == 0), stop=(k == KC - 1))
                    ins.then_inc(pe_q1.sem, 1)
                    wait(pe, pool_yd, j)
                    wait(pe, dve_va, 2 * NT + j - 1)
                    wait(pe, dve_x, 4 * NT + i * G - 1)
                    for b in range(2):
                        ins = pe.matmul(PS[0:NDCA, 2, b * D:(b + 1) * D], yds[:, g, b * NDCA:(b + 1) * NDCA],
                                        wkv_d[:, D:2 * D], start=True, stop=True)
                    ins.then_inc(pe_v.sem, 1)
                for g, j in enumerate(js):
                    wait(pe, dve_q1n, j)
                    wait(pe, act_q1, j - 1)
                    wait(pe, act_pT, 4 * NT + 2 * i * G - 1)
                    for k in range(KC):
                        ins = pe.transpose(PS[:, 5, k * R:(k + 1) * R], qs[0:R, g, k * P:(k + 1) * P], ident[0:R, 0:R])
                    ins.then_inc(pe_q1T.sem, 1)
                attention(js, 2 * NT, DCA, 4 * NT, [(act_q1, 0), (dve_kmd, 0)], wo_x1, 2)
            wait(pe, dve_q1m, NT - 1)
            wait(pe, dve_x, 5 * NT - 1)
            cross_attention_1()
            output_rows(1, 5 * NT, None)

            pe.wait_ge(sp_moe, 3 * 16)
            wait(pe, dve_x, 6 * NT - 1)
            with pe.Fori(0, NT // G) as i:
                js = [i * G + g for g in range(G)]
                norm_T(js, 5 * NT)
                for g, j in enumerate(js):
                    wait(pe, act_xT, 5 * NT + j)
                    wait(pe, dve_lg, j - 1)
                    wait(pe, dve_hT, i * G - 1)
                    for k in range(KC):
                        ins = pe.matmul(PS[0:R, 7, 0:E + 1], xT[:, g, k], wr[:, k, :], start=(k == 0), stop=(k == KC - 1))
                    ins.then_inc(pe_lg.sem, 1)
                for g, j in enumerate(js):
                    wait(pe, dve_h, j - 1)
                    wait(pe, dve_x, 6 * NT + i * G - 1)
                    for w in range(2):
                        for c in range(0, FA, 512):
                            n = min(512, FA - c)
                            for k in range(KC):
                                ins = pe.matmul(PS[0:R, 1 + 3 * w + c // 512, 0:n], xT[:, g, k], w13[:, k, w, c:c + n],
                                                start=(k == 0), stop=(k == KC - 1))
                    ins.then_inc(pe_h.sem, 1)
                for g, j in enumerate(js):
                    wait(pe, dve_h, j)
                    for n in range(3):
                        if n == 0:
                            wait(pe, act_hT, j * 2 - 1)
                            wait(pe, act_xT, 5 * NT + i * G + G - 1)
                        elif n == 1:
                            wait(pe, dve_hT, j - 1)
                            wait(pe, dve_lg, i * G + G - 1)
                        else:
                            wait(pe, act_hT, j * 2)
                        for c in range(4 * n, min(4 * n + 4, FA // P)):
                            ins = pe.transpose(PS[:, 7 if n == 1 else 0, (c % 4) * R:(c % 4 + 1) * R],
                                               hm[0:R, g, c * P:(c + 1) * P], ident[0:R, 0:R])
                        ins.then_inc(pe_hT.sem, 1)
                for g, j in enumerate(js):
                    wait(pe, act_hT, j * 2 + 1)
                    wait(pe, dve_hT, j)
                    project(j, 6 * NT, [hT[:, g, c] for c in range(FA // P)], [w2[:, c, :] for c in range(FA // P)], None)

        @block.scalar
        def _(act):
            for s in by_engine["act"]:
                s.credit(act)

            def norm_T(js, L):
                for g, j in enumerate(js):
                    wait(act, pe_xT, L + j)
                    act.copy(xT[:, g], PS[:, 0, 0:KC * R].rearrange("p (k r) -> p k r", k=KC))\
                       .then_inc(act_xT.sem, 1)

            def attention(js, U, V, scale):
                T = V.T
                for g, j in enumerate(js):
                    z = V.Z[:, g, :]
                    wait(act, dve_z, U + j)
                    if U == 0:
                        act.activation(z, z, ACT.Tanh, scale=1.0 / (30.0 * HD ** 0.5)).then_inc(act_tanh.sem, 1)
                        wait(act, act_tanh, j)
                    act.activation(z, z, ACT.Exp, scale=30.0 if U == 0 else scale).then_inc(act_e.sem, 1)
                for g, j in enumerate(js):
                    for n in (0, 2):
                        wait(act, pe_pT, (U + j) * 4 + n)
                        act.copy(V.PT[0:T, g, 4 * n:4 * n + 4, :], PS[0:T, 5, :].rearrange("p (h q) -> p h q", h=4))\
                           .then_inc(act_pT.sem, 1)
                for g, j in enumerate(js):
                    wait(act, pe_cT, U + j)
                    c = PS[:, 0, 0:KC * P].rearrange("p (k b s) -> p k b s", k=KC, b=2)[:, :, :, 0:S]
                    to = V.cT[:, g].rearrange("p k (b s) -> p k b s", b=2)
                    if U == 2 * NT:
                        act.activation(to[:, 0], c[:, 0], ACT.Identity, bias=bvcol[:, 0:1])
                        act.activation(to[:, 1], c[:, 1], ACT.Identity, bias=bvcol[:, 1:2]).then_inc(act_cT.sem, 1)
                    else:
                        act.copy(to, c).then_inc(act_cT.sem, 1)

            with act.Fori(0, NT // G) as i:
                js = [i * G + g for g in range(G)]
                act.wait_ge(pool_init, 4)
                norm_T(js, 0)
                for g, j in enumerate(js):
                    wait(act, pe_q, j)
                    for m in range(KC):
                        act.activation(SA.qT[:, g, m, 0:R], PS[:, 1, m * R:(m + 1) * R], ACT.Identity,
                                       bias=bqk0[:, 0, m:m + 1]).then_inc(act_q.sem, 1)
                attention(js, 0, SA, None)

            def squares(b, t):
                K = b * CT + t
                for n in range(4):
                    wait(act, pe_kp, K * 4 + n)
                    wait(act, dve_ss, K * 4 + n - 2)
                    act.activation(sqr[0:CR, n % 2, :], PS[0:CR, n % 2, :], ACT.Square).then_inc(act_sq.sem, 1)

            def probabilities(X, b, t, scale):
                K = (X * B + b) * CT + t
                n_rows = rows_in(X, t)
                wait(act, pool_d, K)
                wait(act, pe_pv, K - 3)
                wait(act, dve_sum, K - 3)
                act.activation(Pr[0:n_rows, t % 3, :], Dr[0:n_rows, t % 2, :], ACT.Exp, scale=scale).then_inc(act_p.sem, 1)

            def maximum(X, b):
                u = X * B + b
                wait(act, pe_mb, u)
                if X == 1 or not isinstance(b, int) or b > 0:
                    wait(act, pool_d, u * CT - 1)
                act.copy(Mb[0:CR, :].rearrange("p (m w) -> p m w", m=2), PS[0:CR, 6:8, 0:W]).then_inc(act_mb.sem, 1)

            def stage_outputs(X):
                with act.Fori(0, NT // G) as i:
                    for g in range(G):
                        j = i * G + g
                        wait(act, dve_ot, X * B + B - 1)
                        wait(act, pe_y, (1 if X == 0 else 5) * NT + j - G)
                        act.copy(OTs[:, g, :, 0:S], Qall[:, 2 * j].rearrange("p m (h s) -> p (m h) s", h=HM))\
                           .then_inc(act_ots.sem, 1)

            with act.Fori(0, NT // G) as i:
                js = [i * G + g for g in range(G)]
                norm_T(js, NT)
                for g, j in enumerate(js):
                    wait(act, pe_qx, j)
                    wait(act, dve_ssa, j - 1)
                    act.activation(sq_a[0:R, :], PS[0:R, 1:5, :].rearrange("p a n -> p (a n)"), ACT.Square)\
                       .then_inc(act_sqa.sem, 1)
                    for n in range(4):
                        wait(act, pe_qhT, j * 4 + n)
                        if g > 0:
                            wait(act, pe_qt, (j - 1) * 4 + n)
                        else:
                            wait(act, pe_qt, i * G * 4 - 1)
                        act.copy(qhT[:, 4 * n:4 * n + 4, :], PS[:, 5 + n % 2, 0:4 * R].rearrange("p (h r) -> p h r", h=4))\
                           .then_inc(act_qhT.sem, 1)
            wait(act, pe_qt, 4 * NT - 1)
            for t in range(CT):
                squares(0, t)
            maximum(0, 0)
            with act.Fori(1, B) as b:
                for t in range(CT):
                    squares(b, t)
                    probabilities(0, b - 1, t, XD ** -0.5)
                maximum(0, b)
            for t in range(CT):
                probabilities(0, B - 1, t, XD ** -0.5)
            stage_outputs(0)

            with act.Fori(0, NT // G) as i:
                norm_T([i * G + g for g in range(G)], 2 * NT)

            act.wait_ge(pool_init, 6)
            with act.Fori(0, NT // G) as i:
                js = [i * G + g for g in range(G)]
                norm_T(js, 3 * NT)
                attention(js, NT, SA, D ** -0.5)

            def key_squares_1(b, t):
                n_rows = rows_in(1, t)
                wait(act, dve_k1c, b * CT + t)
                wait(act, dve_k1ss, b * CT + t - 2)
                act.activation(sqr[0:n_rows, t % 2, 0:D], sqr[0:n_rows, t % 2, D:2 * D], ACT.Square).then_inc(act_k1s.sem, 1)

            def keys_T(b, t):
                n_rows = rows_in(1, t)
                wait(act, pe_k1T, b * CT + t)
                wait(act, pe_sx, B * CT + b * CT + t - 2)
                act.activation(KT[:, t % 2, :, 0:n_rows],
                               PS[:, t % 2, D:D + KC * CR].rearrange("p (m r) -> p m r", m=KC)[:, :, 0:n_rows],
                               ACT.Identity, scale=lncol[:, 2:3], bias=lncol[:, 3:4]).then_inc(act_k1T.sem, 1)

            def keep_scores(b, t):
                n_rows = rows_in(1, t)
                K = B * CT + b * CT + t
                wait(act, pe_sx, K)
                wait(act, pool_d, K - CT)
                act.copy(Sall[0:n_rows, t, :].rearrange("p (m w) -> p m w", m=2), PS[0:n_rows, 2:4, 0:W])\
                   .then_inc(act_t.sem, 1)

            act.wait_ge(sp_wx1, 12 * 16)
            for n in range(2):
                act.wait_ge(dve_kd, 2 * n + 1 if n == 0 else 3)
                act.activation(sq1a[:, n, :], kd[:, n, :], ACT.Square).then_inc(act_kd, 1)
            for n in range(2):
                act.wait_ge(pe_kdT, n + 1)
                act.activation(kTd[:, :, n * P:(n + 1) * P], PS[:, 5, 0:KC * P].rearrange("p (m r) -> p m r", m=KC),
                               ACT.Identity, scale=lncol[:, 4:5], bias=lncol[:, 5:6]).then_inc(act_kd, 1)
            act.wait_ge(pool_init, 8)
            with act.Fori(0, NT // G) as i:
                js = [i * G + g for g in range(G)]
                norm_T(js, 4 * NT)
                for g, j in enumerate(js):
                    wait(act, dve_qs, j)
                    act.activation(sq1a[0:R, g, :], qs[0:R, g, :], ACT.Square).then_inc(act_q1s.sem, 1)
                for g, j in enumerate(js):
                    wait(act, pe_q1T, j)
                    act.activation(DCA.qT[:, g, :, 0:R], PS[:, 5, 0:KC * R].rearrange("p (m r) -> p m r", m=KC),
                                   ACT.Identity, scale=lncol[:, 0:1], bias=lncol[:, 1:2]).then_inc(act_q1.sem, 1)
                attention(js, 2 * NT, DCA, HD ** -0.5)
            wait(act, dve_x, 5 * NT - 1)

            def batch(b, before):
                for u in range(CT + 2):
                    if u < CT:
                        key_squares_1(b, u)
                    if 1 <= u <= CT:
                        keys_T(b, u - 1)
                    if u >= 2:
                        keep_scores(b, u - 2)
                    if before is not None and u < CT:
                        probabilities(1, before, u, HD ** -0.5)
                maximum(1, b)
            batch(0, None)
            with act.Fori(1, B) as b:
                batch(b, b - 1)
            for t in range(CT):
                probabilities(1, B - 1, t, HD ** -0.5)
            stage_outputs(1)

            with act.Fori(0, NT // G) as i:
                js = [i * G + g for g in range(G)]
                norm_T(js, 5 * NT)
                for g, j in enumerate(js):
                    wait(act, dve_le, j)
                    act.activation(le[0:R, g, :], le[0:R, g, :], ACT.Exp).then_inc(act_le.sem, 1)
                    act.activation(lg[0:R, g, E:E + 1], lg[0:R, g, E:E + 1], ACT.Tanh, scale=0.5).then_inc(act_le.sem, 1)
                for g, j in enumerate(js):
                    wait(act, pe_h, j)
                    act.activation(th[0:R, g, :], PS[0:R, 1:4, :].rearrange("p a n -> p (a n)")[:, 0:FA], ACT.Tanh,
                                   scale=0.5).then_inc(act_th.sem, 1)
                for g, j in enumerate(js):
                    for n in (0, 2):
                        wait(act, pe_hT, j * 3 + n)
                        c = min(4, FA // P - 4 * n)
                        act.copy(hT[:, g, 4 * n:4 * n + c, :], PS[:, 0, 0:c * R].rearrange("p (c r) -> p c r", c=c))\
                           .then_inc(act_hT.sem, 1)

        @block.vector
        def _(dve):
            for s in by_engine["dve"]:
                s.credit(dve)

            def norm(js, L, J):
                for g, j in enumerate(js):
                    if J > 0:
                        wait(dve, dve_x, J - NT + j)
                    dve.bn_stats(lnst[0:R, g, :], x[0:R, j, :]).then_inc(dve_stats.sem, 1)
                for g, j in enumerate(js):
                    wait(dve, dve_stats, L + j)
                    dve.sem_inc(dve_beat, 1)
                    dve.bn_aggr(lnmv[0:R, g, :], lnst[0:R, g, :]).then_inc(dve_aggr.sem, 1)
                for g, j in enumerate(js):
                    wait(dve, pool_rs, L + j)
                    dve.tensor_scalar(xn[0:R, g, :], x[0:R, j, :], lnmv[0:R, g, 0:1], lnrs[0:R, g:g + 1],
                                      ALU.subtract, ALU.mult).then_inc(dve_xn.sem, 1)

            def head_sel(T):
                return hmask[:, :].unsqueeze(2).broadcast_to([P, HM, T])

            def attention(js, U, V):
                T = V.T
                for g, j in enumerate(js):
                    wait(dve, pe_s, U + j)
                    s = PS[:, 3:5, 0:HM * T]
                    z = V.Z[:, g, :].rearrange("p (m z) -> p m z", m=KC)
                    if U == 0:
                        dve.tensor_tensor(z, s, abias[:, :, :].rearrange("p (m h) t -> p m (h t)", m=KC), ALU.add)\
                           .then_inc(dve_z.sem, 1)
                    else:
                        s = s.rearrange("p m (h t) -> p m h t", h=HM)
                        z = z.rearrange("p m (h t) -> p m h t", h=HM)
                        largest = V.mx[:, g, :].rearrange("p (m h) -> p m h", m=KC)
                        dve.tensor_reduce(largest, s, AX.X, ALU.max).then_inc(dve_mx.sem, 1)
                        wait(dve, dve_mx, U - NT + j)
                        dve.tensor_tensor(z, s, largest.unsqueeze(3).broadcast_to([P, KC, HM, T]), ALU.subtract)\
                           .then_inc(dve_z.sem, 1)
                for g, j in enumerate(js):
                    if U == 0:
                        wait(dve, act_e, j)
                        z = V.Z[:, g, :].rearrange("p (h t) -> p h t", h=H)
                        dve.tensor_tensor(z, z, causal[:, :].unsqueeze(1).broadcast_to([P, H, S]), ALU.mult)\
                           .then_inc(dve_p.sem, 1)
                for g, j in enumerate(js):
                    for n in (1, 3):
                        wait(dve, pe_pT, (U + j) * 4 + n)
                        dve.tensor_copy(V.PT[0:T, g, 4 * n:4 * n + 4, :], PS[0:T, 6, :].rearrange("p (h q) -> p h q", h=4))\
                           .then_inc(dve_pT.sem, 1)
                for g, j in enumerate(js):
                    wait(dve, pe_o, U + j)
                    o = PS[:, 7, 0:H * (HD + 1)].rearrange("p (h d) -> p h d", h=H)
                    dve.reciprocal(V.rc[:, g, :], o[:, :, HD]).then_inc(dve_rc.sem, 1)
                    wait(dve, dve_rc, U + j)
                    if U == NT:
                        dve.tensor_tensor(V.cx[:, g, :].rearrange("p (h m d) -> p m h d", h=HM, m=KC),
                                          o[:, :, 0:HD].rearrange("p (m h) d -> p m h d", m=KC),
                                          V.rc[:, g, :].rearrange("p (m h) -> p m h", m=KC).unsqueeze(3)
                                          .broadcast_to([P, KC, HM, HD]), ALU.mult).then_inc(dve_cx.sem, 1)
                    else:
                        dve.tensor_tensor(V.cx[:, g, :].rearrange("p (h d) -> p h d", h=H), o[:, :, 0:HD],
                                          V.rc[:, g, :].unsqueeze(2).broadcast_to([P, H, HD]), ALU.mult)\
                           .then_inc(dve_cx.sem, 1)

            def add_rows(js, J):
                for g, j in enumerate(js):
                    wait(dve, pe_y, J + j)
                    dve.tensor_tensor(x[0:R, j, :], x[0:R, j, :], PS[0:R, 2, 0:D], ALU.add).then_inc(dve_x.sem, 1)

            dve.wait_ge(sp_w0, 15 * 16)
            dve.wait_ge(sp_x, 16)
            dve.wait_ge(pool_init, 4)
            dve.tensor_tensor(abias[:, :, :], rel[:, :].unsqueeze(1).broadcast_to([P, H, S]),
                              slopes[:, :].unsqueeze(2).broadcast_to([P, H, S]), ALU.mult).then_inc(dve_setup, 1)
            dve.wait_ge(dve_setup, 1)
            with dve.Fori(0, NT // G) as i:
                js = [i * G + g for g in range(G)]
                norm(js, 0, 0)
                for g, j in enumerate(js):
                    wait(dve, pe_k, j)
                    for b in range(2):
                        for m in range(KC):
                            kb = PS[:, 7, m * R + b * S:m * R + b * S + S]
                            dve.scalar_tensor_tensor(SA.Km[:, g, b, m].rearrange("p (h t) -> p h t", h=HM), kb.unsqueeze(1).broadcast_to([P, HM, S]),
                                                     bqk0[:, 1, m:m + 1], head_sel(S), ALU.add, ALU.mult)\
                               .then_inc(dve_km0.sem, 1)
                    wait(dve, pe_v, j)
                    dve.tensor_tensor(SA.va[0:S, g, :, :, 0:HD],
                                      PS[0:S, 2, :].rearrange("p (b h d) -> p b h d", b=2, h=H),
                                      bv0[0:S, :].rearrange("p (h d) -> p h d", h=H).unsqueeze(1)
                                      .broadcast_to([S, 2, H, HD]), ALU.add).then_inc(dve_va.sem, 1)
                attention(js, 0, SA)
                add_rows(js, 0)

            def value_output(V):
                for n in range(H // 2):
                    wait(dve, pe_vo, V + n)
                    dve.tensor_copy(vo[:, 2 * n:2 * n + 2, :], PS[:, 7, :].rearrange("p (h d) -> p h d", h=2))\
                       .then_inc(dve_vo.sem, 1)

            def by_head(row):
                return row.rearrange("p (m h) -> p m h", m=2).unsqueeze(3).broadcast_to([row.shape[0], 2, HM, S])

            def key_norms(b, t):
                K = b * CT + t
                wait(dve, pool_vek, K - 2)
                for n in range(4):
                    wait(dve, act_sq, K * 4 + n)
                    dve.tensor_reduce(ssr[0:CR, t % 2, 4 * n:4 * n + 4],
                                      sqr[0:CR, n % 2, :].rearrange("p (h d) -> p h d", h=4), AX.X, ALU.add)\
                       .then_inc(dve_ss.sem, 1)

            def scores(b, t):
                K = b * CT + t
                wait(dve, pool_rk, K)
                wait(dve, pe_sx, K)
                if not isinstance(b, int) or b > 0:
                    wait(dve, pool_d, K - CT)
                dve.tensor_tensor(Sall[0:CR, t, :].rearrange("p (m h s) -> p m h s", m=2, h=HM),
                                  PS[0:CR, 2:4, 0:W].rearrange("p m (h s) -> p m h s", h=HM),
                                  by_head(rkr[0:CR, t % 2, :]), ALU.mult).then_inc(dve_t.sem, 1)

            def running_maximum(X, b, t):
                K = (X * B + b) * CT + t
                n_rows = rows_in(X, t)
                if X == 0:
                    wait(dve, dve_t, K)
                else:
                    wait(dve, act_t, b * CT + t)
                if t == 0:
                    wait(dve, pe_mT, X * B + b - 1)
                    dve.tensor_copy(Mx[0:CR, :], Sall[0:CR, 0, :]).then_inc(dve_mxr.sem, 1)
                else:
                    wait(dve, dve_mxr, K - 1)
                    dve.tensor_tensor(Mx[0:n_rows, :], Mx[0:n_rows, :], Sall[0:n_rows, t, :], ALU.max)\
                       .then_inc(dve_mxr.sem, 1)

            def sum_probabilities(X, b, t):
                K = (X * B + b) * CT + t
                n_rows = rows_in(X, t)
                wait(dve, act_p, K)
                if t == 0:
                    wait(dve, pe_den, X * B + b - 1)
                    dve.tensor_copy(Zs[0:CR, :], Pr[0:CR, 0, :]).then_inc(dve_sum.sem, 1)
                else:
                    wait(dve, dve_sum, K - 1)
                    dve.tensor_tensor(Zs[0:n_rows, :], Zs[0:n_rows, :], Pr[0:n_rows, t % 3, :], ALU.add)\
                       .then_inc(dve_sum.sem, 1)

            def maximum(X, b):
                u = X * B + b
                wait(dve, pe_mT, u)
                for bank, n in ((6, 4), (7, 3)):
                    dve.tensor_reduce(mcol[:, 4 * (bank - 6):4 * (bank - 6) + n],
                                      PS[:, bank, 0:n * CR].rearrange("p (a r) -> p a r", a=n), AX.X, ALU.max)\
                       .then_inc(dve_mcol.sem, 1)
                wait(dve, dve_mcol, u)
                wait(dve, pe_mb, u - 1)
                dve.tensor_tensor(mdiag[:, :, :], ident[:, :].unsqueeze(1).broadcast_to([P, 7, P]),
                                  mcol[:, 0:7].unsqueeze(2).broadcast_to([P, 7, P]), ALU.mult).then_inc(dve_diag.sem, 1)

            def outputs(X, b):
                u = X * B + b
                wait(dve, pe_den, u)
                dve.reciprocal(rz[:, :].rearrange("p (m w) -> p m w", m=2), PS[:, 6:8, 0:W]).then_inc(dve_rz.sem, 1)
                wait(dve, dve_rz, u)
                wait(dve, pe_pv, u * CT + CT - 1)
                dve.tensor_tensor(Qall[:, b], PS[:, 4:6, 0:W], rz[:, :].rearrange("p (m w) -> p m w", m=2), ALU.mult)\
                   .then_inc(dve_ot.sem, 1)

            dve.wait_ge(sp_wx0, 6 * 16)
            dve.tensor_scalar(wkT_x0, wkT_x0, gqk[:, 0:1], gqk[:, 1:2], ALU.mult, ALU.mult).then_inc(dve_setup, 1)
            value_output(0)
            with dve.Fori(0, NT // G) as i:
                js = [i * G + g for g in range(G)]
                norm(js, NT, NT)
                for g, j in enumerate(js):
                    wait(dve, act_sqa, j)
                    dve.tensor_reduce(ss_a[0:R, g, :], sq_a[0:R, :].rearrange("p (h d) -> p h d", h=H), AX.X, ALU.add)\
                       .then_inc(dve_ssa.sem, 1)
                    wait(dve, pool_rqa, j)
                    if g > 0:
                        wait(dve, pe_qhT, (j - 1) * 4 + 3)
                    else:
                        wait(dve, pe_qhT, i * G * 4 - 1)
                    dve.tensor_tensor(qn_a[0:R, :, :], PS[0:R, 1:5, :].rearrange("p a (h d) -> p (a h) d", h=4),
                                      rq_a[0:R, g, :].unsqueeze(2).broadcast_to([R, H, XD]), ALU.mult)\
                       .then_inc(dve_qh.sem, 1)
                    for n in range(4):
                        wait(dve, pe_qt, j * 4 + n)
                        q = Qall[:, bass.ds(2 * j, 2)].rearrange("p b m (h s) -> p (m h) b s", h=HM)
                        dve.tensor_copy(q[:, 4 * n:4 * n + 4],
                                        PS[:, 7, 0:4 * R].rearrange("p (h b s) -> p h b s", h=4, b=2))\
                           .then_inc(dve_qt.sem, 1)
            for t in range(CT):
                key_norms(0, t)
                scores(0, t)
                running_maximum(0, 0, t)
            maximum(0, 0)
            with dve.Fori(1, B) as b:
                for t in range(CT):
                    key_norms(b, t)
                    scores(b, t)
                    running_maximum(0, b, t)
                    sum_probabilities(0, b - 1, t)
                maximum(0, b)
                outputs(0, b - 1)
            for t in range(CT):
                sum_probabilities(0, B - 1, t)
            outputs(0, B - 1)
            with dve.Fori(0, NT // G) as i:
                add_rows([i * G + g for g in range(G)], NT)

            dve.wait_ge(sp_fac, 16)
            mixed = fmix[:, :, :].rearrange("p k n -> p (k n)")
            dve.tensor_reduce(mixed, factors, AX.X, ALU.add).then_inc(dve_setup, 1)
            dve.wait_ge(dve_setup, 3)
            dve.tensor_scalar(mixed, mixed, 8 ** -0.5, None, ALU.mult).then_inc(dve_setup, 1)
            with dve.Fori(0, NT // G) as i:
                js = [i * G + g for g in range(G)]
                norm(js, 2 * NT, 2 * NT)
                add_rows(js, 2 * NT)

            dve.wait_ge(pool_init, 6)
            with dve.Fori(0, NT // G) as i:
                js = [i * G + g for g in range(G)]
                norm(js, 3 * NT, 3 * NT)
                for g, j in enumerate(js):
                    wait(dve, pe_q, NT + j)
                    q = PS[:, 1, 0:2 * KC * R].rearrange("p (z r) -> p z r", z=2 * KC)
                    along = lambda tab: tab[:, :].unsqueeze(1).broadcast_to([P, KC, R])
                    dve.tensor_tensor(rope[:, 0], q[:, 0:KC], along(cosT), ALU.mult).then_inc(dve_rope.sem, 1)
                    dve.tensor_tensor(rope[:, 1], q[:, KC:2 * KC], along(sinT), ALU.mult).then_inc(dve_rope.sem, 1)
                    wait(dve, pe_k, NT + j)
                    dve.tensor_tensor(rope[:, 2, 0], PS[:, 7, 0:R], cosT[:, :], ALU.mult).then_inc(dve_rope.sem, 1)
                    dve.tensor_tensor(rope[:, 2, 1], PS[:, 7, R:2 * R], sinT[:, :], ALU.mult).then_inc(dve_rope.sem, 1)
                    wait(dve, dve_rope, j)
                    dve.tensor_tensor(SA.qT[:, g, :, 0:R], rope[:, 0], rope[:, 1], ALU.add).then_inc(dve_qk1.sem, 1)
                    dve.tensor_tensor(rope[:, 2, 0], rope[:, 2, 0], rope[:, 2, 1], ALU.add).then_inc(dve_qk1.sem, 1)
                    wait(dve, dve_qk1, j)
                    for b in range(2):
                        dve.tensor_tensor(SA.Km[:, g, b, 0].rearrange("p (h t) -> p h t", h=HM),
                                          rope[:, 2, 0, b * S:(b + 1) * S].unsqueeze(1).broadcast_to([P, HM, S]),
                                          head_sel(S), ALU.mult).then_inc(dve_km1.sem, 1)
                    wait(dve, dve_km1, j)
                    wait(dve, pe_v, NT + j)
                    dve.tensor_copy(SA.va[0:S, g, :, 0:HM, 0:HD],
                                    PS[0:S, 2, 0:2 * P].rearrange("p (b h d) -> p b h d", b=2, h=HM)).then_inc(dve_va.sem, 1)
                attention(js, NT, SA)
                add_rows(js, 3 * NT)

            def centre(v, n, at):
                v = v.rearrange("p (n d) -> p n d", d=HD)
                dve.wait_ge(dve_setup, at)
                dve.tensor_reduce(mean[:, 0:n], v, AX.X, ALU.add).then_inc(dve_setup, 1)
                dve.wait_ge(dve_setup, at + 1)
                dve.tensor_scalar(mean[:, 0:n], mean[:, 0:n], 1.0 / HD, None, ALU.mult).then_inc(dve_setup, 1)
                dve.wait_ge(dve_setup, at + 2)
                dve.tensor_tensor(v, v, mean[:, 0:n].unsqueeze(2).broadcast_to([P, n, HD]), ALU.subtract)\
                   .then_inc(dve_setup, 1)

            def spread(v, rows, T):
                return v.unsqueeze(2).broadcast_to([rows, H, T])

            dve.wait_ge(sp_wx1, 12 * 16)
            centre(wq_x1.rearrange("p k n -> p (k n)"), KC * H, 4)
            centre(wkv_d[:, 0:D], H, 7)
            centre(wk_x1, H, 10)
            centre(bq_x1, H, 13)
            centre(bkv_d[:, 0:D], H, 16)
            centre(bk_x1, H, 19)
            dve.wait_ge(dve_setup, 22)
            value_output(H // 2)
            for n in range(2):
                dve.wait_ge(pe_kd, n + 1)
                dve.tensor_tensor(kd[:, n, :], PS[:, 1, 0:D], bkv_d[:, 0:D], ALU.add).then_inc(dve_kd, 1)
                dve.wait_ge(act_kd, n + 1)
                dve.tensor_reduce(ss1a[:, n, :], sq1a[:, n, :].rearrange("p (h d) -> p h d", h=H), AX.X, ALU.add)\
                   .then_inc(dve_kd, 1)
            for n in range(2):
                dve.wait_ge(pool_kd, 2 * n + 2)
                dve.tensor_tensor(kd[:, n, :].rearrange("p (h d) -> p h d", h=H), kd[:, n, :].rearrange("p (h d) -> p h d", h=H),
                                  spread(rs1a[:, n, :], P, HD), ALU.mult).then_inc(dve_kd, 1)
            dve.wait_ge(pool_init, 8)
            dve.wait_ge(act_kd, 4)
            with dve.Fori(0, NT // G) as i:
                js = [i * G + g for g in range(G)]
                norm(js, 4 * NT, 4 * NT)
                for g, j in enumerate(js):
                    wait(dve, pe_q1, j)
                    dve.tensor_tensor(qs[0:R, g, :], PS[0:R, 1, 0:D], bq_x1[0:R, :], ALU.add).then_inc(dve_qs.sem, 1)
                    wait(dve, pe_v, 2 * NT + j)
                    dve.tensor_tensor(DCA.va[0:NDCA, g, :, :, 0:HD],
                                      PS[0:NDCA, 2, :].rearrange("p (b h d) -> p b h d", b=2, h=H),
                                      bkv_d[0:NDCA, D:2 * D].rearrange("p (h d) -> p h d", h=H).unsqueeze(1)
                                      .broadcast_to([NDCA, 2, H, HD]), ALU.add).then_inc(dve_va.sem, 1)
                for g, j in enumerate(js):
                    wait(dve, act_q1s, j)
                    dve.tensor_reduce(ss1a[0:R, g, :], sq1a[0:R, g, :].rearrange("p (h d) -> p h d", h=H), AX.X, ALU.add)\
                       .then_inc(dve_q1ss.sem, 1)
                for g, j in enumerate(js):
                    wait(dve, pool_q1r, j)
                    q = qs[0:R, g, :].rearrange("p (h d) -> p h d", h=H)
                    dve.tensor_tensor(q, q, spread(rs1a[0:R, g, :], R, HD), ALU.mult).then_inc(dve_q1n.sem, 1)
                    for b in range(2):
                        for m in range(KC):
                            dve.tensor_tensor(DCA.Km[:, g, b, m].rearrange("p (h t) -> p h t", h=HM),
                                              kTd[:, m, bass.ds((2 * j + b) * NDCA, NDCA)].unsqueeze(1)
                                              .broadcast_to([P, HM, NDCA]), head_sel(NDCA), ALU.mult)\
                               .then_inc(dve_kmd.sem, 1)
                for g, j in enumerate(js):
                    wait(dve, act_q1, j)
                    for b in range(2):
                        for m in range(KC):
                            dve.tensor_tensor(Qall[:, 2 * j + b, m].rearrange("p (h s) -> p h s", h=HM),
                                              DCA.qT[:, g, m, b * S:(b + 1) * S].unsqueeze(1).broadcast_to([P, HM, S]),
                                              head_sel(S), ALU.mult).then_inc(dve_q1m.sem, 1)
                attention(js, 2 * NT, DCA)
                add_rows(js, 4 * NT)

            def keys(b, t):
                n_rows = rows_in(1, t)
                wait(dve, pe_k1, b * CT + t)
                wait(dve, pe_k1T, b * CT + t - 2)
                dve.tensor_tensor(sqr[0:n_rows, t % 2, D:2 * D], PS[0:n_rows, t % 2, 0:D], bk_x1[0:n_rows, :], ALU.add)\
                   .then_inc(dve_k1c.sem, 1)

            def key_sums(b, t):
                n_rows = rows_in(1, t)
                wait(dve, act_k1s, b * CT + t)
                wait(dve, pool_k1v, b * CT + t - 2)
                dve.tensor_reduce(ssr[0:n_rows, t % 2, :], sqr[0:n_rows, t % 2, 0:D].rearrange("p (h d) -> p h d", h=H),
                                  AX.X, ALU.add).then_inc(dve_k1ss.sem, 1)

            def normal_keys(b, t):
                n_rows = rows_in(1, t)
                wait(dve, pool_k1r, b * CT + t)
                k = sqr[0:n_rows, t % 2, D:2 * D].rearrange("p (h d) -> p h d", h=H)
                dve.tensor_tensor(k, k, spread(rkr[0:n_rows, t % 2, :], n_rows, HD), ALU.mult).then_inc(dve_k1n.sem, 1)

            def batch(b, before):
                for u in range(CT + 2):
                    if u < CT:
                        keys(b, u)
                    if 1 <= u <= CT:
                        normal_keys(b, u - 1)
                    if u < CT:
                        key_sums(b, u)
                    if before is not None and u < CT:
                        sum_probabilities(1, before, u)
                    if u >= 2:
                        running_maximum(1, b, u - 2)
                maximum(1, b)
            batch(0, None)
            with dve.Fori(1, B) as b:
                batch(b, b - 1)
                outputs(1, b - 1)
            for t in range(CT):
                sum_probabilities(1, B - 1, t)
            outputs(1, B - 1)
            with dve.Fori(0, NT // G) as i:
                add_rows([i * G + g for g in range(G)], 5 * NT)

            with dve.Fori(0, NT // G) as i:
                js = [i * G + g for g in range(G)]
                norm(js, 5 * NT, 6 * NT)
                for g, j in enumerate(js):
                    wait(dve, pe_lg, j)
                    dve.tensor_copy(lg[0:R, g, :], PS[0:R, 7, 0:E + 1]).then_inc(dve_lg.sem, 1)
                for g, j in enumerate(js):
                    wait(dve, dve_lg, j)
                    dve.tensor_reduce(lm[0:R, g, :], lg[0:R, g, 0:E], AX.X, ALU.max).then_inc(dve_lm.sem, 1)
                for g, j in enumerate(js):
                    wait(dve, dve_lm, j)
                    dve.tensor_scalar(le[0:R, g, :], lg[0:R, g, 0:E], lm[0:R, g, :], None, ALU.subtract)\
                       .then_inc(dve_le.sem, 1)
                for g, j in enumerate(js):
                    wait(dve, act_le, j)
                    dve.sem_inc(dve_beat, 1)
                    dve.max(top[0:R, g, :], le[0:R, g, :]).then_inc(dve_top.sem, 1)
                    wait(dve, dve_top, j)
                    dve.sem_inc(dve_beat, 1)
                    dve.max_index(topi[0:R, g, :], top[0:R, g, :], le[0:R, g, :]).then_inc(dve_topi.sem, 1)
                    wait(dve, dve_topi, j)
                    dve.tensor_copy(topf[0:R, g, :], topi[0:R, g, :]).then_inc(dve_topf.sem, 1)
                    dve.tensor_tensor(tw[0:R, g, 0:1], top[0:R, g, 0:1], top[0:R, g, 1:2], ALU.add).then_inc(dve_tw.sem, 1)
                    dve.wait_ge(dve_tw.sem, dve_tw.done(j) - 2)
                    dve.reciprocal(tw[0:R, g, 1:2], tw[0:R, g, 0:1]).then_inc(dve_tw.sem, 1)
                    dve.wait_ge(dve_tw.sem, dve_tw.done(j) - 1)
                    dve.tensor_scalar(tw[0:R, g, 2:4], top[0:R, g, 0:2], tw[0:R, g, 1:2], 0.5, ALU.mult, ALU.mult)\
                       .then_inc(dve_tw.sem, 1)
                    wait(dve, dve_tw, j)
                    wait(dve, dve_topf, j)
                    for n in range(2):
                        dve.tensor_scalar(hot[0:R, g, n, :], eidx[0:R, :], topf[0:R, g, n:n + 1], tw[0:R, g, 2 + n:3 + n],
                                          ALU.is_equal, ALU.mult).then_inc(dve_hot.sem, 1)
                    wait(dve, dve_hot, j)
                    dve.tensor_tensor(comb[0:R, g, 0:E], hot[0:R, g, 0, :], hot[0:R, g, 1, :], ALU.add).then_inc(dve_comb.sem, 1)
                    dve.tensor_scalar(comb[0:R, g, E:EW], lg[0:R, g, E:E + 1].broadcast_to([R, EW - E]), 1.0, 0.25,
                                      ALU.add, ALU.mult).then_inc(dve_comb.sem, 1)
                for g, j in enumerate(js):
                    wait(dve, act_th, j)
                    wait(dve, pe_h, j)
                    flat_h = hm[0:R, g, :]
                    h1, h3 = (PS[0:R, c:c + 3, :].rearrange("p a n -> p (a n)")[:, 0:FA] for c in (1, 4))
                    dve.scalar_tensor_tensor(flat_h, th[0:R, g, :], 1.0, h1, ALU.add, ALU.mult).then_inc(dve_h.sem, 1)
                    dve.wait_ge(dve_h.sem, dve_h.done(j) - 2)
                    dve.tensor_tensor(flat_h, flat_h, h3, ALU.mult).then_inc(dve_h.sem, 1)
                    dve.wait_ge(dve_h.sem, dve_h.done(j) - 1)
                    wait(dve, dve_comb, j)
                    blocks = flat_h.rearrange("p (e i) -> p e i", i=FI)
                    dve.tensor_tensor(blocks, blocks, comb[0:R, g, :].unsqueeze(2).broadcast_to([R, EW, FI]), ALU.mult)\
                       .then_inc(dve_h.sem, 1)
                for g, j in enumerate(js):
                    wait(dve, pe_hT, j * 3 + 1)
                    dve.tensor_copy(hT[:, g, 4:8, :], PS[:, 7, 0:4 * R].rearrange("p (c r) -> p c r", c=4)).then_inc(dve_hT.sem, 1)
                add_rows(js, 6 * NT)

        @block.gpsimd
        def _(pool):
            for s in by_engine["pool"]:
                s.credit(pool)
            pool.memset(nhalf[:, :], -0.5).then_inc(pool_init, 1)
            pool.memset(ones[:, :], 1.0).then_inc(pool_init, 1)
            pool.memset(SA.qT, 0.0).then_inc(pool_init, 1)
            pool.memset(SA.va, 1.0).then_inc(pool_init, 1)
            pool.wait_ge(pool_init, 4)

            def norm(js, L, eps):
                for g, j in enumerate(js):
                    wait(pool, dve_aggr, L + j)
                    pool.sem_inc(pool_beat, 1)
                    pool.tensor_scalar(lnve[0:R, g:g + 1], lnmv[0:R, g, 1:2], eps, None, ALU.add).then_inc(pool_ve.sem, 1)
                    wait(pool, pool_ve, L + j)
                    pool.tensor_tensor(lnrs[0:R, g:g + 1], lnve[0:R, g:g + 1], nhalf[0:R, 0:1], ALU.pow)\
                        .then_inc(pool_rs.sem, 1)

            with pool.Fori(0, NT // G) as i:
                norm([i * G + g for g in range(G)], 0, 1e-5)

            def key_norms(b, t):
                K = b * CT + t
                wait(pool, dve_ss, K * 4 + 3)
                wait(pool, dve_t, K - 2)
                pool.sem_inc(pool_beat, 1)
                pool.tensor_scalar(vek[0:CR, t % 2, :], ssr[0:CR, t % 2, :], 1.0 / XD, 1e-5, ALU.mult, ALU.add)\
                    .then_inc(pool_vek.sem, 1)
                wait(pool, pool_vek, K)
                pool.tensor_tensor(rkr[0:CR, t % 2, :], vek[0:CR, t % 2, :], nhalf[0:CR, 0:H], ALU.pow)\
                    .then_inc(pool_rk.sem, 1)

            def less_maximum(X, b, t):
                K = (X * B + b) * CT + t
                n_rows = rows_in(X, t)
                if t == 0:
                    wait(pool, act_mb, X * B + b)
                if X == 0:
                    wait(pool, dve_t, K)
                else:
                    wait(pool, act_t, b * CT + t)
                wait(pool, act_p, K - 2)
                pool.tensor_tensor(Dr[0:n_rows, t % 2, :], Sall[0:n_rows, t, :], Mb[0:n_rows, :], ALU.subtract)\
                    .then_inc(pool_d.sem, 1)

            def stage_outputs(X):
                with pool.Fori(0, NT // G) as i:
                    for g in range(G):
                        j = i * G + g
                        wait(pool, dve_ot, X * B + B - 1)
                        wait(pool, pe_y, (1 if X == 0 else 5) * NT + j - G)
                        pool.sem_inc(pool_beat, 1)
                        pool.tensor_copy(OTs[:, g, :, S:R], Qall[:, 2 * j + 1].rearrange("p m (h s) -> p (m h) s", h=HM))\
                            .then_inc(pool_ots.sem, 1)

            with pool.Fori(0, NT // G) as i:
                js = [i * G + g for g in range(G)]
                norm(js, NT, 1e-5)
                for g, j in enumerate(js):
                    wait(pool, dve_ssa, j)
                    pool.sem_inc(pool_beat, 1)
                    pool.tensor_scalar(ss_a[0:R, g, :], ss_a[0:R, g, :], 1.0 / XD, 1e-5, ALU.mult, ALU.add)\
                        .then_inc(pool_vea.sem, 1)
                    wait(pool, pool_vea, j)
                    pool.tensor_tensor(rq_a[0:R, g, :], ss_a[0:R, g, :], nhalf[0:R, 0:H], ALU.pow)\
                        .then_inc(pool_rqa.sem, 1)
            wait(pool, pe_qt, 4 * NT - 1)
            for t in range(CT):
                key_norms(0, t)
            with pool.Fori(1, B) as b:
                for t in range(CT):
                    less_maximum(0, b - 1, t)
                    key_norms(b, t)
            for t in range(CT):
                less_maximum(0, B - 1, t)
            stage_outputs(0)

            with pool.Fori(0, NT // G) as i:
                norm([i * G + g for g in range(G)], 2 * NT, 1e-5)

            wait(pool, act_ots, NT - 1)
            pool.memset(SA.qT, 0.0).then_inc(pool_init, 1)
            pool.memset(SA.va, 1.0).then_inc(pool_init, 1)
            with pool.Fori(0, NT // G) as i:
                norm([i * G + g for g in range(G)], 3 * NT, 1e-5)

            def rsqrt_rows(to, v, rows, n, ready_v, ready_r, index):
                pool.sem_inc(pool_beat, 1)
                pool.tensor_scalar(v, v, 1.0 / HD, 1e-6, ALU.mult, ALU.add).then_inc(ready_v.sem, 1)
                wait(pool, ready_v, index)
                pool.tensor_tensor(to, v, nhalf[0:rows, 0:n], ALU.pow).then_inc(ready_r.sem, 1)

            wait(pool, pe_y, 4 * NT - 1)
            pool.memset(DCA.qT, 0.0).then_inc(pool_init, 1)
            pool.memset(DCA.va, 1.0).then_inc(pool_init, 1)
            for n in range(2):
                pool.wait_ge(dve_kd, 2 * n + 2)
                pool.tensor_scalar(ss1a[:, n, :], ss1a[:, n, :], 1.0 / HD, 1e-6, ALU.mult, ALU.add).then_inc(pool_kd, 1)
                pool.wait_ge(pool_kd, 2 * n + 1)
                pool.tensor_tensor(rs1a[:, n, :], ss1a[:, n, :], nhalf[:, 0:H], ALU.pow).then_inc(pool_kd, 1)
            pool.wait_ge(sp_wx1, 12 * 16)
            with pool.Fori(0, NT // G) as i:
                js = [i * G + g for g in range(G)]
                for g, j in enumerate(js):
                    wait(pool, pe_v, 2 * NT + i * G - 1)
                    pool.sem_inc(pool_beat, 1)
                    pool.tensor_copy(yds[:, g, :], ydT[:, bass.ds(2 * NDCA * j, 2 * NDCA)]).then_inc(pool_yd.sem, 1)
                norm(js, 4 * NT, 1e-5)
                for g, j in enumerate(js):
                    wait(pool, dve_q1ss, j)
                    rsqrt_rows(rs1a[0:R, g, :], ss1a[0:R, g, :], R, H, pool_q1v, pool_q1r, j)
            wait(pool, dve_x, 5 * NT - 1)

            def key_norms_1(b, t):
                n_rows = rows_in(1, t)
                wait(pool, dve_k1ss, b * CT + t)
                wait(pool, dve_k1n, b * CT + t - 2)
                pool.sem_inc(pool_beat, 1)
                pool.tensor_scalar(vek[0:n_rows, t % 2, :], ssr[0:n_rows, t % 2, :], 1.0 / HD, 1e-6, ALU.mult, ALU.add)\
                    .then_inc(pool_k1v.sem, 1)
                wait(pool, pool_k1v, b * CT + t)
                pool.tensor_tensor(rkr[0:n_rows, t % 2, :], vek[0:n_rows, t % 2, :], nhalf[0:n_rows, 0:H], ALU.pow)\
                    .then_inc(pool_k1r.sem, 1)

            for t in range(CT):
                key_norms_1(0, t)
            with pool.Fori(1, B) as b:
                for t in range(CT):
                    key_norms_1(b, t)
                    less_maximum(1, b - 1, t)
            for t in range(CT):
                less_maximum(1, B - 1, t)
            stage_outputs(1)

            with pool.Fori(0, NT // G) as i:
                norm([i * G + g for g in range(G)], 5 * NT, 1e-5)


def layout(v):
    f = {n: np.asarray(t) for n, t in v.items()}

    def chunks(w):
        return np.ascontiguousarray(w.reshape(-1, P, w.shape[1]).transpose(1, 0, 2))

    def column(b):
        return np.ascontiguousarray(b.reshape(-1, P).T)

    out = {
        "x": f["x"].reshape(B * S, D),
        "wq0": chunks(f["L0_attn_Wq"].T), "wk0": chunks(f["L0_attn_Wk"].T), "wv0": chunks(f["L0_attn_Wv"].T),
        "wo0": chunks(f["L0_attn_Wo"].T),
        "bqk0": np.stack([column(f["L0_attn_bq"]), column(f["L0_attn_bk"])], axis=1),
        "bv0": f["L0_attn_bv"], "slopes": f["L0_attn_alibi_slopes"],
        "rows": np.stack([f["L0_attn_bo"], f["L0_ffn_bias"], f["L1_xattn_bo"], f["L1_xattn_bo"]]),
        "wq_x0": chunks(f["L0_xattn_Wq"]),
        "wkT_x0": f["L0_xattn_Wk"].reshape(CD, H, XD).transpose(2, 1, 0),
        "wvT_x0": f["L0_xattn_Wv"].reshape(CD, H, XD).transpose(2, 1, 0),
        "wo_x0": f["L0_xattn_Wo"].reshape(H, XD, D).transpose(1, 0, 2),
        "wk_x0": f["L0_xattn_Wk"],
        "ctx": f["ctx_1024"], "ctxT": f["ctx_1024"].transpose(0, 2, 1),
        "gqk": np.stack([f["L0_xattn_gq"], f["L0_xattn_gk"]], axis=1),
    }
    heads = f["L1_attn_W_Q"].reshape(HD, HM, KC, D).transpose(2, 1, 0, 3)
    keys = f["L1_attn_W_K"].reshape(HD, HM, D).transpose(1, 0, 2)
    swap = (np.arange(HD) + HD // 2) % HD
    out.update(
        factors=f["L0_ffn_factors"].reshape(8, KC, P, D).transpose(2, 1, 3, 0).reshape(P, KC * D, 8),
        wq1=chunks(np.concatenate([heads.reshape(D, D), heads[:, :, swap].reshape(D, D)]).T),
        wk1=chunks(np.concatenate([keys.reshape(P, D), keys[:, swap].reshape(P, D)]).T),
        wv1=chunks(f["L1_attn_W_V"].reshape(HD, HM, D).transpose(1, 0, 2).reshape(P, D).T),
        wo1=chunks(f["L1_attn_W_O"].T),
        wq_x1=chunks(f["L1_xattn_Wq"]), wk_x1=f["L1_xattn_Wk"], wkv_d=f["L1_xattn_Wkv_dca"],
        bq_x1=f["L1_xattn_bq"], bk_x1=f["L1_xattn_bk"], bkv_d=f["L1_xattn_bkv_dca"],
        wo_x1=chunks(f["L1_xattn_Wo"]), woh_x1=f["L1_xattn_Wo"].reshape(H, HD, D).transpose(1, 0, 2),
        ydT=f["ctx_1024"][:, C - NDCA:].reshape(B * NDCA, CD).T,
    )
    kv = np.concatenate([f["L1_xattn_Wk"], f["L1_xattn_Wv"]], axis=1).reshape(CD, H, 2, HD)
    bkv = np.concatenate([f["L1_xattn_bk"], f["L1_xattn_bv"]]).reshape(H, 2, HD)
    out.update(
        wk_x1=kv[:, :, 0].reshape(CD, D), bk_x1=bkv[:, 0].reshape(D),
        wvT_x1=kv[:, :, 1].transpose(2, 1, 0), bvcol=column(bkv[:, 1].reshape(D)),
        lncol=np.stack([np.concatenate([f[n]] * HM) for n in (
            "L1_xattn_qn_w", "L1_xattn_qn_b", "L1_xattn_kn_w", "L1_xattn_kn_b", "L1_xattn_kn_dca_w", "L1_xattn_kn_dca_b")], axis=1),
        w13=np.stack([chunks(np.concatenate([f[e].reshape(E * FI, D), f[w]]).T)
                      for e, w in (("L1_ffn_w1", "L1_ffn_ws_gate"), ("L1_ffn_w3", "L1_ffn_ws_up"))], axis=2),
        w2=chunks(np.concatenate([f["L1_ffn_w2"].transpose(0, 2, 1).reshape(E * FI, D), f["L1_ffn_ws_down"].T])),
        wr=chunks(np.concatenate([f["L1_ffn_gate_w"], f["L1_ffn_shared_gate_w"]]).T),
    )
    row = np.arange(P)
    q = (row % SL).astype(np.float32)
    key = np.arange(S, dtype=np.float32)
    d = row % HD
    half = HD // 2
    inv = (1.0 / 10000.0 ** (np.arange(half, dtype=np.float32) * 2.0 / HD)).astype(np.float32)
    pos = (np.arange(R) % S).astype(np.float32)
    ang = (pos[None, :] * inv[d % half][:, None]).astype(np.float32)
    sign = np.where(d < half, -1.0, 1.0).astype(np.float32)
    out.update(
        ident=np.eye(P, dtype=np.float32),
        hmask=(row[:, None] // HD == np.arange(HM)[None, :]).astype(np.float32),
        rel=(key[None, :] - q[:, None]).astype(np.float32),
        causal=(key[None, :] <= q[:, None]).astype(np.float32),
        eidx=np.broadcast_to(np.arange(E, dtype=np.float32), (P, E)),
        cosT=np.cos(ang), sinT=np.sin(ang) * sign[:, None],
    )
    return {n: np.ascontiguousarray(t) for n, t in out.items()}


def kernel(**inputs):
    import concourse.bacc as bacc
    from concourse.bass_utils import run_bass_kernel_spmd

    nc = bacc.Bacc("TRN2", target_bir_lowering=False, num_devices=1)
    arrays, aps = {}, {}
    for name, v in layout(inputs).items():
        arrays[f"in_{name}_dram"] = v
        aps[name] = nc.dram_tensor(f"in_{name}_dram", v.shape, mybir.dt.from_np(v.dtype), kind="ExternalInput").ap()
    result = nc.dram_tensor("out_dram", (B * S, D), F32, kind="ExternalOutput").ap()
    build(nc, aps, result)
    r = run_bass_kernel_spmd(nc, [arrays], core_ids=[0])
    return r.results[0]["out_dram"].reshape(B, S, D)
```

```python
from contextlib import ExitStack

import numpy as np

import concourse.bass as bass
from concourse import mybir
from concourse.alu_op_type import AluOpType as ALU

ACT = mybir.ActivationFunctionType
AX = mybir.AxisListType
F32 = mybir.dt.float32
F32R = mybir.dt.float32r
U32 = mybir.dt.uint32

P = 128
B, S, D = 16, 56, 256
R = 2 * S
NT = B // 2
G = 2
SL = 64
H, HD = 16, 16
HM = 8
KC = D // P
W = HM * S
C = 1500
CD = 128
CR = 125
CT = C // CR
NDCA = 16
XD = 128
E, FI = 16, 64
FA = E * FI + D
EW = FA // FI
CHUNK = 3
CREDIT = 6
ACC = 8
SQ = (H - ACC) // 4
LAG = (3, 3)
LESS = (1, 1)
DIFF = (4 * S, 11 * S)


class Step:

    def __init__(self, sem, n=1):
        self.sem, self.n = sem, n

    def credit(self, eng):
        eng.sem_inc(self.sem, CREDIT * self.n)

    def done(self, index):
        return (index + 1 + CREDIT) * self.n


def wait(eng, step, index):
    eng.wait_ge(step.sem, step.done(index))


def rows_in(layer, t):
    return CR if layer == 0 else min(CR, C - NDCA - t * CR)


def at_first(b):
    return isinstance(b, int) and b == 0


def split_now(X, b, u, stage, ahead):
    now = []
    for c in range(CT // CHUNK):
        free = CHUNK * (c + 1) + (LAG[0] if X == 0 else 0)
        if free < CT + LAG[X] and free == u and ahead:
            now.append((b + 1, c))
        if free >= CT + LAG[X] and free - CT - LAG[X] == u and stage and not at_first(b):
            now.append((b, c))
    return now


class Buffers:

    def __init__(self, T, PT, va, Km, qT, Z, mx, rc, cx, cT):
        self.T, self.PT, self.va, self.Km, self.qT = T, PT, va, Km, qT
        self.Z, self.mx, self.rc, self.cx, self.cT = Z, mx, rc, cx, cT


def build(nc, a, out):
    ctx = ExitStack()
    with ctx:
        def sb(name, shape, dt=F32):
            return ctx.enter_context(nc.sbuf_tensor(name, shape, dt))

        def sem(name):
            return ctx.enter_context(nc.semaphore(name))

        by_engine = {"pe": [], "act": [], "dve": [], "pool": [], "sp": []}

        def step(name, n=1):
            s = Step(sem(name), n)
            by_engine[name.split("_")[0]].append(s)
            return s

        PS = ctx.enter_context(nc.psum_tensor("PS", [P, 8, 512], F32))

        x = sb("x", [P, NT, D])
        ident = sb("ident", [P, P])
        ones = sb("ones", [P, P])
        hmask = sb("hmask", [P, HM])
        cosT = sb("cosT", [P, R])
        sinT = sb("sinT", [P, R])
        causal = sb("causal", [P, S])
        rel = sb("rel", [P, S])
        slopes = sb("slopes", [P, H])
        eidx = sb("eidx", [P, E])
        bqk0 = sb("bqk0", [P, 2, KC])
        rows = sb("rows", [P, D])
        w_hi, w_lo = (sb(n, [P, H * XD], F32R) for n in ("w_hi", "w_lo"))
        c_hi, c_lo = (sb(n, [P, C], F32R) for n in ("c_hi", "c_lo"))
        q_hi, q_lo = (sb(n, [P, 2, W], F32R) for n in ("q_hi", "q_lo"))
        b_hi, b_lo = (w[0:1, 2 * D:3 * D] for w in (w_hi, w_lo))
        ones_r = w_hi[0:1, 3 * D:3 * D + P]
        keyT = sb("keyT", [P, 3, KC, CR])
        bk_x1 = sb("bk_x1", [P, D])
        lncol = sb("lncol", [P, 6])
        bvcol = sb("bvcol", [P, KC])
        gqk = sb("gqk", [P, 2])
        vo = sb("vo", [P, H, D])

        lnst = sb("lnst", [P, G, 6])
        lnmv = sb("lnmv", [P, G, 2])
        lnve = sb("lnve", [P, G])
        lnrs = sb("lnrs", [P, G])
        xn = sb("xn", [P, G, D])
        xT = sb("xT", [P, G, KC, R])
        nhalf = sb("nhalf", [P, 64])

        QREG = B * H * S
        SREG = CT * H * S
        MREG = 4 * H * S + KC * D
        CREG = 1024 + C + CT * CD
        big = sb("big", [P, QREG + SREG + MREG + CREG])
        used = {}

        def region(start, size):
            used[start] = 0

            def take(*shape, dt=None):
                n = int(np.prod(shape))
                at = start + used[start]
                used[start] += n
                assert used[start] <= size, (start, used[start], size)
                v = big[:, at:at + n]
                names = "abcde"[:len(shape)]
                if len(shape) > 1:
                    v = v.rearrange(f"p ({' '.join(names)}) -> p {' '.join(names)}",
                                    **{names[i]: shape[i] for i in range(1, len(shape))})
                return v
            return take

        Q0, S0, M0, C0 = 0, QREG, QREG + SREG, QREG + SREG + MREG

        def attention_buffers(first, second, third, T):
            return Buffers(T, first(G, H, P), second(G, 2, H, HD + 1), second(G, 2, KC, HM * T), second(G, KC, S + SL),
                           second(G, H * T), third(G, H), third(G, H), third(G, D), third(G, KC, R))

        take = region(Q0, QREG)
        SA = attention_buffers(take, take, take, S)
        rope = take(3, KC, R)
        abias = take(H, S)
        take = region(C0, CREG)
        wq0, wk0, wv0, wo0 = (take(KC, D) for _ in range(4))
        bv0 = take(D)
        take = region(Q0, QREG)
        th = take(G, FA)
        hm = take(G, FA)
        hT = take(G, FA // P, R)
        lg = take(G, H + 1)
        le = take(G, H)
        lm = take(G, 1)
        top = take(G, 8)
        topi = sb("topi", [P, G, 8], U32)
        topf = take(G, 8)
        tw = take(G, 4)
        hot = take(G, 2, E)
        comb = take(G, EW)
        take = region(S0, SREG)
        factors = take(KC * D, 8)
        take = region(S0, SREG)
        w13 = take(KC, 2, FA)
        w2 = take(FA // P, D)
        wr = take(KC, E + 1)
        take = region(S0, SREG)
        wq_x1 = take(KC, D)
        wkv_d = take(2 * D)
        wvT_x1 = take(H, CD)
        woh_x1 = take(H, D)
        wo_x1 = take(KC, D)
        ydT = take(B * NDCA)
        kTd = take(KC, B * NDCA)
        bq_x1 = take(D)
        bkv_d = take(2 * D)
        qs = take(G, D)
        sq1a = take(G, D)
        mean = take(2 * D // HD)
        wk_x1 = take(D)
        take_c = region(C0, CREG)
        kd = take_c(2, D)
        yds = take_c(G, 2 * NDCA)
        ss1a = take_c(G, H)
        rs1a = take_c(G, H)
        take = region(M0, MREG)
        DCA = attention_buffers(region(S0 + KC * D + 2 * D + H * CD, H * D), take, take_c, NDCA)

        take = region(S0, SREG)
        wq_x0 = take(KC, H * XD)
        wkT_x0 = take(H, CD)
        wvT_x0 = take(H, CD)
        take = region(M0, MREG)
        wo_x0 = take(H, D)
        qn_a = region(S0 + KC * H * XD + 2 * H * CD, H * XD)(H, XD)
        take = region(C0, CREG)
        sq_a = take(H * XD)
        qhT = take(H, R)
        ss_a = take(G, H)
        rq_a = take(G, H)
        wk_x0 = vo[:, 0:H // 2, :].rearrange("p h d -> p (h d)")
        take = region(Q0, QREG)
        Qall = take(B, 2, W)
        take = region(S0, SREG)
        Sall = take(CT, 2 * W)
        take = region(M0, MREG)
        Mx = take(2 * W)
        Mb = take(2 * W)
        Zs = take(2 * W)
        rz = take(2 * W)
        take = region(M0 + 4 * H * S, KC * D)
        fmix = take(KC, D)
        take = region(C0, CREG)
        sqr = take(2, 512)
        squared = sqr.rearrange("p a n -> p (a n)")[:, 3 * D:4 * D]

        def centred(t):
            return sqr.rearrange("p a n -> p (a n)")[:, (t % 3) * D:(t % 3 + 1) * D]

        cxT = take(C)
        cxn = take(CT, CD)
        scrap = sb("scrap", [P, XD])
        ssr = sb("ssr", [P, 2, H])
        vek = sb("vek", [P, 2, H])
        rkr = sb("rkr", [P, 6, H])
        mcol = sb("mcol", [P, 8])
        zcol = sb("zcol", [P, 8])
        mdiag = sb("mdiag", [P, 7, P])
        take = region(M0, MREG)
        OTs = take(G, H, R)
        flat = vo[:, :, :].rearrange("p h d -> p (h d)")
        wq1 = flat[:, 0:2 * KC * D].rearrange("p (k n) -> p k n", k=KC)
        wk1 = flat[:, 2 * KC * D:3 * KC * D].rearrange("p (k n) -> p k n", k=KC)
        wv1 = flat[:, 3 * KC * D:3 * KC * D + KC * P].rearrange("p (k n) -> p k n", k=KC)
        wo1 = flat[:, 3 * KC * D + KC * P:4 * KC * D + KC * P].rearrange("p (k n) -> p k n", k=KC)
        sp_const = sem("sp_const")
        sp_x = sem("sp_x")
        sp_w0 = sem("sp_w0")
        sp_wx0 = sem("sp_wx0")
        sp_fac = sem("sp_fac")
        sp_w1 = sem("sp_w1")
        sp_out = sem("sp_out")
        pool_init = sem("pool_init")
        pe_beat, dve_beat, pool_beat = sem("pe_beat"), sem("dve_beat"), sem("pool_beat")
        dve_setup = sem("dve_setup")
        dve_x = step("dve_x")
        dve_stats, dve_aggr, dve_xn = step("dve_stats"), step("dve_aggr"), step("dve_xn")
        pool_ve, pool_rs = step("pool_ve"), step("pool_rs")
        pe_xT, act_xT = step("pe_xT"), step("act_xT")
        pe_y = step("pe_y")
        pe_q, pe_k, pe_v = step("pe_q"), step("pe_k"), step("pe_v")
        act_q = step("act_q", KC)
        dve_km0, dve_km1 = step("dve_km0", 4), step("dve_km1", 2)
        dve_va = step("dve_va")
        dve_rope, dve_qk1 = step("dve_rope", 4), step("dve_qk1", 2)
        pe_s, dve_mx, dve_z = step("pe_s"), step("dve_mx"), step("dve_z")
        act_tanh, act_e, dve_p = step("act_tanh"), step("act_e"), step("dve_p")
        pe_pT, act_pT, dve_pT = step("pe_pT"), step("act_pT"), step("dve_pT")
        pe_o, dve_rc, dve_cx = step("pe_o"), step("dve_rc"), step("dve_cx")
        pe_cT, act_cT = step("pe_cT"), step("act_cT")
        pe_qx, act_sqa, dve_ssa = step("pe_qx"), step("act_sqa"), step("dve_ssa")
        pool_vea, pool_rqa = step("pool_vea"), step("pool_rqa")
        dve_qh = step("dve_qh")
        pe_qhT, act_qhT, pe_qt, dve_qt = step("pe_qhT"), step("act_qhT"), step("pe_qt"), step("dve_qt")
        pe_vo, dve_vo = step("pe_vo"), step("dve_vo")
        sp_cxT = [step(f"sp_cxT{c}", 16) for c in range(CT // CHUNK)]
        sp_cxn = [step(f"sp_cxn{c}", 16) for c in range(CT // CHUNK)]
        act_whi, dve_wlo = sem("act_whi"), sem("dve_wlo")
        act_chi, dve_clo, act_qhi, dve_qlo = step("act_chi"), step("dve_clo"), step("act_qhi"), step("dve_qlo")
        pe_kp, act_sq, dve_ss = step("pe_kp"), step("act_sq"), step("dve_ss")
        pool_vek, pool_rk = step("pool_vek"), step("pool_rk")
        pe_sx, dve_t, dve_mxr = step("pe_sx"), step("dve_t"), step("dve_mxr")
        pool_d, dve_d, act_p, dve_sum, pe_pv = (
            step("pool_d"), step("dve_d"), step("act_p"), step("dve_sum"), step("pe_pv"))
        pe_mT, dve_mcol, dve_diag, pe_mb, act_mb = (
            step("pe_mT"), step("dve_mcol", 2), step("dve_diag", 2), step("pe_mb", 2), step("act_mb", 2))
        pe_zc, dve_zcol, dve_zdiag, pe_zb, act_rz, act_un, dve_ot = (
            step("pe_zc"), step("dve_zcol"), step("dve_zdiag", 2), step("pe_zb", 2), step("act_rz"), step("act_un"), step("dve_ot"))
        act_ots, pool_ots = step("act_ots"), step("pool_ots")
        sp_wx1, pe_kd, dve_kd, act_kd, pool_kd, pe_kdT = (
            sem("sp_wx1"), sem("pe_kd"), sem("dve_kd"), sem("act_kd"), sem("pool_kd"), sem("pe_kdT"))
        pe_q1, dve_qs, act_q1s, dve_q1ss = step("pe_q1"), step("dve_qs"), step("act_q1s"), step("dve_q1ss")
        pool_q1v, pool_q1r, dve_q1n, pe_q1T = step("pool_q1v"), step("pool_q1r"), step("dve_q1n"), step("pe_q1T")
        act_q1, dve_q1m, dve_kmd, pool_yd = step("act_q1"), step("dve_q1m", 4), step("dve_kmd", 4), step("pool_yd")
        pe_k1, act_k1c, act_k1s, dve_k1ss = step("pe_k1"), step("act_k1c"), step("act_k1s"), step("dve_k1ss")
        pool_k1v, pool_k1r, dve_k1n, pe_k1T, act_k1T = (
            step("pool_k1v"), step("pool_k1r"), step("dve_k1n"), step("pe_k1T"), step("act_k1T"))
        act_scrap = step("act_scrap")
        act_t = step("act_t")
        sp_moe = sem("sp_moe")
        pe_lg, dve_lg, dve_lm, dve_le, act_le = step("pe_lg"), step("dve_lg"), step("dve_lm"), step("dve_le"), step("act_le", 2)
        dve_top, dve_topi, dve_topf, dve_tw, dve_hot, dve_comb = (
            step("dve_top"), step("dve_topi"), step("dve_topf"), step("dve_tw", 3), step("dve_hot", 2), step("dve_comb", 2))
        pe_h, act_th, dve_h, pe_hT, act_hT, dve_hT = (
            step("pe_h"), step("act_th"), step("dve_h", 3), step("pe_hT"), step("act_hT"), step("dve_hT"))

        block = ctx.enter_context(nc.Block())

        @block.sync
        def _(sp):
            for s in by_engine["sp"]:
                s.credit(sp)
            sp.dma_start(x[0:R, :, :], a["x"].rearrange("(j r) c -> r j c", r=R)).then_inc(sp_x, 16)
            for dst, name in ((ident, "ident"), (wq0, "wq0"), (wk0, "wk0"), (wv0, "wv0"), (bqk0, "bqk0")):
                sp.dma_start(dst[:], a[name]).then_inc(sp_w0, 16)
            sp.dma_start(bv0[:, :], a["bv0"].partition_broadcast(P)).then_inc(sp_w0, 16)
            for dst, name in ((hmask, "hmask"), (causal, "causal"), (rel, "rel"), (wo0, "wo0"), (cosT, "cosT"), (sinT, "sinT"), (eidx, "eidx")):
                sp.dma_start(dst[:], a[name]).then_inc(sp_w0, 16)
            sp.dma_start(rows[0:P:32, :], a["rows"]).then_inc(sp_w0, 16)
            sp.dma_start(slopes[:, :], a["slopes"].partition_broadcast(P)).then_inc(sp_w0, 16)
            for dst, name in ((wq_x0, "wq_x0"), (wkT_x0, "wkT_x0"), (wvT_x0, "wvT_x0"), (wo_x0, "wo_x0"),
                              (wk_x0, "wk_x0"), (gqk, "gqk"), (lncol, "lncol"), (bvcol, "bvcol")):
                sp.dma_start(dst[:], a[name]).then_inc(sp_wx0, 16)

            def context(X):
                def part(b, c):
                    span = slice(c * CHUNK * CR, (c + 1) * CHUNK * CR)
                    sp.dma_start(cxT[:, span], a["ctxT"][b, :, span]).then_inc(sp_cxT[c].sem, 16)

                def part_rows(b, c):
                    span = slice(c * CHUNK * CR, (c + 1) * CHUNK * CR)
                    sp.dma_start(cxn[0:CR, c * CHUNK:(c + 1) * CHUNK, :],
                                 a["ctx"][b, span, :].rearrange("(t r) c -> r t c", r=CR)).then_inc(sp_cxn[c].sem, 16)

                def parts(b):
                    for c in range(CT // CHUNK):
                        wait(sp, act_chi, (X * B + b - 1) * (CT // CHUNK) + c)
                        wait(sp, dve_clo, (X * B + b - 1) * (CT // CHUNK) + c)
                        part(b, c)

                def parts_rows(b):
                    for c in range(CT // CHUNK):
                        wait(sp, pe_pv, (X * B + b - 1) * CT + CHUNK * c + CHUNK - 1)
                        part_rows(b, c)

                for c in range(CT // CHUNK):
                    part(0, c)
                for c in range(CT // CHUNK):
                    part_rows(0, c)
                parts(1)
                with sp.Fori(1, B - 1) as b:
                    parts(b + 1)
                    parts_rows(b)
                parts_rows(B - 1)

            wait(sp, pe_qt, 4 * NT - 1)
            context(0)
            wait(sp, dve_ot, B - 1)
            sp.dma_start(factors, a["factors"]).then_inc(sp_fac, 16)
            wait(sp, pe_y, 2 * NT - 1)
            for dst, name in ((wq1, "wq1"), (wk1, "wk1"), (wv1, "wv1"), (wo1, "wo1")):
                sp.dma_start(dst, a[name]).then_inc(sp_w1, 16)
            sp.wait_ge(dve_setup, 4)
            for dst, name in ((wq_x1, "wq_x1"), (wkv_d, "wkv_d"), (wo_x1, "wo_x1"), (ydT, "ydT"),
                              (wk_x1, "wk_x1")):
                sp.dma_start(dst, a[name]).then_inc(sp_wx1, 16)
            sp.dma_start(wvT_x1[0:HD], a["wvT_x1"]).then_inc(sp_wx1, 16)
            sp.dma_start(woh_x1[0:HD], a["woh_x1"]).then_inc(sp_wx1, 16)
            for dst, name in ((bq_x1, "bq_x1"), (bkv_d, "bkv_d"), (bk_x1, "bk_x1")):
                sp.dma_start(dst[:, :], a[name].partition_broadcast(P)).then_inc(sp_wx1, 16)
            wait(sp, dve_x, 5 * NT - 1)
            context(1)
            wait(sp, dve_ot, 2 * B - 1)
            for dst, name in ((w13, "w13"), (w2, "w2"), (wr, "wr")):
                sp.dma_start(dst, a[name]).then_inc(sp_moe, 16)

            wait(sp, dve_x, 7 * NT - 1)
            sp.dma_start(out.rearrange("(j r) c -> r j c", r=R), x[0:R, :, :]).then_inc(sp_out, 16)
            sp.wait_ge(sp_out, 16)

        @block.tensor
        def _(pe):
            for s in by_engine["pe"]:
                s.credit(pe)

            def norm_T(js, L):
                for g, j in enumerate(js):
                    wait(pe, dve_xn, L + j)
                    wait(pe, act_xT, L + j - 1)
                    for k in range(KC):
                        ins = pe.transpose(PS[:, 0, k * R:(k + 1) * R], xn[0:R, g, k * P:(k + 1) * P],
                                           ident[0:R, 0:R])
                    ins.then_inc(pe_xT.sem, 1)

            def attention(js, U, V, J, ready, wout, row):
                T = V.T
                for g, j in enumerate(js):
                    for s, n in ready:
                        wait(pe, s, n + j)
                    wait(pe, dve_z, U + j - 1)
                    for b in range(2):
                        for m in range(KC):
                            ins = pe.matmul(PS[SL * b:SL * b + SL, 3 + m, 0:HM * T], V.qT[:, g, m, S * b:S * b + SL],
                                            V.Km[:, g, b, 0 if U == NT else m],
                                            start=True, stop=True)
                    ins.then_inc(pe_s.sem, 1)
                for g, j in enumerate(js):
                    if U == 0:
                        wait(pe, dve_p, j)
                    else:
                        wait(pe, act_e, U + j)
                    for n in range(4):
                        wait(pe, (act_pT, dve_pT)[n % 2], (U + j) * 2 + n // 2 - 1)
                        pe.sem_inc(pe_beat, 1)
                        for h in range(4):
                            s0 = (4 * n + h) * T
                            ins = pe.transpose(PS[0:T, 5 + n % 2, h * P:(h + 1) * P], V.Z[:, g, s0:s0 + T],
                                               ident[:, :])
                        ins.then_inc(pe_pT.sem, 1)
                for g, j in enumerate(js):
                    wait(pe, act_pT, (U + j) * 2 + 1)
                    wait(pe, dve_pT, (U + j) * 2 + 1)
                    wait(pe, dve_va, U + j)
                    wait(pe, dve_cx, U + j - 1)
                    pe.sem_inc(pe_beat, 1)
                    for b in range(2):
                        for h in range(H):
                            vh = h % HM if U == NT else h
                            ins = pe.matmul(PS[SL * b:SL * b + SL, 7, h * (HD + 1):(h + 1) * (HD + 1)],
                                            V.PT[0:T, g, h, SL * b:SL * b + SL], V.va[0:T, g, b, vh, :],
                                            start=True, stop=True, skip_group_check=True)
                    ins.then_inc(pe_o.sem, 1)
                for g, j in enumerate(js):
                    wait(pe, dve_cx, U + j)
                    wait(pe, act_cT, U + j - 1)
                    for k in range(KC):
                        ins = pe.transpose(PS[:, 0, k * P:(k + 1) * P], V.cx[:, g, k * P:(k + 1) * P], ident[:, :])
                    ins.then_inc(pe_cT.sem, 1)
                for g, j in enumerate(js):
                    wait(pe, act_cT, U + j)
                    project(j, J, [V.cT[:, g, k] for k in range(KC)], [wout[:, k, :] for k in range(KC)], row)

            def project(j, J, left, right, row):
                wait(pe, dve_x, J + j - 1)
                for n, (le, ri) in enumerate(zip(left, right)):
                    ins = pe.matmul(PS[0:R, 2, 0:D], le, ri, start=(n == 0), stop=(row is None and n == len(left) - 1))
                if row is not None:
                    ins = pe.matmul(PS[0:R, 2, 0:D], ones[32 * row:32 * row + 1, 0:R], rows[32 * row:32 * row + 1, :], start=False, stop=True)
                ins.then_inc(pe_y.sem, 1)

            pe.wait_ge(sp_w0, 15 * 16)
            pe.wait_ge(pool_init, 4)
            with pe.Fori(0, NT // G) as i:
                js = [i * G + g for g in range(G)]
                norm_T(js, 0)
                for g, j in enumerate(js):
                    wait(pe, act_xT, j)
                    wait(pe, act_q, j - 1)
                    for m in range(KC):
                        for k in range(KC):
                            ins = pe.matmul(PS[:, 1, m * R:(m + 1) * R], wq0[:, k, m * P:(m + 1) * P],
                                            xT[:, g, k], start=(k == 0), stop=(k == KC - 1))
                    ins.then_inc(pe_q.sem, 1)
                    wait(pe, dve_km0, j - 1)
                    wait(pe, dve_cx, i * G - 1)
                    for m in range(KC):
                        for k in range(KC):
                            ins = pe.matmul(PS[:, 7, m * R:(m + 1) * R], wk0[:, k, m * P:(m + 1) * P],
                                            xT[:, g, k], start=(k == 0), stop=(k == KC - 1))
                    ins.then_inc(pe_k.sem, 1)
                    wait(pe, dve_va, j - 1)
                    wait(pe, dve_x, i * G - 1)
                    for b in range(2):
                        for k in range(KC):
                            ins = pe.matmul(PS[0:S, 2, b * D:(b + 1) * D], xT[:, g, k, b * S:(b + 1) * S], wv0[:, k, :],
                                            start=(k == 0), stop=(k == KC - 1))
                    ins.then_inc(pe_v.sem, 1)
                attention(js, 0, SA, 0, [(act_q, 0), (dve_km0, 0)], wo0, 0)

            def value_output(pairs, wvT, wo, V):
                for n in range(H // 2):
                    wait(pe, dve_vo, V + n - 2)
                    for h in range(2):
                        ins = pe.matmul(PS[:, 6 + n % 2, h * D:(h + 1) * D], wvT[0:pairs, 2 * n + h, :], wo[0:pairs, 2 * n + h, :],
                                        start=True, stop=True, skip_group_check=True)
                    ins.then_inc(pe_vo.sem, 1)

            def three_passes(out, left, right, more=False):
                (l_hi, l_lo), (r_hi, r_lo) = left, right
                pe.matmul(out, l_hi, r_hi, start=True, stop=False)
                pe.matmul(out, l_hi, r_lo, start=False, stop=False)
                return pe.matmul(out, l_lo, r_hi, start=False, stop=not more)

            def context_part(X, b, t):
                if t % CHUNK == 0:
                    wait(pe, act_chi, (X * B + b) * (CT // CHUNK) + t // CHUNK)
                    wait(pe, dve_clo, (X * B + b) * (CT // CHUNK) + t // CHUNK)

            def tile_of(t, n_rows):
                return [c[:, t * CR:t * CR + n_rows] for c in (c_hi, c_lo)]

            def keys(b, t, half):
                K = b * CT + t
                context_part(0, b, t)
                for n in (0, 1) if half == 0 else (2, 3):
                    wait(pe, act_sq, K * 4 + n - 2)
                    three_passes(PS[0:CR, n % 2, :], tile_of(t, CR), [w[:, n * 512:(n + 1) * 512] for w in (w_hi, w_lo)])\
                        .then_inc(pe_kp.sem, 1)

            def scores(b, t):
                K = b * CT + t
                if t == 0:
                    wait(pe, act_qhi, b)
                    wait(pe, dve_qlo, b)
                wait(pe, dve_t, K - 1)
                for m in range(2):
                    ins = three_passes(PS[0:CR, 2 + m, 0:W], tile_of(t, CR), (q_hi[:, m, :], q_lo[:, m, :]))
                ins.then_inc(pe_sx.sem, 1)

            def keys_1(b, t):
                k = b * CT + t
                context_part(1, b, t)
                wait(pe, act_k1s, k - 1)
                n_rows = rows_in(1, t)
                three_passes(PS[0:n_rows, 0, 0:D], tile_of(t, n_rows), (w_hi[:, 0:D], w_lo[:, 0:D]), more=True)
                pe.matmul(PS[0:n_rows, 0, 0:D], ones_r[:, 0:n_rows], b_hi, start=False, stop=False)
                pe.matmul(PS[0:n_rows, 0, 0:D], ones_r[:, 0:n_rows], b_lo, start=False, stop=True).then_inc(pe_k1.sem, 1)

            def keys_1T(b, t):
                n_rows = rows_in(1, t)
                wait(pe, dve_k1n, b * CT + t)
                wait(pe, act_k1T, b * CT + t - 1)
                for m in range(KC):
                    ins = pe.transpose(PS[:, 1, m * CR:m * CR + n_rows],
                                       centred(t)[0:n_rows, m * P:(m + 1) * P], ident[0:n_rows, 0:n_rows])
                ins.then_inc(pe_k1T.sem, 1)

            def scores_1(b, t):
                n_rows = rows_in(1, t)
                wait(pe, act_k1T, b * CT + t)
                wait(pe, act_t, b * CT + t - 1)
                for m in range(2):
                    ins = pe.matmul(PS[0:n_rows, 2 + m, 0:W], keyT[:, t % 3, m, 0:n_rows], Qall[:, b, m, :],
                                    start=True, stop=True)
                ins.then_inc(pe_sx.sem, 1)

            def weighted_context(X, b, t):
                K = (X * B + b) * CT + t
                n_rows = rows_in(X, t)
                if t % CHUNK == 0:
                    wait(pe, sp_cxn[t // CHUNK], X * B + b)
                if t == 0:
                    wait(pe, act_un, X * B + b - 1)
                wait(pe, act_p, K)
                for m in range(2):
                    ins = pe.matmul(PS[:, 4 + m, 0:W], cxn[0:n_rows, t, :], Sall[0:n_rows, t, m * W:(m + 1) * W],
                                    start=(t == 0), stop=(t == CT - 1))
                ins.then_inc(pe_pv.sem, 1)

            def maxima_T(u):
                wait(pe, dve_mxr, u * CT + CT - 1)
                for q in range(7):
                    ins = pe.transpose(PS[:, 6 + q // 4, (q % 4) * CR:(q % 4 + 1) * CR], Mx[0:CR, q * P:(q + 1) * P],
                                       ident[0:CR, 0:CR])
                ins.then_inc(pe_mT.sem, 1)

            def to_all_partitions(ready, u, done):
                for m in range(2):
                    pe.wait_ge(ready.sem, ready.done(u) - 1 + m)
                    pe.matmul(PS[:, 6 + m, 0:W], ones[:, :],
                              mdiag[:, :, :].rearrange("p a q -> p (a q)")[:, m * W:(m + 1) * W], start=True, stop=True)\
                        .then_inc(done.sem, 1)

            def sum_columns(u):
                wait(pe, dve_sum, u * CT + CT - 1)
                for q in range(7):
                    ins = pe.matmul(PS[:, 7, 4 * CR + q:4 * CR + q + 1], Zs[0:CR, q * P:(q + 1) * P], ones[0:CR, 0:1],
                                    start=True, stop=True, skip_group_check=True)
                ins.then_inc(pe_zc.sem, 1)

            def cross_attention(X):
                def iteration(b, stage, before, sums):
                    u0 = X * B + b
                    for u in range(CT + LAG[X]):
                        if stage and u < CT:
                            if X == 0:
                                keys(b, u, 0)
                            else:
                                keys_1(b, u)
                        if before and 3 <= u < CT + 3:
                            weighted_context(X, b - 1, u - 3)
                        if stage and X == 1 and 2 <= u < CT + 2:
                            keys_1T(b, u - 2)
                        if u == 0 and (before or sums):
                            wait(pe, act_rz, u0 - 3)
                        if u == 0 and sums:
                            sum_columns(u0 - 2)
                        if u == 0 and before:
                            maxima_T(u0 - 1)
                        if u == 1 and before:
                            to_all_partitions(dve_diag, u0 - 1, pe_mb)
                        if stage and X == 0 and u < CT:
                            keys(b, u, 1)
                        if u >= LAG[X] and stage:
                            (scores, scores_1)[X](b, u - LAG[X])
                        if u == LAG[X] + 2 and sums:
                            if before:
                                wait(pe, act_mb, u0 - 1)
                            to_all_partitions(dve_zdiag, u0 - 2, pe_zb)

                iteration(0, True, False, False)
                iteration(1, True, True, False)
                with pe.Fori(2, B) as b:
                    iteration(b, True, True, True)
                iteration(B, False, True, True)
                iteration(B + 1, False, False, True)

            def output_rows(X, J, row):
                with pe.Fori(0, NT // G) as i:
                    for g in range(G):
                        j = i * G + g
                        wait(pe, act_ots, X * NT + j)
                        wait(pe, pool_ots, X * NT + j)
                        project(j, J, [OTs[:, g, h, :] for h in range(H)], [vo[:, h, :] for h in range(H)], row)

            pe.wait_ge(sp_wx0, 8 * 16)
            wait(pe, dve_x, NT - 1)
            value_output(P, wvT_x0, wo_x0, 0)
            pe.wait_ge(dve_setup, 2)
            with pe.Fori(0, NT // G) as i:
                js = [i * G + g for g in range(G)]
                norm_T(js, NT)
                for u in range(4 * G + 3):
                    if u < 4 * G:
                        g, n, k4 = u // 4, u % 4, 4 * js[0] + u
                        if n == 0:
                            wait(pe, act_xT, NT + js[g])
                        wait(pe, dve_qh, k4 - 4)
                        for k in range(KC):
                            ins = pe.matmul(PS[0:R, 1 + n, :], xT[:, g, k], wq_x0[:, k, n * 512:(n + 1) * 512],
                                            start=(k == 0), stop=(k == KC - 1))
                        ins.then_inc(pe_qx.sem, 1)
                    if 2 <= u < 4 * G + 2:
                        n, k4 = (u - 2) % 4, 4 * js[0] + u - 2
                        wait(pe, dve_qh, k4)
                        wait(pe, act_qhT, k4 - 2)
                        for h in range(4):
                            ins = pe.transpose(PS[:, 5 + n % 2, h * R:(h + 1) * R], qn_a[0:R, 4 * n + h, :],
                                               ident[0:R, 0:R])
                        ins.then_inc(pe_qhT.sem, 1)
                    if u >= 3:
                        n, k4 = (u - 3) % 4, 4 * js[0] + u - 3
                        wait(pe, act_qhT, k4)
                        wait(pe, dve_qt, k4 - 1)
                        for h in range(4 * n, 4 * n + 4):
                            ins = pe.matmul(PS[:, 7, (h % 4) * R:(h % 4 + 1) * R], wkT_x0[:, h, :], qhT[:, h, :],
                                            start=True, stop=True, skip_group_check=True)
                        ins.then_inc(pe_qt.sem, 1)
            wait(pe, dve_qt, 4 * NT - 1)
            pe.wait_ge(dve_wlo, 1)
            cross_attention(0)
            output_rows(0, NT, None)

            pe.wait_ge(dve_setup, 4)
            with pe.Fori(0, NT // G) as i:
                js = [i * G + g for g in range(G)]
                norm_T(js, 2 * NT)
                for g, j in enumerate(js):
                    wait(pe, act_xT, 2 * NT + j)
                    project(j, 2 * NT, [xT[:, g, k] for k in range(KC)], [fmix[:, k, :] for k in range(KC)], 1)

            pe.wait_ge(sp_w1, 4 * 16)
            pe.wait_ge(pool_init, 6)
            wait(pe, dve_x, 3 * NT - 1)
            with pe.Fori(0, NT // G) as i:
                js = [i * G + g for g in range(G)]
                norm_T(js, 3 * NT)
                for g, j in enumerate(js):
                    wait(pe, act_xT, 3 * NT + j)
                    wait(pe, dve_rope, j - 1)
                    for m in range(2 * KC):
                        for k in range(KC):
                            ins = pe.matmul(PS[:, 1, m * R:(m + 1) * R], wq1[:, k, m * P:(m + 1) * P], xT[:, g, k],
                                            start=(k == 0), stop=(k == KC - 1))
                    ins.then_inc(pe_q.sem, 1)
                    wait(pe, dve_cx, NT + i * G - 1)
                    for m in range(KC):
                        for k in range(KC):
                            ins = pe.matmul(PS[:, 7, m * R:(m + 1) * R], wk1[:, k, m * P:(m + 1) * P], xT[:, g, k],
                                            start=(k == 0), stop=(k == KC - 1))
                    ins.then_inc(pe_k.sem, 1)
                    wait(pe, dve_va, NT + j - 1)
                    wait(pe, dve_x, 3 * NT + i * G - 1)
                    for b in range(2):
                        for k in range(KC):
                            ins = pe.matmul(PS[0:S, 2, b * P:(b + 1) * P], xT[:, g, k, b * S:(b + 1) * S], wv1[:, k, :],
                                            start=(k == 0), stop=(k == KC - 1))
                    ins.then_inc(pe_v.sem, 1)
                attention(js, NT, SA, 3 * NT, [(dve_km1, 0)], wo1, None)

            pe.wait_ge(sp_wx1, 10 * 16)
            wait(pe, dve_x, 4 * NT - 1)
            value_output(HD, wvT_x1, woh_x1, H // 2)
            pe.wait_ge(dve_setup, 13)
            for n in range(2):
                if n:
                    pe.wait_ge(dve_kd, 3 * n - 2)
                pe.matmul(PS[:, 1, 0:D], ydT[:, n * P:(n + 1) * P], wkv_d[:, 0:D], start=True, stop=True)\
                    .then_inc(pe_kd, 1)
            for n in range(2):
                pe.wait_ge(dve_kd, 2 + 2 + n + 1)
                if n:
                    pe.wait_ge(act_kd, 2 + n)
                for m in range(KC):
                    ins = pe.transpose(PS[:, 5, m * P:(m + 1) * P], kd[:, n, m * P:(m + 1) * P], ident[:, :])
                ins.then_inc(pe_kdT, 1)
            pe.wait_ge(act_kd, 4)
            with pe.Fori(0, NT // G) as i:
                js = [i * G + g for g in range(G)]
                norm_T(js, 4 * NT)
                for g, j in enumerate(js):
                    wait(pe, act_xT, 4 * NT + j)
                    wait(pe, dve_qs, j - 1)
                    for k in range(KC):
                        ins = pe.matmul(PS[0:R, 1, 0:D], xT[:, g, k], wq_x1[:, k, :], start=(k == 0), stop=(k == KC - 1))
                    ins.then_inc(pe_q1.sem, 1)
                    wait(pe, pool_yd, j)
                    wait(pe, dve_va, 2 * NT + j - 1)
                    wait(pe, dve_x, 4 * NT + i * G - 1)
                    for b in range(2):
                        ins = pe.matmul(PS[0:NDCA, 2, b * D:(b + 1) * D], yds[:, g, b * NDCA:(b + 1) * NDCA],
                                        wkv_d[:, D:2 * D], start=True, stop=True)
                    ins.then_inc(pe_v.sem, 1)
                for g, j in enumerate(js):
                    wait(pe, dve_q1n, j)
                    wait(pe, act_q1, j - 1)
                    wait(pe, act_pT, 4 * NT + 2 * i * G - 1)
                    for k in range(KC):
                        ins = pe.transpose(PS[:, 5, k * R:(k + 1) * R], qs[0:R, g, k * P:(k + 1) * P], ident[0:R, 0:R])
                    ins.then_inc(pe_q1T.sem, 1)
                attention(js, 2 * NT, DCA, 4 * NT, [(act_q1, 0), (dve_kmd, 0)], wo_x1, 2)
            wait(pe, dve_q1m, NT - 1)
            pe.wait_ge(dve_wlo, 3)
            wait(pe, dve_x, 5 * NT - 1)
            cross_attention(1)
            output_rows(1, 5 * NT, None)

            pe.wait_ge(sp_moe, 3 * 16)
            wait(pe, dve_x, 6 * NT - 1)
            with pe.Fori(0, NT // G) as i:
                js = [i * G + g for g in range(G)]
                norm_T(js, 5 * NT)
                for g, j in enumerate(js):
                    wait(pe, act_xT, 5 * NT + j)
                    wait(pe, dve_lg, j - 1)
                    wait(pe, dve_hT, i * G - 1)
                    for k in range(KC):
                        ins = pe.matmul(PS[0:R, 7, 0:E + 1], xT[:, g, k], wr[:, k, :], start=(k == 0), stop=(k == KC - 1))
                    ins.then_inc(pe_lg.sem, 1)
                for g, j in enumerate(js):
                    wait(pe, dve_h, j - 1)
                    wait(pe, dve_x, 6 * NT + i * G - 1)
                    for w in range(2):
                        for c in range(0, FA, 512):
                            n = min(512, FA - c)
                            for k in range(KC):
                                ins = pe.matmul(PS[0:R, 1 + 3 * w + c // 512, 0:n], xT[:, g, k], w13[:, k, w, c:c + n],
                                                start=(k == 0), stop=(k == KC - 1))
                    ins.then_inc(pe_h.sem, 1)
                for g, j in enumerate(js):
                    wait(pe, dve_h, j)
                    for n in range(3):
                        if n == 0:
                            wait(pe, act_hT, j * 2 - 1)
                            wait(pe, act_xT, 5 * NT + i * G + G - 1)
                        elif n == 1:
                            wait(pe, dve_hT, j - 1)
                            wait(pe, dve_lg, i * G + G - 1)
                        else:
                            wait(pe, act_hT, j * 2)
                        for c in range(4 * n, min(4 * n + 4, FA // P)):
                            ins = pe.transpose(PS[:, 7 if n == 1 else 0, (c % 4) * R:(c % 4 + 1) * R],
                                               hm[0:R, g, c * P:(c + 1) * P], ident[0:R, 0:R])
                        ins.then_inc(pe_hT.sem, 1)
                for g, j in enumerate(js):
                    wait(pe, act_hT, j * 2 + 1)
                    wait(pe, dve_hT, j)
                    project(j, 6 * NT, [hT[:, g, c] for c in range(FA // P)], [w2[:, c, :] for c in range(FA // P)], None)

        @block.scalar
        def _(act):
            for s in by_engine["act"]:
                s.credit(act)

            def norm_T(js, L):
                for g, j in enumerate(js):
                    wait(act, pe_xT, L + j)
                    act.copy(xT[:, g], PS[:, 0, 0:KC * R].rearrange("p (k r) -> p k r", k=KC))\
                       .then_inc(act_xT.sem, 1)

            def attention(js, U, V, scale):
                T = V.T
                for g, j in enumerate(js):
                    z = V.Z[:, g, :]
                    wait(act, dve_z, U + j)
                    if U == 0:
                        act.activation(z, z, ACT.Tanh, scale=1.0 / (30.0 * HD ** 0.5)).then_inc(act_tanh.sem, 1)
                        wait(act, act_tanh, j)
                    act.activation(z, z, ACT.Exp, scale=30.0 if U == 0 else scale).then_inc(act_e.sem, 1)
                for g, j in enumerate(js):
                    for n in (0, 2):
                        wait(act, pe_pT, (U + j) * 4 + n)
                        act.copy(V.PT[0:T, g, 4 * n:4 * n + 4, :], PS[0:T, 5, :].rearrange("p (h q) -> p h q", h=4))\
                           .then_inc(act_pT.sem, 1)
                for g, j in enumerate(js):
                    wait(act, pe_cT, U + j)
                    c = PS[:, 0, 0:KC * P].rearrange("p (k b s) -> p k b s", k=KC, b=2)[:, :, :, 0:S]
                    to = V.cT[:, g].rearrange("p k (b s) -> p k b s", b=2)
                    if U == 2 * NT:
                        act.activation(to[:, 0], c[:, 0], ACT.Identity, bias=bvcol[:, 0:1])
                        act.activation(to[:, 1], c[:, 1], ACT.Identity, bias=bvcol[:, 1:2]).then_inc(act_cT.sem, 1)
                    else:
                        act.copy(to, c).then_inc(act_cT.sem, 1)

            with act.Fori(0, NT // G) as i:
                js = [i * G + g for g in range(G)]
                act.wait_ge(pool_init, 4)
                norm_T(js, 0)
                for g, j in enumerate(js):
                    wait(act, pe_q, j)
                    for m in range(KC):
                        act.activation(SA.qT[:, g, m, 0:R], PS[:, 1, m * R:(m + 1) * R], ACT.Identity,
                                       bias=bqk0[:, 0, m:m + 1]).then_inc(act_q.sem, 1)
                attention(js, 0, SA, None)

            def squares(b, t, half):
                K = b * CT + t
                for n in (0, 1) if half == 0 else (2, 3):
                    wait(act, pe_kp, K * 4 + n)
                    if 4 * n >= ACC:
                        i = n - ACC // 4
                        wait(act, dve_ss, K * SQ + i - 2)
                        act.activation(sqr[0:CR, i % 2, :], PS[0:CR, n % 2, :], ACT.Square).then_inc(act_sq.sem, 1)
                    else:
                        wait(act, pool_vek, K - 2)
                        for h in range(4):
                            wait(act, act_scrap, K * ACC + 4 * n + h - 1)
                            ins = act.activation(scrap[0:CR, :], PS[0:CR, n % 2, h * XD:(h + 1) * XD], ACT.Square,
                                                 accum_out=ssr[0:CR, t % 2, 4 * n + h:4 * n + h + 1])
                            ins.then_inc(act_scrap.sem, 1)
                        wait(act, act_scrap, K * ACC + 4 * n + 3)
                        act.sem_inc(act_sq.sem, 1)

            def key_squares_1(b, t):
                n_rows = rows_in(1, t)
                wait(act, pe_k1, b * CT + t)
                wait(act, pe_k1T, b * CT + t - 3)
                act.copy(centred(t)[0:n_rows, :], PS[0:n_rows, 0, 0:D]).then_inc(act_k1c.sem, 1)
                wait(act, dve_k1ss, b * CT + t - 1)
                act.activation(squared[0:n_rows, :], PS[0:n_rows, 0, 0:D], ACT.Square).then_inc(act_k1s.sem, 1)

            def keys_T(b, t):
                n_rows = rows_in(1, t)
                wait(act, pe_k1T, b * CT + t)
                wait(act, pe_sx, B * CT + b * CT + t - 3)
                act.activation(keyT[:, t % 3, :, 0:n_rows], PS[:, 1, 0:KC * CR].rearrange("p (m r) -> p m r", m=KC)[:, :, 0:n_rows],
                               ACT.Identity, scale=lncol[:, 2:3], bias=lncol[:, 3:4]).then_inc(act_k1T.sem, 1)

            def keep_scores(b, t):
                n_rows = rows_in(1, t)
                K = B * CT + b * CT + t
                wait(act, pe_sx, K)
                wait(act, pe_pv, K - CT)
                wait(act, dve_sum, K - CT)
                act.copy(Sall[0:n_rows, t, :].rearrange("p (m w) -> p m w", m=2), PS[0:n_rows, 2:4, 0:W])\
                   .then_inc(act_t.sem, 1)

            def split_context(X, b, c):
                span = slice(c * CHUNK * CR, (c + 1) * CHUNK * CR)
                wait(act, sp_cxT[c], X * B + b)
                last = (b - 1) * CT + CHUNK * c + CHUNK - 1
                if X == 0 and not at_first(b):
                    wait(act, pe_sx, last)
                elif X == 1 and not at_first(b):
                    wait(act, pe_k1, last)
                act.copy(c_hi[:, span], cxT[:, span]).then_inc(act_chi.sem, 1)

            def split_queries(b):
                if not at_first(b):
                    wait(act, pe_sx, b * CT - 1)
                act.copy(q_hi[:, :, :], Qall[:, b]).then_inc(act_qhi.sem, 1)

            def probabilities(X, b, t, scale):
                K = (X * B + b) * CT + t
                n_rows = rows_in(X, t)
                wait(act, pool_d, K)
                wait(act, dve_d, K)
                p = Sall[0:n_rows, t, :]
                act.activation(p, p, ACT.Exp, scale=scale).then_inc(act_p.sem, 1)

            def keep_maxima(X, b):
                u = X * B + b
                if X == 1 or not at_first(b):
                    wait(act, pool_d, u * CT - 1)
                    wait(act, dve_d, u * CT - 1)
                for m in range(2):
                    act.wait_ge(pe_mb.sem, pe_mb.done(u) - 1 + m)
                    act.copy(Mb[0:CR, m * W:(m + 1) * W], PS[0:CR, 6 + m, 0:W]).then_inc(act_mb.sem, 1)

            def keep_sums(u):
                wait(act, pe_zb, u)
                wait(act, dve_ot, u - 1)
                act.copy(rz[:, :].rearrange("p (m w) -> p m w", m=2), PS[:, 6:8, 0:W]).then_inc(act_rz.sem, 1)

            def keep_outputs(X, b):
                wait(act, pe_pv, (X * B + b) * CT + CT - 1)
                act.copy(Qall[:, b], PS[:, 4:6, 0:W]).then_inc(act_un.sem, 1)

            def cross_attention(X):
                def iteration(b, stage, before, sums, ahead):
                    for u in range(CT + LAG[X]):
                        if stage and X == 0 and u == 2:
                            split_queries(b)
                        if stage and u < CT:
                            if X == 0:
                                squares(b, u, 0)
                            else:
                                key_squares_1(b, u)
                        if u == 1 and before:
                            keep_maxima(X, b - 1)
                        if X == 0 and u == 2 and before:
                            probabilities(X, b - 1, 0, XD ** -0.5)
                        if stage and X == 0 and u < CT:
                            squares(b, u, 1)
                        for c in split_now(X, b, u, stage, ahead):
                            split_context(X, *c)
                        if stage and X == 1 and 2 <= u < CT + 2:
                            keys_T(b, u - 2)
                        if before and 3 - X <= u < CT + 2:
                            probabilities(X, b - 1, u - 2, (XD, HD)[X] ** -0.5)
                        if stage and X == 1 and u >= LAG[X]:
                            keep_scores(b, u - LAG[X])
                        if u == CT + LAG[X] - 1 and before:
                            keep_outputs(X, b - 1)
                        if u == LAG[X] + 2 and sums:
                            keep_sums(X * B + b - 2)

                for c in range(CT // CHUNK):
                    split_context(X, 0, c)
                iteration(0, True, False, False, True)
                iteration(1, True, True, False, True)
                with act.Fori(2, B - 1) as b:
                    iteration(b, True, True, True, True)
                iteration(B - 1, True, True, True, False)
                iteration(B, False, True, True, False)
                iteration(B + 1, False, False, True, False)

            def stage_outputs(X):
                with act.Fori(0, NT // G) as i:
                    for g in range(G):
                        j = i * G + g
                        wait(act, dve_ot, X * B + B - 1)
                        wait(act, pe_y, (1 if X == 0 else 5) * NT + j - G)
                        act.copy(OTs[:, g, :, 0:S], Qall[:, 2 * j].rearrange("p m (h s) -> p (m h) s", h=HM))\
                           .then_inc(act_ots.sem, 1)

            act.wait_ge(sp_wx0, 8 * 16)
            act.copy(w_hi[:, :], wk_x0).then_inc(act_whi, 1)
            with act.Fori(0, NT // G) as i:
                js = [i * G + g for g in range(G)]
                norm_T(js, NT)
                for u in range(4 * G + 2):
                    if u < 4 * G:
                        n, k4 = u % 4, 4 * js[0] + u
                        wait(act, pe_qx, k4)
                        wait(act, dve_ssa, k4 - 4)
                        act.activation(sq_a[0:R, n * 512:(n + 1) * 512], PS[0:R, 1 + n, :], ACT.Square)\
                           .then_inc(act_sqa.sem, 1)
                    if u >= 2:
                        n, k4 = (u - 2) % 4, 4 * js[0] + u - 2
                        wait(act, pe_qhT, k4)
                        wait(act, pe_qt, k4 - 4)
                        act.copy(qhT[:, 4 * n:4 * n + 4, :], PS[:, 5 + n % 2, 0:4 * R].rearrange("p (h r) -> p h r", h=4))\
                           .then_inc(act_qhT.sem, 1)
            wait(act, pe_qt, 4 * NT - 1)
            cross_attention(0)
            stage_outputs(0)

            with act.Fori(0, NT // G) as i:
                norm_T([i * G + g for g in range(G)], 2 * NT)

            act.wait_ge(pool_init, 6)
            with act.Fori(0, NT // G) as i:
                js = [i * G + g for g in range(G)]
                norm_T(js, 3 * NT)
                attention(js, NT, SA, D ** -0.5)

            act.wait_ge(sp_wx1, 10 * 16)
            act.wait_ge(dve_setup, 13)
            act.copy(w_hi[:, 0:D], wk_x1).then_inc(act_whi, 1)
            act.wait_ge(dve_setup, 22)
            act.copy(b_hi, bk_x1[0:1, :]).then_inc(act_whi, 1)
            act.copy(ones_r, ones[0:1, :]).then_inc(act_whi, 1)
            for n in range(2):
                act.wait_ge(dve_kd, 2 * n + 1 if n == 0 else 3)
                act.activation(sq1a[:, n, :], kd[:, n, :], ACT.Square).then_inc(act_kd, 1)
            for n in range(2):
                act.wait_ge(pe_kdT, n + 1)
                act.activation(kTd[:, :, n * P:(n + 1) * P], PS[:, 5, 0:KC * P].rearrange("p (m r) -> p m r", m=KC),
                               ACT.Identity, scale=lncol[:, 4:5], bias=lncol[:, 5:6]).then_inc(act_kd, 1)
            act.wait_ge(pool_init, 8)
            with act.Fori(0, NT // G) as i:
                js = [i * G + g for g in range(G)]
                norm_T(js, 4 * NT)
                for g, j in enumerate(js):
                    wait(act, dve_qs, j)
                    act.activation(sq1a[0:R, g, :], qs[0:R, g, :], ACT.Square).then_inc(act_q1s.sem, 1)
                for g, j in enumerate(js):
                    wait(act, pe_q1T, j)
                    act.activation(DCA.qT[:, g, :, 0:R], PS[:, 5, 0:KC * R].rearrange("p (m r) -> p m r", m=KC),
                                   ACT.Identity, scale=lncol[:, 0:1], bias=lncol[:, 1:2]).then_inc(act_q1.sem, 1)
                attention(js, 2 * NT, DCA, HD ** -0.5)
            wait(act, dve_x, 5 * NT - 1)

            cross_attention(1)
            stage_outputs(1)

            with act.Fori(0, NT // G) as i:
                js = [i * G + g for g in range(G)]
                norm_T(js, 5 * NT)
                for g, j in enumerate(js):
                    wait(act, dve_le, j)
                    act.activation(le[0:R, g, :], le[0:R, g, :], ACT.Exp).then_inc(act_le.sem, 1)
                    act.activation(lg[0:R, g, E:E + 1], lg[0:R, g, E:E + 1], ACT.Tanh, scale=0.5).then_inc(act_le.sem, 1)
                for g, j in enumerate(js):
                    wait(act, pe_h, j)
                    act.activation(th[0:R, g, :], PS[0:R, 1:4, :].rearrange("p a n -> p (a n)")[:, 0:FA], ACT.Tanh,
                                   scale=0.5).then_inc(act_th.sem, 1)
                for g, j in enumerate(js):
                    for n in (0, 2):
                        wait(act, pe_hT, j * 3 + n)
                        c = min(4, FA // P - 4 * n)
                        act.copy(hT[:, g, 4 * n:4 * n + c, :], PS[:, 0, 0:c * R].rearrange("p (c r) -> p c r", c=c))\
                           .then_inc(act_hT.sem, 1)

        @block.vector
        def _(dve):
            for s in by_engine["dve"]:
                s.credit(dve)

            def norm(js, L, J):
                for g, j in enumerate(js):
                    if J > 0:
                        wait(dve, dve_x, J - NT + j)
                    dve.bn_stats(lnst[0:R, g, :], x[0:R, j, :]).then_inc(dve_stats.sem, 1)
                for g, j in enumerate(js):
                    wait(dve, dve_stats, L + j)
                    dve.sem_inc(dve_beat, 1)
                    dve.bn_aggr(lnmv[0:R, g, :], lnst[0:R, g, :]).then_inc(dve_aggr.sem, 1)
                for g, j in enumerate(js):
                    wait(dve, pool_rs, L + j)
                    dve.tensor_scalar(xn[0:R, g, :], x[0:R, j, :], lnmv[0:R, g, 0:1], lnrs[0:R, g:g + 1],
                                      ALU.subtract, ALU.mult).then_inc(dve_xn.sem, 1)

            def head_sel(T):
                return hmask[:, :].unsqueeze(2).broadcast_to([P, HM, T])

            def attention(js, U, V):
                T = V.T
                for g, j in enumerate(js):
                    wait(dve, pe_s, U + j)
                    s = PS[:, 3:5, 0:HM * T]
                    z = V.Z[:, g, :].rearrange("p (m z) -> p m z", m=KC)
                    if U == 0:
                        dve.tensor_tensor(z, s, abias[:, :, :].rearrange("p (m h) t -> p m (h t)", m=KC), ALU.add)\
                           .then_inc(dve_z.sem, 1)
                    else:
                        s = s.rearrange("p m (h t) -> p m h t", h=HM)
                        z = z.rearrange("p m (h t) -> p m h t", h=HM)
                        largest = V.mx[:, g, :].rearrange("p (m h) -> p m h", m=KC)
                        dve.tensor_reduce(largest, s, AX.X, ALU.max).then_inc(dve_mx.sem, 1)
                        wait(dve, dve_mx, U - NT + j)
                        dve.tensor_tensor(z, s, largest.unsqueeze(3).broadcast_to([P, KC, HM, T]), ALU.subtract)\
                           .then_inc(dve_z.sem, 1)
                for g, j in enumerate(js):
                    if U == 0:
                        wait(dve, act_e, j)
                        z = V.Z[:, g, :].rearrange("p (h t) -> p h t", h=H)
                        dve.tensor_tensor(z, z, causal[:, :].unsqueeze(1).broadcast_to([P, H, S]), ALU.mult)\
                           .then_inc(dve_p.sem, 1)
                for g, j in enumerate(js):
                    for n in (1, 3):
                        wait(dve, pe_pT, (U + j) * 4 + n)
                        dve.tensor_copy(V.PT[0:T, g, 4 * n:4 * n + 4, :], PS[0:T, 6, :].rearrange("p (h q) -> p h q", h=4))\
                           .then_inc(dve_pT.sem, 1)
                for g, j in enumerate(js):
                    wait(dve, pe_o, U + j)
                    o = PS[:, 7, 0:H * (HD + 1)].rearrange("p (h d) -> p h d", h=H)
                    dve.reciprocal(V.rc[:, g, :], o[:, :, HD]).then_inc(dve_rc.sem, 1)
                    wait(dve, dve_rc, U + j)
                    if U == NT:
                        dve.tensor_tensor(V.cx[:, g, :].rearrange("p (h m d) -> p m h d", h=HM, m=KC),
                                          o[:, :, 0:HD].rearrange("p (m h) d -> p m h d", m=KC),
                                          V.rc[:, g, :].rearrange("p (m h) -> p m h", m=KC).unsqueeze(3)
                                          .broadcast_to([P, KC, HM, HD]), ALU.mult).then_inc(dve_cx.sem, 1)
                    else:
                        dve.tensor_tensor(V.cx[:, g, :].rearrange("p (h d) -> p h d", h=H), o[:, :, 0:HD],
                                          V.rc[:, g, :].unsqueeze(2).broadcast_to([P, H, HD]), ALU.mult)\
                           .then_inc(dve_cx.sem, 1)

            def add_rows(js, J):
                for g, j in enumerate(js):
                    wait(dve, pe_y, J + j)
                    dve.tensor_tensor(x[0:R, j, :], x[0:R, j, :], PS[0:R, 2, 0:D], ALU.add).then_inc(dve_x.sem, 1)

            dve.wait_ge(sp_w0, 15 * 16)
            dve.wait_ge(sp_x, 16)
            dve.wait_ge(pool_init, 4)
            dve.tensor_tensor(abias[:, :, :], rel[:, :].unsqueeze(1).broadcast_to([P, H, S]),
                              slopes[:, :].unsqueeze(2).broadcast_to([P, H, S]), ALU.mult).then_inc(dve_setup, 1)
            dve.wait_ge(dve_setup, 1)
            with dve.Fori(0, NT // G) as i:
                js = [i * G + g for g in range(G)]
                norm(js, 0, 0)
                for g, j in enumerate(js):
                    wait(dve, pe_k, j)
                    for b in range(2):
                        for m in range(KC):
                            kb = PS[:, 7, m * R + b * S:m * R + b * S + S]
                            dve.scalar_tensor_tensor(SA.Km[:, g, b, m].rearrange("p (h t) -> p h t", h=HM), kb.unsqueeze(1).broadcast_to([P, HM, S]),
                                                     bqk0[:, 1, m:m + 1], head_sel(S), ALU.add, ALU.mult)\
                               .then_inc(dve_km0.sem, 1)
                    wait(dve, pe_v, j)
                    dve.tensor_tensor(SA.va[0:S, g, :, :, 0:HD],
                                      PS[0:S, 2, :].rearrange("p (b h d) -> p b h d", b=2, h=H),
                                      bv0[0:S, :].rearrange("p (h d) -> p h d", h=H).unsqueeze(1)
                                      .broadcast_to([S, 2, H, HD]), ALU.add).then_inc(dve_va.sem, 1)
                attention(js, 0, SA)
                add_rows(js, 0)

            def value_output(V):
                for n in range(H // 2):
                    wait(dve, pe_vo, V + n)
                    dve.tensor_copy(vo[:, 2 * n:2 * n + 2, :], PS[:, 6 + n % 2, :].rearrange("p (h d) -> p h d", h=2))\
                       .then_inc(dve_vo.sem, 1)

            def by_head(row):
                return row.rearrange("p (m h) -> p m h", m=2).unsqueeze(3).broadcast_to([row.shape[0], 2, HM, S])

            def key_norms(b, t):
                K = b * CT + t
                wait(dve, pool_vek, K - 2)
                for n in range(ACC // 4, 4):
                    wait(dve, act_sq, K * 4 + n)
                    dve.tensor_reduce(ssr[0:CR, t % 2, 4 * n:4 * n + 4],
                                      sqr[0:CR, (n - ACC // 4) % 2, :].rearrange("p (h d) -> p h d", h=4), AX.X, ALU.add)\
                       .then_inc(dve_ss.sem, 1)

            def scores(b, t):
                K = b * CT + t
                wait(dve, pool_rk, K)
                wait(dve, pe_sx, K)
                if not isinstance(b, int) or b > 0:
                    wait(dve, pe_pv, K - CT)
                    wait(dve, dve_sum, K - CT)
                dve.tensor_tensor(Sall[0:CR, t, :].rearrange("p (m h s) -> p m h s", m=2, h=HM),
                                  PS[0:CR, 2:4, 0:W].rearrange("p m (h s) -> p m h s", h=HM),
                                  by_head(rkr[0:CR, t % 6, :]), ALU.mult).then_inc(dve_t.sem, 1)

            def running_maximum(X, b, t):
                K = (X * B + b) * CT + t
                n_rows = rows_in(X, t)
                if X == 0:
                    wait(dve, dve_t, K)
                else:
                    wait(dve, act_t, b * CT + t)
                if t == 0:
                    wait(dve, pe_mT, X * B + b - 1)
                    dve.tensor_copy(Mx[0:CR, :], Sall[0:CR, 0, :]).then_inc(dve_mxr.sem, 1)
                else:
                    wait(dve, dve_mxr, K - 1)
                    dve.tensor_tensor(Mx[0:n_rows, :], Mx[0:n_rows, :], Sall[0:n_rows, t, :], ALU.max)\
                       .then_inc(dve_mxr.sem, 1)

            def sum_probabilities(X, b, t):
                K = (X * B + b) * CT + t
                n_rows = rows_in(X, t)
                wait(dve, act_p, K)
                if t == 0:
                    wait(dve, pe_zc, X * B + b - 1)
                    dve.tensor_copy(Zs[0:CR, :], Sall[0:CR, 0, :]).then_inc(dve_sum.sem, 1)
                else:
                    wait(dve, dve_sum, K - 1)
                    dve.tensor_tensor(Zs[0:n_rows, :], Zs[0:n_rows, :], Sall[0:n_rows, t, :], ALU.add)\
                       .then_inc(dve_sum.sem, 1)

            def spread(v, rows, T):
                return v.unsqueeze(2).broadcast_to([rows, H, T])

            def diagonal(col, after, n, done):
                wait(dve, after, n)
                for q in (slice(0, 4), slice(4, 7)):
                    size = q.stop - q.start
                    dve.tensor_tensor(mdiag[:, q, :], ident[:, :].unsqueeze(1).broadcast_to([P, size, P]),
                                      col[:, q].unsqueeze(2).broadcast_to([P, size, P]), ALU.mult).then_inc(done.sem, 1)

            def maxima(u):
                wait(dve, pe_mT, u)
                for bank, n in ((6, 4), (7, 3)):
                    dve.tensor_reduce(mcol[:, 4 * (bank - 6):4 * (bank - 6) + n],
                                      PS[:, bank, 0:n * CR].rearrange("p (a r) -> p a r", a=n), AX.X, ALU.max)\
                       .then_inc(dve_mcol.sem, 1)
                wait(dve, dve_mcol, u)

            def reciprocal_sums(u):
                wait(dve, pe_zc, u)
                dve.reciprocal(zcol[:, 0:7], PS[:, 7, 4 * CR:4 * CR + 7]).then_inc(dve_zcol.sem, 1)

            def outputs(X, b):
                wait(dve, act_rz, X * B + b)
                wait(dve, act_un, X * B + b)
                o = Qall[:, b].rearrange("p m w -> p (m w)")
                dve.tensor_tensor(o, o, rz[:, :], ALU.mult).then_inc(dve_ot.sem, 1)

            def split_context(X, b, c):
                span = slice(c * CHUNK * CR, (c + 1) * CHUNK * CR)
                wait(dve, act_chi, (X * B + b) * (CT // CHUNK) + c)
                dve.tensor_tensor(c_lo[:, span], cxT[:, span], c_hi[:, span].bitcast(F32), ALU.subtract)\
                   .then_inc(dve_clo.sem, 1)

            def split_queries(b):
                wait(dve, act_qhi, b)
                dve.tensor_tensor(q_lo[:, :, :], Qall[:, b], q_hi[:, :, :].bitcast(F32), ALU.subtract)\
                   .then_inc(dve_qlo.sem, 1)

            def key_sums(b, t):
                n_rows = rows_in(1, t)
                wait(dve, act_k1s, b * CT + t)
                wait(dve, pool_k1v, b * CT + t - 2)
                dve.tensor_reduce(ssr[0:n_rows, t % 2, :], squared[0:n_rows, :].rearrange("p (h d) -> p h d", h=H),
                                  AX.X, ALU.add).then_inc(dve_k1ss.sem, 1)

            def normal_keys(b, t):
                n_rows = rows_in(1, t)
                wait(dve, pool_k1r, b * CT + t)
                wait(dve, act_k1c, b * CT + t)
                k = centred(t)[0:n_rows, :].rearrange("p (h d) -> p h d", h=H)
                dve.tensor_tensor(k, k, spread(rkr[0:n_rows, t % 6, :], n_rows, HD), ALU.mult).then_inc(dve_k1n.sem, 1)

            def less_maximum(X, b, t):
                K = (X * B + b) * CT + t
                n_rows = rows_in(X, t)
                if t == 0:
                    wait(dve, act_mb, X * B + b)
                wait(dve, dve_mxr, K)
                s = Sall[0:n_rows, t, 0:DIFF[X]]
                dve.tensor_tensor(s, s, Mb[0:n_rows, 0:DIFF[X]], ALU.subtract).then_inc(dve_d.sem, 1)

            def cross_attention(X):
                def iteration(b, stage, before, sums, ahead):
                    u0 = X * B + b
                    for u in range(CT + LAG[X]):
                        if stage and X == 1 and u == 0:
                            key_sums(b, 0)
                        if u == 0 and before:
                            maxima(u0 - 1)
                        if u == 0 and sums:
                            reciprocal_sums(u0 - 2)
                        if u == 0 and before:
                            diagonal(mcol, pe_zb, u0 - 3, dve_diag)
                        if stage and X == 0 and u == 2:
                            split_queries(b)
                        if stage and X == 0 and u < CT:
                            key_norms(b, u)
                        if stage and X == 1 and 2 <= u < CT + 2:
                            normal_keys(b, u - 2)
                        if stage and X == 1 and 1 <= u < CT:
                            key_sums(b, u)
                        for c in split_now(X, b, u, stage, ahead):
                            split_context(X, *c)
                        if before and 0 <= u - LESS[X] < CT:
                            less_maximum(X, b - 1, u - LESS[X])
                        if before and 3 <= u < CT + 3:
                            sum_probabilities(X, b - 1, u - 3)
                        if stage and X == 0 and u >= LAG[X]:
                            scores(b, u - LAG[X])
                            running_maximum(X, b, u - LAG[X])
                        if stage and X == 1 and u > LAG[X]:
                            running_maximum(X, b, u - LAG[X] - 1)
                        if stage and X == 1 and u == CT + LAG[X] - 1:
                            running_maximum(X, b, u - LAG[X])
                        if u == LAG[X] + 1 and sums:
                            wait(dve, dve_zcol, u0 - 2)
                            diagonal(zcol, pe_mb, u0 - 1 if before else u0 - 2, dve_zdiag)
                        if u == LAG[X] + 3 and sums:
                            outputs(X, b - 2)

                for c in range(CT // CHUNK):
                    split_context(X, 0, c)
                iteration(0, True, False, False, True)
                iteration(1, True, True, False, True)
                with dve.Fori(2, B - 1) as b:
                    iteration(b, True, True, True, True)
                iteration(B - 1, True, True, True, False)
                iteration(B, False, True, True, False)
                iteration(B + 1, False, False, True, False)

            dve.wait_ge(sp_wx0, 8 * 16)
            dve.tensor_scalar(wkT_x0, wkT_x0, gqk[:, 0:1], gqk[:, 1:2], ALU.mult, ALU.mult).then_inc(dve_setup, 1)
            dve.wait_ge(act_whi, 1)
            dve.tensor_tensor(w_lo[:, :], wk_x0, w_hi[:, :].bitcast(F32), ALU.subtract).then_inc(dve_wlo, 1)
            dve.wait_ge(dve_wlo, 1)
            value_output(0)
            with dve.Fori(0, NT // G) as i:
                js = [i * G + g for g in range(G)]
                norm(js, NT, NT)
                for u in range(4 * G + 3):
                    if u < 4 * G:
                        g, n, k4 = u // 4, u % 4, 4 * js[0] + u
                        wait(dve, act_sqa, k4)
                        dve.tensor_reduce(ss_a[0:R, g, 4 * n:4 * n + 4],
                                          sq_a[0:R, n * 512:(n + 1) * 512].rearrange("p (h d) -> p h d", h=4),
                                          AX.X, ALU.add).then_inc(dve_ssa.sem, 1)
                    if 1 <= u <= 4 * G:
                        g, n, k4 = (u - 1) // 4, (u - 1) % 4, 4 * js[0] + u - 1
                        wait(dve, pool_rqa, k4)
                        wait(dve, pe_qhT, k4 - 4)
                        dve.tensor_tensor(qn_a[0:R, 4 * n:4 * n + 4, :], PS[0:R, 1 + n, :].rearrange("p (h d) -> p h d", h=4),
                                          rq_a[0:R, g, 4 * n:4 * n + 4].unsqueeze(2).broadcast_to([R, 4, XD]), ALU.mult)\
                           .then_inc(dve_qh.sem, 1)
                    if u >= 3:
                        g, n, k4 = (u - 3) // 4, (u - 3) % 4, 4 * js[0] + u - 3
                        wait(dve, pe_qt, k4)
                        q = Qall[:, bass.ds(2 * js[g], 2)].rearrange("p b m (h s) -> p (m h) b s", h=HM)
                        dve.tensor_copy(q[:, 4 * n:4 * n + 4],
                                        PS[:, 7, 0:4 * R].rearrange("p (h b s) -> p h b s", h=4, b=2))\
                           .then_inc(dve_qt.sem, 1)
            cross_attention(0)
            with dve.Fori(0, NT // G) as i:
                add_rows([i * G + g for g in range(G)], NT)

            dve.wait_ge(sp_fac, 16)
            mixed = fmix[:, :, :].rearrange("p k n -> p (k n)")
            dve.tensor_reduce(mixed, factors, AX.X, ALU.add).then_inc(dve_setup, 1)
            dve.wait_ge(dve_setup, 3)
            dve.tensor_scalar(mixed, mixed, 8 ** -0.5, None, ALU.mult).then_inc(dve_setup, 1)
            with dve.Fori(0, NT // G) as i:
                js = [i * G + g for g in range(G)]
                norm(js, 2 * NT, 2 * NT)
                add_rows(js, 2 * NT)

            dve.wait_ge(pool_init, 6)
            with dve.Fori(0, NT // G) as i:
                js = [i * G + g for g in range(G)]
                norm(js, 3 * NT, 3 * NT)
                for g, j in enumerate(js):
                    wait(dve, pe_q, NT + j)
                    q = PS[:, 1, 0:2 * KC * R].rearrange("p (z r) -> p z r", z=2 * KC)
                    along = lambda tab: tab[:, :].unsqueeze(1).broadcast_to([P, KC, R])
                    dve.tensor_tensor(rope[:, 0], q[:, 0:KC], along(cosT), ALU.mult).then_inc(dve_rope.sem, 1)
                    dve.tensor_tensor(rope[:, 1], q[:, KC:2 * KC], along(sinT), ALU.mult).then_inc(dve_rope.sem, 1)
                    wait(dve, pe_k, NT + j)
                    dve.tensor_tensor(rope[:, 2, 0], PS[:, 7, 0:R], cosT[:, :], ALU.mult).then_inc(dve_rope.sem, 1)
                    dve.tensor_tensor(rope[:, 2, 1], PS[:, 7, R:2 * R], sinT[:, :], ALU.mult).then_inc(dve_rope.sem, 1)
                    wait(dve, dve_rope, j)
                    dve.tensor_tensor(SA.qT[:, g, :, 0:R], rope[:, 0], rope[:, 1], ALU.add).then_inc(dve_qk1.sem, 1)
                    dve.tensor_tensor(rope[:, 2, 0], rope[:, 2, 0], rope[:, 2, 1], ALU.add).then_inc(dve_qk1.sem, 1)
                    wait(dve, dve_qk1, j)
                    for b in range(2):
                        dve.tensor_tensor(SA.Km[:, g, b, 0].rearrange("p (h t) -> p h t", h=HM),
                                          rope[:, 2, 0, b * S:(b + 1) * S].unsqueeze(1).broadcast_to([P, HM, S]),
                                          head_sel(S), ALU.mult).then_inc(dve_km1.sem, 1)
                    wait(dve, dve_km1, j)
                    wait(dve, pe_v, NT + j)
                    dve.tensor_copy(SA.va[0:S, g, :, 0:HM, 0:HD],
                                    PS[0:S, 2, 0:2 * P].rearrange("p (b h d) -> p b h d", b=2, h=HM)).then_inc(dve_va.sem, 1)
                attention(js, NT, SA)
                add_rows(js, 3 * NT)

            def centre(v, n, at):
                v = v.rearrange("p (n d) -> p n d", d=HD)
                dve.wait_ge(dve_setup, at)
                dve.tensor_reduce(mean[:, 0:n], v, AX.X, ALU.add).then_inc(dve_setup, 1)
                dve.wait_ge(dve_setup, at + 1)
                dve.tensor_scalar(mean[:, 0:n], mean[:, 0:n], 1.0 / HD, None, ALU.mult).then_inc(dve_setup, 1)
                dve.wait_ge(dve_setup, at + 2)
                dve.tensor_tensor(v, v, mean[:, 0:n].unsqueeze(2).broadcast_to([P, n, HD]), ALU.subtract)\
                   .then_inc(dve_setup, 1)

            dve.wait_ge(sp_wx1, 10 * 16)
            centre(wq_x1.rearrange("p k n -> p (k n)"), KC * H, 4)
            centre(wkv_d[:, 0:D], H, 7)
            centre(wk_x1, H, 10)
            centre(bq_x1, H, 13)
            centre(bkv_d[:, 0:D], H, 16)
            centre(bk_x1, H, 19)
            dve.wait_ge(dve_setup, 22)
            dve.wait_ge(act_whi, 4)
            dve.tensor_tensor(b_lo, bk_x1[0:1, :], b_hi.bitcast(F32), ALU.subtract).then_inc(dve_wlo, 1)
            dve.tensor_tensor(w_lo[:, 0:D], wk_x1, w_hi[:, 0:D].bitcast(F32), ALU.subtract).then_inc(dve_wlo, 1)
            value_output(H // 2)
            for n in range(2):
                dve.wait_ge(pe_kd, n + 1)
                dve.tensor_tensor(kd[:, n, :], PS[:, 1, 0:D], bkv_d[:, 0:D], ALU.add).then_inc(dve_kd, 1)
                dve.wait_ge(act_kd, n + 1)
                dve.tensor_reduce(ss1a[:, n, :], sq1a[:, n, :].rearrange("p (h d) -> p h d", h=H), AX.X, ALU.add)\
                   .then_inc(dve_kd, 1)
            for n in range(2):
                dve.wait_ge(pool_kd, 2 * n + 2)
                dve.tensor_tensor(kd[:, n, :].rearrange("p (h d) -> p h d", h=H), kd[:, n, :].rearrange("p (h d) -> p h d", h=H),
                                  spread(rs1a[:, n, :], P, HD), ALU.mult).then_inc(dve_kd, 1)
            dve.wait_ge(pool_init, 8)
            dve.wait_ge(act_kd, 4)
            with dve.Fori(0, NT // G) as i:
                js = [i * G + g for g in range(G)]
                norm(js, 4 * NT, 4 * NT)
                for g, j in enumerate(js):
                    wait(dve, pe_q1, j)
                    dve.tensor_tensor(qs[0:R, g, :], PS[0:R, 1, 0:D], bq_x1[0:R, :], ALU.add).then_inc(dve_qs.sem, 1)
                    wait(dve, pe_v, 2 * NT + j)
                    dve.tensor_tensor(DCA.va[0:NDCA, g, :, :, 0:HD],
                                      PS[0:NDCA, 2, :].rearrange("p (b h d) -> p b h d", b=2, h=H),
                                      bkv_d[0:NDCA, D:2 * D].rearrange("p (h d) -> p h d", h=H).unsqueeze(1)
                                      .broadcast_to([NDCA, 2, H, HD]), ALU.add).then_inc(dve_va.sem, 1)
                for g, j in enumerate(js):
                    wait(dve, act_q1s, j)
                    dve.tensor_reduce(ss1a[0:R, g, :], sq1a[0:R, g, :].rearrange("p (h d) -> p h d", h=H), AX.X, ALU.add)\
                       .then_inc(dve_q1ss.sem, 1)
                for g, j in enumerate(js):
                    wait(dve, pool_q1r, j)
                    q = qs[0:R, g, :].rearrange("p (h d) -> p h d", h=H)
                    dve.tensor_tensor(q, q, spread(rs1a[0:R, g, :], R, HD), ALU.mult).then_inc(dve_q1n.sem, 1)
                    for b in range(2):
                        for m in range(KC):
                            dve.tensor_tensor(DCA.Km[:, g, b, m].rearrange("p (h t) -> p h t", h=HM),
                                              kTd[:, m, bass.ds((2 * j + b) * NDCA, NDCA)].unsqueeze(1)
                                              .broadcast_to([P, HM, NDCA]), head_sel(NDCA), ALU.mult)\
                               .then_inc(dve_kmd.sem, 1)
                for g, j in enumerate(js):
                    wait(dve, act_q1, j)
                    for b in range(2):
                        for m in range(KC):
                            dve.tensor_tensor(Qall[:, 2 * j + b, m].rearrange("p (h s) -> p h s", h=HM),
                                              DCA.qT[:, g, m, b * S:(b + 1) * S].unsqueeze(1).broadcast_to([P, HM, S]),
                                              head_sel(S), ALU.mult).then_inc(dve_q1m.sem, 1)
                attention(js, 2 * NT, DCA)
                add_rows(js, 4 * NT)

            cross_attention(1)
            with dve.Fori(0, NT // G) as i:
                add_rows([i * G + g for g in range(G)], 5 * NT)

            with dve.Fori(0, NT // G) as i:
                js = [i * G + g for g in range(G)]
                norm(js, 5 * NT, 6 * NT)
                for g, j in enumerate(js):
                    wait(dve, pe_lg, j)
                    dve.tensor_copy(lg[0:R, g, :], PS[0:R, 7, 0:E + 1]).then_inc(dve_lg.sem, 1)
                for g, j in enumerate(js):
                    wait(dve, dve_lg, j)
                    dve.tensor_reduce(lm[0:R, g, :], lg[0:R, g, 0:E], AX.X, ALU.max).then_inc(dve_lm.sem, 1)
                for g, j in enumerate(js):
                    wait(dve, dve_lm, j)
                    dve.tensor_scalar(le[0:R, g, :], lg[0:R, g, 0:E], lm[0:R, g, :], None, ALU.subtract)\
                       .then_inc(dve_le.sem, 1)
                for g, j in enumerate(js):
                    wait(dve, act_le, j)
                    dve.sem_inc(dve_beat, 1)
                    dve.max(top[0:R, g, :], le[0:R, g, :]).then_inc(dve_top.sem, 1)
                    wait(dve, dve_top, j)
                    dve.sem_inc(dve_beat, 1)
                    dve.max_index(topi[0:R, g, :], top[0:R, g, :], le[0:R, g, :]).then_inc(dve_topi.sem, 1)
                    wait(dve, dve_topi, j)
                    dve.tensor_copy(topf[0:R, g, :], topi[0:R, g, :]).then_inc(dve_topf.sem, 1)
                    dve.tensor_tensor(tw[0:R, g, 0:1], top[0:R, g, 0:1], top[0:R, g, 1:2], ALU.add).then_inc(dve_tw.sem, 1)
                    dve.wait_ge(dve_tw.sem, dve_tw.done(j) - 2)
                    dve.reciprocal(tw[0:R, g, 1:2], tw[0:R, g, 0:1]).then_inc(dve_tw.sem, 1)
                    dve.wait_ge(dve_tw.sem, dve_tw.done(j) - 1)
                    dve.tensor_scalar(tw[0:R, g, 2:4], top[0:R, g, 0:2], tw[0:R, g, 1:2], 0.5, ALU.mult, ALU.mult)\
                       .then_inc(dve_tw.sem, 1)
                    wait(dve, dve_tw, j)
                    wait(dve, dve_topf, j)
                    for n in range(2):
                        dve.tensor_scalar(hot[0:R, g, n, :], eidx[0:R, :], topf[0:R, g, n:n + 1], tw[0:R, g, 2 + n:3 + n],
                                          ALU.is_equal, ALU.mult).then_inc(dve_hot.sem, 1)
                    wait(dve, dve_hot, j)
                    dve.tensor_tensor(comb[0:R, g, 0:E], hot[0:R, g, 0, :], hot[0:R, g, 1, :], ALU.add).then_inc(dve_comb.sem, 1)
                    dve.tensor_scalar(comb[0:R, g, E:EW], lg[0:R, g, E:E + 1].broadcast_to([R, EW - E]), 1.0, 0.25,
                                      ALU.add, ALU.mult).then_inc(dve_comb.sem, 1)
                for g, j in enumerate(js):
                    wait(dve, act_th, j)
                    wait(dve, pe_h, j)
                    flat_h = hm[0:R, g, :]
                    h1, h3 = (PS[0:R, c:c + 3, :].rearrange("p a n -> p (a n)")[:, 0:FA] for c in (1, 4))
                    dve.scalar_tensor_tensor(flat_h, th[0:R, g, :], 1.0, h1, ALU.add, ALU.mult).then_inc(dve_h.sem, 1)
                    dve.wait_ge(dve_h.sem, dve_h.done(j) - 2)
                    dve.tensor_tensor(flat_h, flat_h, h3, ALU.mult).then_inc(dve_h.sem, 1)
                    dve.wait_ge(dve_h.sem, dve_h.done(j) - 1)
                    wait(dve, dve_comb, j)
                    blocks = flat_h.rearrange("p (e i) -> p e i", i=FI)
                    dve.tensor_tensor(blocks, blocks, comb[0:R, g, :].unsqueeze(2).broadcast_to([R, EW, FI]), ALU.mult)\
                       .then_inc(dve_h.sem, 1)
                for g, j in enumerate(js):
                    wait(dve, pe_hT, j * 3 + 1)
                    dve.tensor_copy(hT[:, g, 4:8, :], PS[:, 7, 0:4 * R].rearrange("p (c r) -> p c r", c=4)).then_inc(dve_hT.sem, 1)
                add_rows(js, 6 * NT)

        @block.gpsimd
        def _(pool):
            for s in by_engine["pool"]:
                s.credit(pool)
            pool.memset(nhalf[:, :], -0.5).then_inc(pool_init, 1)
            pool.memset(ones[:, :], 1.0).then_inc(pool_init, 1)
            pool.memset(SA.qT, 0.0).then_inc(pool_init, 1)
            pool.memset(SA.va, 1.0).then_inc(pool_init, 1)
            pool.wait_ge(pool_init, 4)

            def norm(js, L, eps):
                for g, j in enumerate(js):
                    wait(pool, dve_aggr, L + j)
                    pool.sem_inc(pool_beat, 1)
                    pool.tensor_scalar(lnve[0:R, g:g + 1], lnmv[0:R, g, 1:2], eps, None, ALU.add).then_inc(pool_ve.sem, 1)
                    wait(pool, pool_ve, L + j)
                    pool.tensor_tensor(lnrs[0:R, g:g + 1], lnve[0:R, g:g + 1], nhalf[0:R, 0:1], ALU.pow)\
                        .then_inc(pool_rs.sem, 1)

            with pool.Fori(0, NT // G) as i:
                norm([i * G + g for g in range(G)], 0, 1e-5)

            def key_norms(b, t):
                K = b * CT + t
                wait(pool, dve_ss, (K + 1) * SQ - 1)
                wait(pool, act_scrap, (K + 1) * ACC - 1)
                wait(pool, dve_t, K - 6)
                pool.sem_inc(pool_beat, 1)
                pool.tensor_scalar(vek[0:CR, t % 2, :], ssr[0:CR, t % 2, :], 1.0 / XD, 1e-5, ALU.mult, ALU.add)\
                    .then_inc(pool_vek.sem, 1)
                wait(pool, pool_vek, K)
                pool.tensor_tensor(rkr[0:CR, t % 6, :], vek[0:CR, t % 2, :], nhalf[0:CR, 0:H], ALU.pow)\
                    .then_inc(pool_rk.sem, 1)

            def less_maximum(X, b, t):
                K = (X * B + b) * CT + t
                n_rows = rows_in(X, t)
                if t == 0:
                    wait(pool, act_mb, X * B + b)
                if X == 0:
                    wait(pool, dve_t, K)
                else:
                    wait(pool, act_t, b * CT + t)
                wait(pool, dve_mxr, K)
                s = Sall[0:n_rows, t, DIFF[X]:]
                pool.tensor_tensor(s, s, Mb[0:n_rows, DIFF[X]:], ALU.subtract).then_inc(pool_d.sem, 1)

            def key_norms_1(b, t):
                n_rows = rows_in(1, t)
                wait(pool, dve_k1ss, b * CT + t)
                wait(pool, dve_k1n, b * CT + t - 2)
                pool.sem_inc(pool_beat, 1)
                pool.tensor_scalar(vek[0:n_rows, t % 2, :], ssr[0:n_rows, t % 2, :], 1.0 / HD, 1e-6, ALU.mult, ALU.add)\
                    .then_inc(pool_k1v.sem, 1)
                wait(pool, pool_k1v, b * CT + t)
                pool.tensor_tensor(rkr[0:n_rows, t % 6, :], vek[0:n_rows, t % 2, :], nhalf[0:n_rows, 0:H], ALU.pow)\
                    .then_inc(pool_k1r.sem, 1)

            def cross_attention(X):
                def iteration(b, stage, before):
                    for u in range(CT + LAG[X]):
                        if X == 1 and stage and u < CT:
                            key_norms_1(b, u)
                        if before and 0 <= u - LESS[X] < CT:
                            less_maximum(X, b - 1, u - LESS[X])
                        if X == 0 and stage and u < CT:
                            key_norms(b, u)

                iteration(0, True, False)
                with pool.Fori(1, B) as b:
                    iteration(b, True, True)
                iteration(B, False, True)

            def stage_outputs(X):
                with pool.Fori(0, NT // G) as i:
                    for g in range(G):
                        j = i * G + g
                        wait(pool, dve_ot, X * B + B - 1)
                        wait(pool, pe_y, (1 if X == 0 else 5) * NT + j - G)
                        pool.sem_inc(pool_beat, 1)
                        pool.tensor_copy(OTs[:, g, :, S:R], Qall[:, 2 * j + 1].rearrange("p m (h s) -> p (m h) s", h=HM))\
                            .then_inc(pool_ots.sem, 1)

            with pool.Fori(0, NT // G) as i:
                js = [i * G + g for g in range(G)]
                norm(js, NT, 1e-5)
                for u in range(4 * G):
                    g, n, k4 = u // 4, u % 4, 4 * js[0] + u
                    heads = slice(4 * n, 4 * n + 4)
                    wait(pool, dve_ssa, k4)
                    pool.sem_inc(pool_beat, 1)
                    pool.tensor_scalar(ss_a[0:R, g, heads], ss_a[0:R, g, heads], 1.0 / XD, 1e-5, ALU.mult, ALU.add)\
                        .then_inc(pool_vea.sem, 1)
                    wait(pool, pool_vea, k4)
                    pool.tensor_tensor(rq_a[0:R, g, heads], ss_a[0:R, g, heads], nhalf[0:R, 0:4], ALU.pow)\
                        .then_inc(pool_rqa.sem, 1)
            wait(pool, pe_qt, 4 * NT - 1)
            cross_attention(0)
            stage_outputs(0)

            with pool.Fori(0, NT // G) as i:
                norm([i * G + g for g in range(G)], 2 * NT, 1e-5)

            wait(pool, act_ots, NT - 1)
            pool.memset(SA.qT, 0.0).then_inc(pool_init, 1)
            pool.memset(SA.va, 1.0).then_inc(pool_init, 1)
            with pool.Fori(0, NT // G) as i:
                norm([i * G + g for g in range(G)], 3 * NT, 1e-5)

            def rsqrt_rows(to, v, rows, n, ready_v, ready_r, index):
                pool.sem_inc(pool_beat, 1)
                pool.tensor_scalar(v, v, 1.0 / HD, 1e-6, ALU.mult, ALU.add).then_inc(ready_v.sem, 1)
                wait(pool, ready_v, index)
                pool.tensor_tensor(to, v, nhalf[0:rows, 0:n], ALU.pow).then_inc(ready_r.sem, 1)

            wait(pool, pe_y, 4 * NT - 1)
            pool.memset(DCA.qT, 0.0).then_inc(pool_init, 1)
            pool.memset(DCA.va, 1.0).then_inc(pool_init, 1)
            for n in range(2):
                pool.wait_ge(dve_kd, 2 * n + 2)
                pool.tensor_scalar(ss1a[:, n, :], ss1a[:, n, :], 1.0 / HD, 1e-6, ALU.mult, ALU.add).then_inc(pool_kd, 1)
                pool.wait_ge(pool_kd, 2 * n + 1)
                pool.tensor_tensor(rs1a[:, n, :], ss1a[:, n, :], nhalf[:, 0:H], ALU.pow).then_inc(pool_kd, 1)
            pool.wait_ge(sp_wx1, 10 * 16)
            with pool.Fori(0, NT // G) as i:
                js = [i * G + g for g in range(G)]
                for g, j in enumerate(js):
                    wait(pool, pe_v, 2 * NT + i * G - 1)
                    pool.sem_inc(pool_beat, 1)
                    pool.tensor_copy(yds[:, g, :], ydT[:, bass.ds(2 * NDCA * j, 2 * NDCA)]).then_inc(pool_yd.sem, 1)
                norm(js, 4 * NT, 1e-5)
                for g, j in enumerate(js):
                    wait(pool, dve_q1ss, j)
                    rsqrt_rows(rs1a[0:R, g, :], ss1a[0:R, g, :], R, H, pool_q1v, pool_q1r, j)
            wait(pool, dve_x, 5 * NT - 1)

            cross_attention(1)
            stage_outputs(1)

            with pool.Fori(0, NT // G) as i:
                norm([i * G + g for g in range(G)], 5 * NT, 1e-5)


def layout(v):
    f = {n: np.asarray(t) for n, t in v.items()}

    def chunks(w):
        return np.ascontiguousarray(w.reshape(-1, P, w.shape[1]).transpose(1, 0, 2))

    def column(b):
        return np.ascontiguousarray(b.reshape(-1, P).T)

    out = {
        "x": f["x"].reshape(B * S, D),
        "wq0": chunks(f["L0_attn_Wq"].T), "wk0": chunks(f["L0_attn_Wk"].T), "wv0": chunks(f["L0_attn_Wv"].T),
        "wo0": chunks(f["L0_attn_Wo"].T),
        "bqk0": np.stack([column(f["L0_attn_bq"]), column(f["L0_attn_bk"])], axis=1),
        "bv0": f["L0_attn_bv"], "slopes": f["L0_attn_alibi_slopes"],
        "rows": np.stack([f["L0_attn_bo"], f["L0_ffn_bias"], f["L1_xattn_bo"], f["L1_xattn_bo"]]),
        "wq_x0": chunks(f["L0_xattn_Wq"]),
        "wkT_x0": f["L0_xattn_Wk"].reshape(CD, H, XD).transpose(2, 1, 0),
        "wvT_x0": f["L0_xattn_Wv"].reshape(CD, H, XD).transpose(2, 1, 0),
        "wo_x0": f["L0_xattn_Wo"].reshape(H, XD, D).transpose(1, 0, 2),
        "wk_x0": f["L0_xattn_Wk"],
        "ctx": f["ctx_1024"], "ctxT": f["ctx_1024"].transpose(0, 2, 1),
        "gqk": np.stack([f["L0_xattn_gq"], f["L0_xattn_gk"]], axis=1),
    }
    heads = f["L1_attn_W_Q"].reshape(HD, HM, KC, D).transpose(2, 1, 0, 3)
    keys = f["L1_attn_W_K"].reshape(HD, HM, D).transpose(1, 0, 2)
    swap = (np.arange(HD) + HD // 2) % HD
    out.update(
        factors=f["L0_ffn_factors"].reshape(8, KC, P, D).transpose(2, 1, 3, 0).reshape(P, KC * D, 8),
        wq1=chunks(np.concatenate([heads.reshape(D, D), heads[:, :, swap].reshape(D, D)]).T),
        wk1=chunks(np.concatenate([keys.reshape(P, D), keys[:, swap].reshape(P, D)]).T),
        wv1=chunks(f["L1_attn_W_V"].reshape(HD, HM, D).transpose(1, 0, 2).reshape(P, D).T),
        wo1=chunks(f["L1_attn_W_O"].T),
        wq_x1=chunks(f["L1_xattn_Wq"]), wk_x1=f["L1_xattn_Wk"], wkv_d=f["L1_xattn_Wkv_dca"],
        bq_x1=f["L1_xattn_bq"], bk_x1=f["L1_xattn_bk"], bkv_d=f["L1_xattn_bkv_dca"],
        wo_x1=chunks(f["L1_xattn_Wo"]), woh_x1=f["L1_xattn_Wo"].reshape(H, HD, D).transpose(1, 0, 2),
        ydT=f["ctx_1024"][:, C - NDCA:].reshape(B * NDCA, CD).T,
    )
    kv = np.concatenate([f["L1_xattn_Wk"], f["L1_xattn_Wv"]], axis=1).reshape(CD, H, 2, HD)
    bkv = np.concatenate([f["L1_xattn_bk"], f["L1_xattn_bv"]]).reshape(H, 2, HD)
    out.update(
        wk_x1=kv[:, :, 0].reshape(CD, D), bk_x1=bkv[:, 0].reshape(D),
        wvT_x1=kv[:, :, 1].transpose(2, 1, 0), bvcol=column(bkv[:, 1].reshape(D)),
        lncol=np.stack([np.concatenate([f[n]] * HM) for n in (
            "L1_xattn_qn_w", "L1_xattn_qn_b", "L1_xattn_kn_w", "L1_xattn_kn_b", "L1_xattn_kn_dca_w", "L1_xattn_kn_dca_b")], axis=1),
        w13=np.stack([chunks(np.concatenate([f[e].reshape(E * FI, D), f[w]]).T)
                      for e, w in (("L1_ffn_w1", "L1_ffn_ws_gate"), ("L1_ffn_w3", "L1_ffn_ws_up"))], axis=2),
        w2=chunks(np.concatenate([f["L1_ffn_w2"].transpose(0, 2, 1).reshape(E * FI, D), f["L1_ffn_ws_down"].T])),
        wr=chunks(np.concatenate([f["L1_ffn_gate_w"], f["L1_ffn_shared_gate_w"]]).T),
    )
    row = np.arange(P)
    q = (row % SL).astype(np.float32)
    key = np.arange(S, dtype=np.float32)
    d = row % HD
    half = HD // 2
    inv = (1.0 / 10000.0 ** (np.arange(half, dtype=np.float32) * 2.0 / HD)).astype(np.float32)
    pos = (np.arange(R) % S).astype(np.float32)
    ang = (pos[None, :] * inv[d % half][:, None]).astype(np.float32)
    sign = np.where(d < half, -1.0, 1.0).astype(np.float32)
    out.update(
        ident=np.eye(P, dtype=np.float32),
        hmask=(row[:, None] // HD == np.arange(HM)[None, :]).astype(np.float32),
        rel=(key[None, :] - q[:, None]).astype(np.float32),
        causal=(key[None, :] <= q[:, None]).astype(np.float32),
        eidx=np.broadcast_to(np.arange(E, dtype=np.float32), (P, E)),
        cosT=np.cos(ang), sinT=np.sin(ang) * sign[:, None],
    )
    return {n: np.ascontiguousarray(t) for n, t in out.items()}


def kernel(**inputs):
    import concourse.bacc as bacc
    from concourse.bass_utils import run_bass_kernel_spmd

    nc = bacc.Bacc("TRN2", target_bir_lowering=False, num_devices=1)
    arrays, aps = {}, {}
    for name, v in layout(inputs).items():
        arrays[f"in_{name}_dram"] = v
        aps[name] = nc.dram_tensor(f"in_{name}_dram", v.shape, mybir.dt.from_np(v.dtype), kind="ExternalInput").ap()
    result = nc.dram_tensor("out_dram", (B * S, D), F32, kind="ExternalOutput").ap()
    build(nc, aps, result)
    r = run_bass_kernel_spmd(nc, [arrays], core_ids=[0])
    return r.results[0]["out_dram"].reshape(B, S, D)
```

```python
from contextlib import ExitStack

import numpy as np

import concourse.bass as bass
from concourse import mybir
from concourse.alu_op_type import AluOpType as ALU

ACT = mybir.ActivationFunctionType
AX = mybir.AxisListType
F32 = mybir.dt.float32
F32R = mybir.dt.float32r
U32 = mybir.dt.uint32

P = 128
B, S, D = 16, 56, 256
R = 2 * S
NT = B // 2
G = 2
SL = 64
H, HD = 16, 16
HM = 8
KC = D // P
W = HM * S
C = 1500
CD = 128
CR = 125
CT = C // CR
NDCA = 16
XD = 128
E, FI = 16, 64
FA = E * FI + D
EW = FA // FI
CHUNK = 3
CREDIT = 6
ACC = [8, 0, 0] + [8] * (CT - 3)
SUMS = [(H - n) // 4 for n in ACC]
assert sum(SUMS) % 2 == 0
LAG, LESS, EXP, PV = 3, 1, 2, 3
Q_BANKS, K_BANKS = (1, 5), (7, 6)
V_BANKS = (2, 7)
PT_BANKS = (5, 6, 0, 1)
CT_BANKS, Y_BANKS = (0, 5), (2, 7)
DIFF = (4 * S, 11 * S)


class Step:

    def __init__(self, sem, n=1):
        self.sem, self.n = sem, n

    def credit(self, eng):
        eng.sem_inc(self.sem, CREDIT * self.n)

    def done(self, index):
        return (index + 1 + CREDIT) * self.n


def wait(eng, step, index):
    eng.wait_ge(step.sem, step.done(index))


def rows_in(layer, t):
    return CR if layer == 0 else min(CR, C - NDCA - t * CR)


def at_first(b):
    return isinstance(b, int) and b == 0


def split_now(X, b, u, stage, ahead):
    now = []
    for c in range(CT // CHUNK):
        free = CHUNK * (c + 1) + (LAG if X == 0 else 0)
        if free < CT + LAG and free == u and ahead:
            now.append((b + 1, c))
        if free >= CT + LAG and free - CT - LAG == u and stage and not at_first(b):
            now.append((b, c))
    return now


class Buffers:

    def __init__(self, T, PT, va, Km, qT, Z, mx, rc, cx, cT):
        self.T, self.PT, self.va, self.Km, self.qT = T, PT, va, Km, qT
        self.Z, self.mx, self.rc, self.cx, self.cT = Z, mx, rc, cx, cT


def build(nc, a, out):
    ctx = ExitStack()
    with ctx:
        def sb(name, shape, dt=F32):
            return ctx.enter_context(nc.sbuf_tensor(name, shape, dt))

        def sem(name):
            return ctx.enter_context(nc.semaphore(name))

        by_engine = {"pe": [], "act": [], "dve": [], "pool": [], "sp": []}

        def step(name, n=1):
            s = Step(sem(name), n)
            by_engine[name.split("_")[0]].append(s)
            return s

        PS = ctx.enter_context(nc.psum_tensor("PS", [P, 8, 512], F32))

        x = sb("x", [P, NT, D])
        ident = sb("ident", [P, P])
        ones = sb("ones", [P, P])
        hmask = sb("hmask", [P, HM])
        cosT = sb("cosT", [P, R])
        sinT = sb("sinT", [P, R])
        causal = sb("causal", [P, S])
        rel = sb("rel", [P, S])
        slopes = sb("slopes", [P, H])
        eidx = sb("eidx", [P, E])
        bqk0 = sb("bqk0", [P, 2, KC])
        rows = sb("rows", [P, D])
        w_hi, w_lo = (sb(n, [P, H * XD], F32R) for n in ("w_hi", "w_lo"))
        c_hi, c_lo = (sb(n, [P, C], F32R) for n in ("c_hi", "c_lo"))
        q_hi, q_lo = (sb(n, [P, 2, W], F32R) for n in ("q_hi", "q_lo"))
        b_hi, b_lo = (w[0:1, 2 * D:3 * D] for w in (w_hi, w_lo))
        ones_r = w_hi[0:1, 3 * D:3 * D + P]
        keyT = sb("keyT", [P, 3, KC, CR])
        bk_x1 = sb("bk_x1", [P, D])
        lncol = sb("lncol", [P, 6])
        bvcol = sb("bvcol", [P, KC])
        gqk = sb("gqk", [P, 2])
        vo = sb("vo", [P, H, D])

        lnst = sb("lnst", [P, G, 6])
        lnmv = sb("lnmv", [P, G, 2])
        lnve = sb("lnve", [P, G])
        lnrs = sb("lnrs", [P, G])
        xn = sb("xn", [P, G, D])
        xT = sb("xT", [P, G, KC, R])
        nhalf = sb("nhalf", [P, 64])

        QREG = B * H * S
        SREG = CT * H * S
        MREG = 4 * H * S + KC * D
        CREG = 1024 + C + CT * CD
        big = sb("big", [P, QREG + SREG + MREG + CREG])
        used = {}

        def region(start, size):
            used[start] = 0

            def take(*shape):
                n = int(np.prod(shape))
                at = start + used[start]
                used[start] += n
                assert used[start] <= size, (start, used[start], size)
                v = big[:, at:at + n]
                names = "abcde"[:len(shape)]
                if len(shape) > 1:
                    v = v.rearrange(f"p ({' '.join(names)}) -> p {' '.join(names)}",
                                    **{names[i]: shape[i] for i in range(1, len(shape))})
                return v
            return take

        Q0, S0, M0, C0 = 0, QREG, QREG + SREG, QREG + SREG + MREG

        def attention_buffers(first, second, third, T):
            return Buffers(T, first(G, H, P), second(G, 2, H, HD + 1), second(G, 2, KC, HM * T), second(G, KC, S + SL),
                           second(G, H * T), third(G, H), third(G, H), third(G, D), third(G, KC, R))

        take = region(Q0, QREG)
        SA = attention_buffers(take, take, take, S)
        rope = take(3, KC, R)
        abias = take(H, S)
        take = region(C0, CREG)
        wq0, wk0, wv0, wo0 = (take(KC, D) for _ in range(4))
        bv0 = take(D)
        take = region(Q0, QREG)
        th = take(G, FA)
        hm = take(G, FA)
        hT = take(G, FA // P, R)
        lg = take(G, H + 1)
        le = take(G, H)
        lm = take(G, 1)
        top = take(G, 8)
        topi = sb("topi", [P, G, 8], U32)
        topf = take(G, 8)
        tw = take(G, 4)
        hot = take(G, 2, E)
        comb = take(G, EW)
        take = region(S0, SREG)
        factors = take(KC * D, 8)
        take = region(S0, SREG)
        w13 = take(KC, 2, FA)
        w2 = take(FA // P, D)
        wr = take(KC, E + 1)
        take = region(S0, SREG)
        wq_x1 = take(KC, D)
        wkv_d = take(2 * D)
        wvT_x1 = take(H, CD)
        woh_x1 = take(H, D)
        wo_x1 = take(KC, D)
        ydT = take(B * NDCA)
        kTd = take(KC, B * NDCA)
        bq_x1 = take(D)
        bkv_d = take(2 * D)
        qs = take(G, D)
        sq1a = take(G, D)
        mean = take(2 * D // HD)
        wk_x1 = take(D)
        take_c = region(C0, CREG)
        kd = take_c(2, D)
        yds = take_c(G, 2 * NDCA)
        ss1a = take_c(G, H)
        rs1a = take_c(G, H)
        take = region(M0, MREG)
        DCA = attention_buffers(region(S0 + KC * D + 2 * D + H * CD, H * D), take, take_c, NDCA)

        take = region(S0, SREG)
        wq_x0 = take(KC, H * XD)
        wkT_x0 = take(H, CD)
        wvT_x0 = take(H, CD)
        take = region(M0, MREG)
        wo_x0 = take(H, D)
        qn_a = region(S0 + KC * H * XD + 2 * H * CD, H * XD)(H, XD)
        take = region(C0, CREG)
        sq_a = take(H * XD)
        qhT = take(H, R)
        ss_a = take(G, H)
        rq_a = take(G, H)
        wk_x0 = vo[:, 0:H // 2, :].rearrange("p h d -> p (h d)")
        take = region(Q0, QREG)
        Qall = take(B, 2, W)
        take = region(S0, SREG)
        Sall = take(CT, 2 * W)
        take = region(M0, MREG)
        Mx = take(2 * W)
        Mb = take(2 * W)
        Zs = take(2 * W)
        rz = take(2 * W)
        take = region(M0 + 4 * H * S, KC * D)
        fmix = take(KC, D)
        take = region(C0, CREG)
        sqr = take(2, 512)
        squared = sqr.rearrange("p a n -> p (a n)")[:, 3 * D:4 * D]

        def centred(t):
            return sqr.rearrange("p a n -> p (a n)")[:, (t % 3) * D:(t % 3 + 1) * D]

        cxT = take(C)
        cxn = take(CT, CD)
        scrap = sb("scrap", [P, XD])
        ssr = sb("ssr", [P, 2, H])
        vek = sb("vek", [P, 2, H])
        rkr = sb("rkr", [P, 6, H])
        mcol = sb("mcol", [P, 8])
        zcol = sb("zcol", [P, 8])
        mdiag = sb("mdiag", [P, 7, P])
        take = region(M0, MREG)
        OTs = take(G, H, R)
        flat = vo[:, :, :].rearrange("p h d -> p (h d)")
        wq1 = flat[:, 0:2 * KC * D].rearrange("p (k n) -> p k n", k=KC)
        wk1 = flat[:, 2 * KC * D:3 * KC * D].rearrange("p (k n) -> p k n", k=KC)
        wv1 = flat[:, 3 * KC * D:3 * KC * D + KC * P].rearrange("p (k n) -> p k n", k=KC)
        wo1 = flat[:, 3 * KC * D + KC * P:4 * KC * D + KC * P].rearrange("p (k n) -> p k n", k=KC)
        sp_x = sem("sp_x")
        sp_w0 = sem("sp_w0")
        sp_wx0 = sem("sp_wx0")
        sp_fac = sem("sp_fac")
        sp_w1 = sem("sp_w1")
        sp_out = sem("sp_out")
        pool_init = sem("pool_init")
        pe_beat, dve_beat, pool_beat = sem("pe_beat"), sem("dve_beat"), sem("pool_beat")
        dve_setup = sem("dve_setup")
        dve_x = step("dve_x")
        dve_stats, dve_aggr, dve_xn = step("dve_stats"), step("dve_aggr"), step("dve_xn")
        pool_ve, pool_rs = step("pool_ve"), step("pool_rs")
        pe_xT, act_xT = step("pe_xT"), step("act_xT")
        pe_y = step("pe_y")
        pe_q, pe_k, pe_v = step("pe_q"), step("pe_k"), step("pe_v")
        act_q = step("act_q", KC)
        dve_km0, dve_km1 = step("dve_km0", 4), step("dve_km1", 2)
        dve_va = step("dve_va")
        dve_rope, dve_qk1 = step("dve_rope", 4), step("dve_qk1", 2)
        pe_s, dve_mx, dve_z = step("pe_s"), step("dve_mx"), step("dve_z")
        act_tanh, act_e, dve_p = step("act_tanh"), step("act_e"), step("dve_p")
        pe_pT, act_pT, dve_pT = step("pe_pT"), step("act_pT"), step("dve_pT")
        pe_o, dve_rc, dve_cx = step("pe_o"), step("dve_rc"), step("dve_cx")
        pe_cT, act_cT = step("pe_cT"), step("act_cT")
        pe_qx, act_sqa, dve_ssa = step("pe_qx"), step("act_sqa"), step("dve_ssa")
        pool_vea, pool_rqa = step("pool_vea"), step("pool_rqa")
        dve_qh = step("dve_qh")
        pe_qhT, act_qhT, pe_qt, dve_qt = step("pe_qhT"), step("act_qhT"), step("pe_qt"), step("dve_qt")
        pe_vo, act_vo = step("pe_vo"), step("act_vo")
        sp_cxT = [step(f"sp_cxT{c}", 16) for c in range(CT // CHUNK)]
        sp_cxn = [step(f"sp_cxn{c}", 16) for c in range(CT // CHUNK)]
        act_whi, dve_wlo = sem("act_whi"), sem("dve_wlo")
        act_chi, dve_clo, act_qhi, dve_qlo = step("act_chi"), step("dve_clo"), step("act_qhi"), step("dve_qlo")
        pe_kp, act_sq, dve_ss = step("pe_kp"), step("act_sq"), step("dve_ss")
        pool_vek, pool_rk = step("pool_vek"), step("pool_rk")
        pe_sx, dve_t, dve_mxr = step("pe_sx"), step("dve_t"), step("dve_mxr")
        pool_d, dve_d, act_p, dve_sum, pe_pv = (
            step("pool_d"), step("dve_d"), step("act_p"), step("dve_sum"), step("pe_pv"))
        pe_mT, dve_mcol, dve_diag, pe_mb, act_mb = (
            step("pe_mT"), step("dve_mcol", 2), step("dve_diag", 2), step("pe_mb", 2), step("act_mb", 2))
        pe_zc, dve_zcol, dve_zdiag, pe_zb, act_rz, act_un, dve_ot = (
            step("pe_zc"), step("dve_zcol"), step("dve_zdiag", 2), step("pe_zb", 2), step("act_rz"), step("act_un"), step("dve_ot"))
        act_ots, pool_ots = step("act_ots"), step("pool_ots")
        sp_wx1, pe_kd, dve_kd, act_kd, pool_kd, pe_kdT = (
            sem("sp_wx1"), sem("pe_kd"), sem("dve_kd"), sem("act_kd"), sem("pool_kd"), sem("pe_kdT"))
        pe_q1, dve_qs, act_q1s, dve_q1ss = step("pe_q1"), step("dve_qs"), step("act_q1s"), step("dve_q1ss")
        pool_q1v, pool_q1r, dve_q1n, pe_q1T = step("pool_q1v"), step("pool_q1r"), step("dve_q1n"), step("pe_q1T")
        act_q1, dve_q1m, dve_kmd, pool_yd = step("act_q1"), step("dve_q1m", 4), step("dve_kmd", 4), step("pool_yd")
        pe_k1, act_k1c, act_k1s, dve_k1ss = step("pe_k1"), step("act_k1c"), step("act_k1s"), step("dve_k1ss")
        pool_k1v, pool_k1r, dve_k1n, pe_k1T, act_k1T = (
            step("pool_k1v"), step("pool_k1r"), step("dve_k1n"), step("pe_k1T"), step("act_k1T"))
        act_scrap = step("act_scrap")
        act_t = step("act_t")
        sp_moe = sem("sp_moe")
        pe_lg, dve_lg, dve_lm, dve_le, act_le = step("pe_lg"), step("dve_lg"), step("dve_lm"), step("dve_le"), step("act_le", 2)
        dve_top, dve_topi, dve_topf, dve_tw, dve_hot, dve_comb = (
            step("dve_top"), step("dve_topi"), step("dve_topf"), step("dve_tw", 3), step("dve_hot", 2), step("dve_comb", 2))
        pe_h, act_th, dve_h, pe_hT, act_hT, dve_hT = (
            step("pe_h"), step("act_th"), step("dve_h", 3), step("pe_hT"), step("act_hT"), step("dve_hT"))

        block = ctx.enter_context(nc.Block())

        @block.sync
        def _(sp):
            for s in by_engine["sp"]:
                s.credit(sp)
            sp.dma_start(x[0:R, :, :], a["x"].rearrange("(j r) c -> r j c", r=R)).then_inc(sp_x, 16)
            for dst, name in ((ident, "ident"), (wq0, "wq0"), (wk0, "wk0"), (wv0, "wv0"), (bqk0, "bqk0")):
                sp.dma_start(dst[:], a[name]).then_inc(sp_w0, 16)
            sp.dma_start(bv0[:, :], a["bv0"].partition_broadcast(P)).then_inc(sp_w0, 16)
            for dst, name in ((hmask, "hmask"), (causal, "causal"), (rel, "rel"), (wo0, "wo0"), (cosT, "cosT"), (sinT, "sinT"), (eidx, "eidx")):
                sp.dma_start(dst[:], a[name]).then_inc(sp_w0, 16)
            sp.dma_start(rows[0:P:32, :], a["rows"]).then_inc(sp_w0, 16)
            sp.dma_start(slopes[:, :], a["slopes"].partition_broadcast(P)).then_inc(sp_w0, 16)
            for dst, name in ((wq_x0, "wq_x0"), (wkT_x0, "wkT_x0"), (wvT_x0, "wvT_x0"), (wo_x0, "wo_x0"),
                              (wk_x0, "wk_x0"), (gqk, "gqk"), (lncol, "lncol"), (bvcol, "bvcol")):
                sp.dma_start(dst[:], a[name]).then_inc(sp_wx0, 16)

            def context(X):
                def part(b, c):
                    span = slice(c * CHUNK * CR, (c + 1) * CHUNK * CR)
                    sp.dma_start(cxT[:, span], a["ctxT"][b, :, span]).then_inc(sp_cxT[c].sem, 16)

                def part_rows(b, c):
                    span = slice(c * CHUNK * CR, (c + 1) * CHUNK * CR)
                    sp.dma_start(cxn[0:CR, c * CHUNK:(c + 1) * CHUNK, :],
                                 a["ctx"][b, span, :].rearrange("(t r) c -> r t c", r=CR)).then_inc(sp_cxn[c].sem, 16)

                def parts(b):
                    for c in range(CT // CHUNK):
                        wait(sp, act_chi, (X * B + b - 1) * (CT // CHUNK) + c)
                        wait(sp, dve_clo, (X * B + b - 1) * (CT // CHUNK) + c)
                        part(b, c)

                def parts_rows(b):
                    for c in range(CT // CHUNK):
                        wait(sp, pe_pv, (X * B + b - 1) * CT + CHUNK * c + CHUNK - 1)
                        part_rows(b, c)

                for c in range(CT // CHUNK):
                    part(0, c)
                for c in range(CT // CHUNK):
                    part_rows(0, c)
                parts(1)
                with sp.Fori(1, B - 1) as b:
                    parts(b + 1)
                    parts_rows(b)
                parts_rows(B - 1)

            wait(sp, pe_qt, 4 * NT - 1)
            context(0)
            wait(sp, dve_ot, B - 1)
            sp.dma_start(factors, a["factors"]).then_inc(sp_fac, 16)
            wait(sp, pe_y, 2 * NT - 1)
            for dst, name in ((wq1, "wq1"), (wk1, "wk1"), (wv1, "wv1"), (wo1, "wo1")):
                sp.dma_start(dst, a[name]).then_inc(sp_w1, 16)
            sp.wait_ge(dve_setup, 4)
            for dst, name in ((wq_x1, "wq_x1"), (wkv_d, "wkv_d"), (wo_x1, "wo_x1"), (ydT, "ydT"),
                              (wk_x1, "wk_x1")):
                sp.dma_start(dst, a[name]).then_inc(sp_wx1, 16)
            sp.dma_start(wvT_x1[0:HD], a["wvT_x1"]).then_inc(sp_wx1, 16)
            sp.dma_start(woh_x1[0:HD], a["woh_x1"]).then_inc(sp_wx1, 16)
            for dst, name in ((bq_x1, "bq_x1"), (bkv_d, "bkv_d"), (bk_x1, "bk_x1")):
                sp.dma_start(dst[:, :], a[name].partition_broadcast(P)).then_inc(sp_wx1, 16)
            wait(sp, dve_x, 5 * NT - 1)
            context(1)
            wait(sp, dve_ot, 2 * B - 1)
            for dst, name in ((w13, "w13"), (w2, "w2"), (wr, "wr")):
                sp.dma_start(dst, a[name]).then_inc(sp_moe, 16)

            wait(sp, dve_x, 7 * NT - 1)
            sp.dma_start(out.rearrange("(j r) c -> r j c", r=R), x[0:R, :, :]).then_inc(sp_out, 16)
            sp.wait_ge(sp_out, 16)

        @block.tensor
        def _(pe):
            for s in by_engine["pe"]:
                s.credit(pe)

            def norm_T(js, L):
                for g, j in enumerate(js):
                    wait(pe, dve_xn, L + j)
                    wait(pe, act_xT, L + j - 1)
                    for k in range(KC):
                        ins = pe.transpose(PS[:, 0, k * R:(k + 1) * R], xn[0:R, g, k * P:(k + 1) * P],
                                           ident[0:R, 0:R])
                    ins.then_inc(pe_xT.sem, 1)

            def attention(js, U, V, J, ready, wout, row, values, between):
                T = V.T
                for g, j in enumerate(js):
                    for s, n in ready:
                        wait(pe, s, n + j)
                    wait(pe, dve_z, U + j - 1)
                    for b in range(2):
                        for m in range(KC):
                            ins = pe.matmul(PS[SL * b:SL * b + SL, 3 + m, 0:HM * T], V.qT[:, g, m, S * b:S * b + SL],
                                            V.Km[:, g, b, 0 if U == NT else m],
                                            start=True, stop=True)
                    ins.then_inc(pe_s.sem, 1)
                values()
                for g, j in enumerate(js):
                    if U == 0:
                        wait(pe, dve_p, j)
                    else:
                        wait(pe, act_e, U + j)
                    for n in range(4):
                        wait(pe, (act_pT, dve_pT)[n % 2], (U + j) * 2 + n // 2 - 2)
                        pe.sem_inc(pe_beat, 1)
                        for h in range(4):
                            s0 = (4 * n + h) * T
                            ins = pe.transpose(PS[0:T, PT_BANKS[n], h * P:(h + 1) * P], V.Z[:, g, s0:s0 + T],
                                               ident[:, :])
                        ins.then_inc(pe_pT.sem, 1)
                for g, j in enumerate(js):
                    wait(pe, act_pT, (U + j) * 2 + 1)
                    wait(pe, dve_pT, (U + j) * 2 + 1)
                    wait(pe, dve_va, U + js[-1])
                    wait(pe, dve_cx, U + j - 1)
                    pe.sem_inc(pe_beat, 1)
                    for b in range(2):
                        for h in range(H):
                            vh = h % HM if U == NT else h
                            ins = pe.matmul(PS[SL * b:SL * b + SL, 7, h * (HD + 1):(h + 1) * (HD + 1)],
                                            V.PT[0:T, g, h, SL * b:SL * b + SL], V.va[0:T, g, b, vh, :],
                                            start=True, stop=True, skip_group_check=True)
                    ins.then_inc(pe_o.sem, 1)
                between()
                for g, j in enumerate(js):
                    wait(pe, dve_cx, U + j)
                    wait(pe, act_cT, U + j - G)
                    for k in range(KC):
                        ins = pe.transpose(PS[:, CT_BANKS[g], k * P:(k + 1) * P], V.cx[:, g, k * P:(k + 1) * P], ident[:, :])
                    ins.then_inc(pe_cT.sem, 1)
                for g, j in enumerate(js):
                    wait(pe, act_cT, U + j)
                    project(j, J, [V.cT[:, g, k] for k in range(KC)], [wout[:, k, :] for k in range(KC)], row,
                            bank=Y_BANKS[g], banks=2)

            def project(j, J, left, right, row, bank=2, banks=1):
                wait(pe, dve_x, J + j - banks)
                for n, (le, ri) in enumerate(zip(left, right)):
                    ins = pe.matmul(PS[0:R, bank, 0:D], le, ri, start=(n == 0), stop=(row is None and n == len(left) - 1))
                if row is not None:
                    at = slice(32 * row, 32 * row + 1)
                    ins = pe.matmul(PS[0:R, bank, 0:D], ones[at, 0:R], rows[at, :], start=False, stop=True)
                ins.then_inc(pe_y.sem, 1)

            pe.wait_ge(sp_w0, 15 * 16)
            pe.wait_ge(pool_init, 4)

            def tiles(i, more):
                js = [i * G + g for g in range(G)]

                def between():
                    if more:
                        norm_T([j + G for j in js], 0)
                        wait(pe, act_xT, js[-1] + G)

                def values():
                    for g, j in enumerate(js):
                        wait(pe, dve_va, j - G)
                        wait(pe, dve_x, i * G - 1)
                        for b in range(2):
                            for k in range(KC):
                                ins = pe.matmul(PS[0:S, V_BANKS[g], b * D:(b + 1) * D], xT[:, g, k, b * S:(b + 1) * S], wv0[:, k, :],
                                                start=(k == 0), stop=(k == KC - 1))
                        ins.then_inc(pe_v.sem, 1)

                for g, j in enumerate(js):
                    wait(pe, act_xT, j)
                    wait(pe, act_q, j - G)
                    for m in range(KC):
                        for k in range(KC):
                            ins = pe.matmul(PS[:, Q_BANKS[g], m * R:(m + 1) * R], wq0[:, k, m * P:(m + 1) * P],
                                            xT[:, g, k], start=(k == 0), stop=(k == KC - 1))
                    ins.then_inc(pe_q.sem, 1)
                    wait(pe, dve_km0, j - G)
                    wait(pe, dve_cx, i * G - 1)
                    wait(pe, dve_x, i * G - 1)
                    for m in range(KC):
                        for k in range(KC):
                            ins = pe.matmul(PS[:, K_BANKS[g], m * R:(m + 1) * R], wk0[:, k, m * P:(m + 1) * P],
                                            xT[:, g, k], start=(k == 0), stop=(k == KC - 1))
                    ins.then_inc(pe_k.sem, 1)
                attention(js, 0, SA, 0, [(act_q, 0), (dve_km0, 0)], wo0, 0, values, between)

            norm_T(range(G), 0)
            with pe.Fori(0, NT // G - 1) as i:
                tiles(i, True)
            tiles(NT // G - 1, False)

            def value_output(pairs, wvT, wo, V):
                for n in range(H // 2):
                    wait(pe, act_vo, V + n - 2)
                    for h in range(2):
                        ins = pe.matmul(PS[:, 6 + n % 2, h * D:(h + 1) * D], wvT[0:pairs, 2 * n + h, :], wo[0:pairs, 2 * n + h, :],
                                        start=True, stop=True, skip_group_check=True)
                    ins.then_inc(pe_vo.sem, 1)

            def three_passes(out, left, right, more=False):
                (l_hi, l_lo), (r_hi, r_lo) = left, right
                pe.matmul(out, l_hi, r_hi, start=True, stop=False)
                pe.matmul(out, l_hi, r_lo, start=False, stop=False)
                return pe.matmul(out, l_lo, r_hi, start=False, stop=not more)

            def context_part(X, b, t):
                if t % CHUNK == 0:
                    wait(pe, act_chi, (X * B + b) * (CT // CHUNK) + t // CHUNK)
                    wait(pe, dve_clo, (X * B + b) * (CT // CHUNK) + t // CHUNK)

            def tile_of(t, n_rows):
                return [c[:, t * CR:t * CR + n_rows] for c in (c_hi, c_lo)]

            def keys(b, t, half):
                K = b * CT + t
                context_part(0, b, t)
                for n in (0, 1) if half == 0 else (2, 3):
                    wait(pe, act_sq, K * 4 + n - 2)
                    three_passes(PS[0:CR, n % 2, :], tile_of(t, CR), [w[:, n * 512:(n + 1) * 512] for w in (w_hi, w_lo)])\
                        .then_inc(pe_kp.sem, 1)

            def scores(b, t):
                K = b * CT + t
                if t == 0:
                    wait(pe, act_qhi, b)
                    wait(pe, dve_qlo, b)
                wait(pe, dve_t, K - 1)
                for m in range(2):
                    ins = three_passes(PS[0:CR, 2 + m, 0:W], tile_of(t, CR), (q_hi[:, m, :], q_lo[:, m, :]))
                ins.then_inc(pe_sx.sem, 1)

            def keys_1(b, t):
                k = b * CT + t
                context_part(1, b, t)
                wait(pe, act_k1s, k - 1)
                n_rows = rows_in(1, t)
                three_passes(PS[0:n_rows, 0, 0:D], tile_of(t, n_rows), (w_hi[:, 0:D], w_lo[:, 0:D]), more=True)
                pe.matmul(PS[0:n_rows, 0, 0:D], ones_r[:, 0:n_rows], b_hi, start=False, stop=False)
                pe.matmul(PS[0:n_rows, 0, 0:D], ones_r[:, 0:n_rows], b_lo, start=False, stop=True).then_inc(pe_k1.sem, 1)

            def keys_1T(b, t):
                n_rows = rows_in(1, t)
                wait(pe, dve_k1n, b * CT + t)
                wait(pe, act_k1T, b * CT + t - 1)
                for m in range(KC):
                    ins = pe.transpose(PS[:, 1, m * CR:m * CR + n_rows],
                                       centred(t)[0:n_rows, m * P:(m + 1) * P], ident[0:n_rows, 0:n_rows])
                ins.then_inc(pe_k1T.sem, 1)

            def scores_1(b, t):
                n_rows = rows_in(1, t)
                wait(pe, act_k1T, b * CT + t)
                wait(pe, act_t, b * CT + t - 1)
                for m in range(2):
                    ins = pe.matmul(PS[0:n_rows, 2 + m, 0:W], keyT[:, t % 3, m, 0:n_rows], Qall[:, b, m, :],
                                    start=True, stop=True)
                ins.then_inc(pe_sx.sem, 1)

            def weighted_context(X, b, t):
                K = (X * B + b) * CT + t
                n_rows = rows_in(X, t)
                if t % CHUNK == 0:
                    wait(pe, sp_cxn[t // CHUNK], X * B + b)
                if t == 0:
                    wait(pe, act_un, X * B + b - 1)
                wait(pe, act_p, K)
                for m in range(2):
                    ins = pe.matmul(PS[:, 4 + m, 0:W], cxn[0:n_rows, t, :], Sall[0:n_rows, t, m * W:(m + 1) * W],
                                    start=(t == 0), stop=(t == CT - 1))
                ins.then_inc(pe_pv.sem, 1)

            def maxima_T(u):
                wait(pe, dve_mxr, u * CT + CT - 1)
                for q in range(7):
                    ins = pe.transpose(PS[:, 6 + q // 4, (q % 4) * CR:(q % 4 + 1) * CR], Mx[0:CR, q * P:(q + 1) * P],
                                       ident[0:CR, 0:CR])
                ins.then_inc(pe_mT.sem, 1)

            def to_all_partitions(ready, u, done):
                for m in range(2):
                    pe.wait_ge(ready.sem, ready.done(u) - 1 + m)
                    pe.matmul(PS[:, 6 + m, 0:W], ones[:, :],
                              mdiag[:, :, :].rearrange("p a q -> p (a q)")[:, m * W:(m + 1) * W], start=True, stop=True)\
                        .then_inc(done.sem, 1)

            def sum_columns(u):
                wait(pe, dve_sum, u * CT + CT - 1)
                for q in range(7):
                    ins = pe.matmul(PS[:, 7, 4 * CR + q:4 * CR + q + 1], Zs[0:CR, q * P:(q + 1) * P], ones[0:CR, 0:1],
                                    start=True, stop=True, skip_group_check=True)
                ins.then_inc(pe_zc.sem, 1)

            def cross_attention(X):
                def iteration(b, stage, before, sums):
                    u0 = X * B + b
                    for u in range(CT + LAG):
                        if stage and u < CT:
                            if X == 0:
                                keys(b, u, 0)
                            else:
                                keys_1(b, u)
                        if before and PV <= u < CT + PV:
                            weighted_context(X, b - 1, u - PV)
                        if stage and X == 1 and 2 <= u < CT + 2:
                            keys_1T(b, u - 2)
                        if u == 0 and (before or sums):
                            wait(pe, act_rz, u0 - 3)
                        if u == 0 and sums:
                            sum_columns(u0 - 2)
                        if u == 0 and before:
                            maxima_T(u0 - 1)
                        if u == 1 and before:
                            to_all_partitions(dve_diag, u0 - 1, pe_mb)
                        if stage and X == 0 and u < CT:
                            keys(b, u, 1)
                        if u >= LAG and stage:
                            (scores, scores_1)[X](b, u - LAG)
                        if u == LAG + 2 and sums:
                            if before:
                                wait(pe, act_mb, u0 - 1)
                            to_all_partitions(dve_zdiag, u0 - 2, pe_zb)

                iteration(0, True, False, False)
                iteration(1, True, True, False)
                with pe.Fori(2, B) as b:
                    iteration(b, True, True, True)
                iteration(B, False, True, True)
                iteration(B + 1, False, False, True)

            def output_rows(X, J, row):
                with pe.Fori(0, NT // G) as i:
                    for g in range(G):
                        j = i * G + g
                        wait(pe, act_ots, X * NT + j)
                        wait(pe, pool_ots, X * NT + j)
                        project(j, J, [OTs[:, g, h, :] for h in range(H)], [vo[:, h, :] for h in range(H)], row,
                                bank=2 + g, banks=2)

            pe.wait_ge(sp_wx0, 8 * 16)
            wait(pe, dve_x, NT - 1)
            value_output(P, wvT_x0, wo_x0, 0)
            pe.wait_ge(dve_setup, 2)

            def tiles(i, more):
                js = [i * G + g for g in range(G)]

                def between():
                    if more:
                        norm_T([j + G for j in js], NT)

                for u in range(4 * G + 3):
                    if u < 4 * G:
                        g, n, k4 = u // 4, u % 4, 4 * js[0] + u
                        if n == 0:
                            wait(pe, act_xT, NT + js[g])
                        wait(pe, dve_qh, k4 - 4)
                        for k in range(KC):
                            ins = pe.matmul(PS[0:R, 1 + n, :], xT[:, g, k], wq_x0[:, k, n * 512:(n + 1) * 512],
                                            start=(k == 0), stop=(k == KC - 1))
                        ins.then_inc(pe_qx.sem, 1)
                    if u == 4 * G:
                        between()
                    if 2 <= u < 4 * G + 2:
                        n, k4 = (u - 2) % 4, 4 * js[0] + u - 2
                        wait(pe, dve_qh, k4)
                        wait(pe, act_qhT, k4 - 2)
                        for h in range(4):
                            ins = pe.transpose(PS[:, 5 + n % 2, h * R:(h + 1) * R], qn_a[0:R, 4 * n + h, :],
                                               ident[0:R, 0:R])
                        ins.then_inc(pe_qhT.sem, 1)
                    if u >= 3:
                        n, k4 = (u - 3) % 4, 4 * js[0] + u - 3
                        wait(pe, act_qhT, k4)
                        wait(pe, dve_qt, k4 - 1)
                        for h in range(4 * n, 4 * n + 4):
                            ins = pe.matmul(PS[:, 7, (h % 4) * R:(h % 4 + 1) * R], wkT_x0[:, h, :], qhT[:, h, :],
                                            start=True, stop=True, skip_group_check=True)
                        ins.then_inc(pe_qt.sem, 1)

            norm_T(range(G), NT)
            with pe.Fori(0, NT // G - 1) as i:
                tiles(i, True)
            tiles(NT // G - 1, False)
            wait(pe, dve_qt, 4 * NT - 1)
            pe.wait_ge(dve_wlo, 1)
            cross_attention(0)
            output_rows(0, NT, None)

            pe.wait_ge(dve_setup, 4)

            def tiles(i, more):
                js = [i * G + g for g in range(G)]

                def between():
                    if more:
                        norm_T([j + G for j in js], 2 * NT)

                for g, j in enumerate(js):
                    wait(pe, act_xT, 2 * NT + j)
                    project(j, 2 * NT, [xT[:, g, k] for k in range(KC)], [fmix[:, k, :] for k in range(KC)], 1,
                            bank=2 + g, banks=2)
                between()

            norm_T(range(G), 2 * NT)
            with pe.Fori(0, NT // G - 1) as i:
                tiles(i, True)
            tiles(NT // G - 1, False)

            pe.wait_ge(sp_w1, 4 * 16)
            pe.wait_ge(pool_init, 6)
            wait(pe, dve_x, 3 * NT - 1)

            def tiles(i, more):
                js = [i * G + g for g in range(G)]

                def between():
                    if more:
                        norm_T([j + G for j in js], 3 * NT)
                        wait(pe, act_xT, 3 * NT + js[-1] + G)

                def values():
                    for g, j in enumerate(js):
                        wait(pe, dve_va, NT + j - G)
                        wait(pe, dve_x, 3 * NT + i * G - 1)
                        for b in range(2):
                            for k in range(KC):
                                ins = pe.matmul(PS[0:S, V_BANKS[g], b * P:(b + 1) * P], xT[:, g, k, b * S:(b + 1) * S], wv1[:, k, :],
                                                start=(k == 0), stop=(k == KC - 1))
                        ins.then_inc(pe_v.sem, 1)

                for g, j in enumerate(js):
                    wait(pe, act_xT, 3 * NT + j)
                    wait(pe, dve_rope, j - G)
                    for m in range(2 * KC):
                        for k in range(KC):
                            ins = pe.matmul(PS[:, Q_BANKS[g], m * R:(m + 1) * R], wq1[:, k, m * P:(m + 1) * P], xT[:, g, k],
                                            start=(k == 0), stop=(k == KC - 1))
                    ins.then_inc(pe_q.sem, 1)
                    wait(pe, dve_cx, NT + i * G - 1)
                    wait(pe, dve_x, 3 * NT + i * G - 1)
                    for m in range(KC):
                        for k in range(KC):
                            ins = pe.matmul(PS[:, K_BANKS[g], m * R:(m + 1) * R], wk1[:, k, m * P:(m + 1) * P], xT[:, g, k],
                                            start=(k == 0), stop=(k == KC - 1))
                    ins.then_inc(pe_k.sem, 1)
                attention(js, NT, SA, 3 * NT, [(dve_km1, 0)], wo1, None, values, between)

            norm_T(range(G), 3 * NT)
            with pe.Fori(0, NT // G - 1) as i:
                tiles(i, True)
            tiles(NT // G - 1, False)

            pe.wait_ge(sp_wx1, 10 * 16)
            wait(pe, dve_x, 4 * NT - 1)
            value_output(HD, wvT_x1, woh_x1, H // 2)
            pe.wait_ge(dve_setup, 13)
            for n in range(2):
                if n:
                    pe.wait_ge(dve_kd, 3 * n - 2)
                pe.matmul(PS[:, 1, 0:D], ydT[:, n * P:(n + 1) * P], wkv_d[:, 0:D], start=True, stop=True)\
                    .then_inc(pe_kd, 1)
            for n in range(2):
                pe.wait_ge(dve_kd, 2 + 2 + n + 1)
                if n:
                    pe.wait_ge(act_kd, 2 + n)
                for m in range(KC):
                    ins = pe.transpose(PS[:, 5, m * P:(m + 1) * P], kd[:, n, m * P:(m + 1) * P], ident[:, :])
                ins.then_inc(pe_kdT, 1)
            pe.wait_ge(act_kd, 4)

            def tiles(i, more):
                js = [i * G + g for g in range(G)]

                def between():
                    if more:
                        norm_T([j + G for j in js], 4 * NT)
                        wait(pe, act_xT, 4 * NT + js[-1] + G)

                def values():
                    for g, j in enumerate(js):
                        wait(pe, pool_yd, j)
                        wait(pe, dve_va, 2 * NT + j - G)
                        wait(pe, dve_x, 4 * NT + i * G - 1)
                        for b in range(2):
                            ins = pe.matmul(PS[0:NDCA, V_BANKS[g], b * D:(b + 1) * D], yds[:, g, b * NDCA:(b + 1) * NDCA],
                                            wkv_d[:, D:2 * D], start=True, stop=True)
                        ins.then_inc(pe_v.sem, 1)

                for g, j in enumerate(js):
                    wait(pe, act_xT, 4 * NT + j)
                    wait(pe, dve_qs, j - 1)
                    for k in range(KC):
                        ins = pe.matmul(PS[0:R, 1, 0:D], xT[:, g, k], wq_x1[:, k, :], start=(k == 0), stop=(k == KC - 1))
                    ins.then_inc(pe_q1.sem, 1)
                for g, j in enumerate(js):
                    wait(pe, dve_q1n, j)
                    wait(pe, act_q1, j - 1)
                    wait(pe, act_pT, 4 * NT + 2 * i * G - 1)
                    for k in range(KC):
                        ins = pe.transpose(PS[:, 5, k * R:(k + 1) * R], qs[0:R, g, k * P:(k + 1) * P], ident[0:R, 0:R])
                    ins.then_inc(pe_q1T.sem, 1)
                attention(js, 2 * NT, DCA, 4 * NT, [(act_q1, 0), (dve_kmd, 0)], wo_x1, 2, values, between)

            norm_T(range(G), 4 * NT)
            with pe.Fori(0, NT // G - 1) as i:
                tiles(i, True)
            tiles(NT // G - 1, False)
            wait(pe, dve_q1m, NT - 1)
            pe.wait_ge(dve_wlo, 3)
            wait(pe, dve_x, 5 * NT - 1)
            cross_attention(1)
            output_rows(1, 5 * NT, None)

            pe.wait_ge(sp_moe, 3 * 16)
            wait(pe, dve_x, 6 * NT - 1)

            def tiles(i, more):
                js = [i * G + g for g in range(G)]

                def between():
                    if more:
                        norm_T([j + G for j in js], 5 * NT)

                for g, j in enumerate(js):
                    wait(pe, act_xT, 5 * NT + j)
                    wait(pe, dve_lg, j - 1)
                    wait(pe, dve_hT, i * G - 1)
                    for k in range(KC):
                        ins = pe.matmul(PS[0:R, 7, 0:E + 1], xT[:, g, k], wr[:, k, :], start=(k == 0), stop=(k == KC - 1))
                    ins.then_inc(pe_lg.sem, 1)
                for g, j in enumerate(js):
                    wait(pe, dve_x, 6 * NT + i * G - 1)
                    for w, c, n in ((0, 0, 512), (0, 512, 512), (0, 1024, 256), (1, 0, 256), (1, 256, 512), (1, 768, 512)):
                        if (w, c) == (0, 0):
                            pe.wait_ge(dve_h.sem, dve_h.done(j - 1) - 2)
                        elif (w, c) == (0, 1024):
                            pe.wait_ge(dve_h.sem, dve_h.done(j - 1) - 1)
                        at = w * FA + c
                        for k in range(KC):
                            ins = pe.matmul(PS[0:R, 1 + at // 512, at % 512:at % 512 + n], xT[:, g, k],
                                            w13[:, k, w, c:c + n], start=(k == 0), stop=(k == KC - 1),
                                            skip_group_check=True)
                    ins.then_inc(pe_h.sem, 1)
                for g, j in enumerate(js):
                    wait(pe, dve_h, j)
                    for n in range(3):
                        if n == 0:
                            wait(pe, act_hT, j * 2 - 1)
                            wait(pe, act_xT, 5 * NT + i * G + G - 1)
                        elif n == 1:
                            wait(pe, dve_hT, j - 1)
                            wait(pe, dve_lg, i * G + G - 1)
                        else:
                            wait(pe, act_hT, j * 2)
                        for c in range(4 * n, min(4 * n + 4, FA // P)):
                            ins = pe.transpose(PS[:, 7 if n == 1 else 0, (c % 4) * R:(c % 4 + 1) * R],
                                               hm[0:R, g, c * P:(c + 1) * P], ident[0:R, 0:R])
                        ins.then_inc(pe_hT.sem, 1)
                    if g == G - 1:
                        wait(pe, act_hT, j * 2 + 1)
                        between()
                    wait(pe, act_hT, j * 2 + 1)
                    wait(pe, dve_hT, j)
                    project(j, 6 * NT, [hT[:, g, c] for c in range(FA // P)], [w2[:, c, :] for c in range(FA // P)], None, bank=6)

            norm_T(range(G), 5 * NT)
            with pe.Fori(0, NT // G - 1) as i:
                tiles(i, True)
            tiles(NT // G - 1, False)

        @block.scalar
        def _(act):
            for s in by_engine["act"]:
                s.credit(act)

            def norm_T(js, L):
                for g, j in enumerate(js):
                    wait(act, pe_xT, L + j)
                    act.copy(xT[:, g], PS[:, 0, 0:KC * R].rearrange("p (k r) -> p k r", k=KC))\
                       .then_inc(act_xT.sem, 1)

            def attention(js, U, V, scale, between):
                T = V.T
                for g, j in enumerate(js):
                    z = V.Z[:, g, :]
                    wait(act, dve_z, U + j)
                    if U == 0:
                        act.activation(z, z, ACT.Tanh, scale=1.0 / (30.0 * HD ** 0.5)).then_inc(act_tanh.sem, 1)
                        wait(act, act_tanh, j)
                    act.activation(z, z, ACT.Exp, scale=30.0 if U == 0 else scale).then_inc(act_e.sem, 1)
                for g, j in enumerate(js):
                    for n in (0, 2):
                        wait(act, pe_pT, (U + j) * 4 + n)
                        act.copy(V.PT[0:T, g, 4 * n:4 * n + 4, :], PS[0:T, PT_BANKS[n], :].rearrange("p (h q) -> p h q", h=4))\
                           .then_inc(act_pT.sem, 1)
                between()
                for g, j in enumerate(js):
                    wait(act, pe_cT, U + j)
                    c = PS[:, CT_BANKS[g], 0:KC * P].rearrange("p (k b s) -> p k b s", k=KC, b=2)[:, :, :, 0:S]
                    to = V.cT[:, g].rearrange("p k (b s) -> p k b s", b=2)
                    if U == 2 * NT:
                        act.activation(to[:, 0], c[:, 0], ACT.Identity, bias=bvcol[:, 0:1])
                        act.activation(to[:, 1], c[:, 1], ACT.Identity, bias=bvcol[:, 1:2]).then_inc(act_cT.sem, 1)
                    else:
                        act.copy(to, c).then_inc(act_cT.sem, 1)

            act.wait_ge(pool_init, 4)

            def tiles(i, more):
                js = [i * G + g for g in range(G)]

                def between():
                    if more:
                        norm_T([j + G for j in js], 0)

                for g, j in enumerate(js):
                    wait(act, pe_q, j)
                    for m in range(KC):
                        act.activation(SA.qT[:, g, m, 0:R], PS[:, Q_BANKS[g], m * R:(m + 1) * R], ACT.Identity,
                                       bias=bqk0[:, 0, m:m + 1]).then_inc(act_q.sem, 1)
                attention(js, 0, SA, None, between)

            norm_T(range(G), 0)
            with act.Fori(0, NT // G - 1) as i:
                tiles(i, True)
            tiles(NT // G - 1, False)

            def value_output(V):
                for n in range(H // 2):
                    wait(act, pe_vo, V + n)
                    act.copy(vo[:, 2 * n:2 * n + 2, :], PS[:, 6 + n % 2, :].rearrange("p (h d) -> p h d", h=2))\
                       .then_inc(act_vo.sem, 1)

            def squares(b, t, half):
                K = b * CT + t
                for n in (0, 1) if half == 0 else (2, 3):
                    wait(act, pe_kp, K * 4 + n)
                    if 4 * n >= ACC[t]:
                        i = sum(SUMS[:t]) + n - ACC[t] // 4
                        wait(act, dve_ss, b * sum(SUMS) + i - 2)
                        act.activation(sqr[0:CR, i % 2, :], PS[0:CR, n % 2, :], ACT.Square).then_inc(act_sq.sem, 1)
                    else:
                        wait(act, pool_vek, K - 2)
                        done = b * sum(ACC) + sum(ACC[:t]) + 4 * n
                        for h in range(4):
                            wait(act, act_scrap, done + h - 1)
                            ins = act.activation(scrap[0:CR, :], PS[0:CR, n % 2, h * XD:(h + 1) * XD], ACT.Square,
                                                 accum_out=ssr[0:CR, t % 2, 4 * n + h:4 * n + h + 1])
                            ins.then_inc(act_scrap.sem, 1)
                        wait(act, act_scrap, done + 3)
                        act.sem_inc(act_sq.sem, 1)

            def key_squares_1(b, t):
                n_rows = rows_in(1, t)
                wait(act, pe_k1, b * CT + t)
                wait(act, pe_k1T, b * CT + t - 3)
                act.copy(centred(t)[0:n_rows, :], PS[0:n_rows, 0, 0:D]).then_inc(act_k1c.sem, 1)
                wait(act, dve_k1ss, b * CT + t - 1)
                act.activation(squared[0:n_rows, :], PS[0:n_rows, 0, 0:D], ACT.Square).then_inc(act_k1s.sem, 1)

            def keys_T(b, t):
                n_rows = rows_in(1, t)
                wait(act, pe_k1T, b * CT + t)
                wait(act, pe_sx, B * CT + b * CT + t - 3)
                act.activation(keyT[:, t % 3, :, 0:n_rows], PS[:, 1, 0:KC * CR].rearrange("p (m r) -> p m r", m=KC)[:, :, 0:n_rows],
                               ACT.Identity, scale=lncol[:, 2:3], bias=lncol[:, 3:4]).then_inc(act_k1T.sem, 1)

            def keep_scores(b, t):
                n_rows = rows_in(1, t)
                K = B * CT + b * CT + t
                wait(act, pe_sx, K)
                wait(act, pe_pv, K - CT)
                wait(act, dve_sum, K - CT)
                act.copy(Sall[0:n_rows, t, :].rearrange("p (m w) -> p m w", m=2), PS[0:n_rows, 2:4, 0:W])\
                   .then_inc(act_t.sem, 1)

            def split_context(X, b, c):
                span = slice(c * CHUNK * CR, (c + 1) * CHUNK * CR)
                wait(act, sp_cxT[c], X * B + b)
                last = (b - 1) * CT + CHUNK * c + CHUNK - 1
                if X == 0 and not at_first(b):
                    wait(act, pe_sx, last)
                elif X == 1 and not at_first(b):
                    wait(act, pe_k1, last)
                act.copy(c_hi[:, span], cxT[:, span]).then_inc(act_chi.sem, 1)

            def split_queries(b):
                if not at_first(b):
                    wait(act, pe_sx, b * CT - 1)
                act.copy(q_hi[:, :, :], Qall[:, b]).then_inc(act_qhi.sem, 1)

            def probabilities(X, b, t, scale):
                K = (X * B + b) * CT + t
                n_rows = rows_in(X, t)
                wait(act, pool_d, K)
                wait(act, dve_d, K)
                p = Sall[0:n_rows, t, :]
                act.activation(p, p, ACT.Exp, scale=scale).then_inc(act_p.sem, 1)

            def keep_maxima(X, b):
                u = X * B + b
                if X == 1 or not at_first(b):
                    wait(act, pool_d, u * CT - 1)
                    wait(act, dve_d, u * CT - 1)
                for m in range(2):
                    act.wait_ge(pe_mb.sem, pe_mb.done(u) - 1 + m)
                    act.copy(Mb[0:CR, m * W:(m + 1) * W], PS[0:CR, 6 + m, 0:W]).then_inc(act_mb.sem, 1)

            def keep_sums(u):
                wait(act, pe_zb, u)
                wait(act, dve_ot, u - 1)
                act.copy(rz[:, :].rearrange("p (m w) -> p m w", m=2), PS[:, 6:8, 0:W]).then_inc(act_rz.sem, 1)

            def keep_outputs(X, b):
                wait(act, pe_pv, (X * B + b) * CT + CT - 1)
                act.copy(Qall[:, b], PS[:, 4:6, 0:W]).then_inc(act_un.sem, 1)

            def cross_attention(X):
                def iteration(b, stage, before, sums, ahead):
                    for u in range(CT + LAG):
                        if stage and X == 0 and u == 2:
                            split_queries(b)
                        if stage and u < CT:
                            if X == 0:
                                squares(b, u, 0)
                            else:
                                key_squares_1(b, u)
                        if u == 1 and before:
                            keep_maxima(X, b - 1)
                        if X == 0 and u == EXP and before:
                            probabilities(X, b - 1, 0, XD ** -0.5)
                        if stage and X == 0 and u < CT:
                            squares(b, u, 1)
                        for c in split_now(X, b, u, stage, ahead):
                            split_context(X, *c)
                        if stage and X == 1 and 2 <= u < CT + 2:
                            keys_T(b, u - 2)
                        if before and EXP + 1 - X <= u < CT + EXP:
                            probabilities(X, b - 1, u - EXP, (XD, HD)[X] ** -0.5)
                        if stage and X == 1 and u >= LAG:
                            keep_scores(b, u - LAG)
                        if u == CT + LAG - 1 and before:
                            keep_outputs(X, b - 1)
                        if u == LAG + 2 and sums:
                            keep_sums(X * B + b - 2)

                for c in range(CT // CHUNK):
                    split_context(X, 0, c)
                iteration(0, True, False, False, True)
                iteration(1, True, True, False, True)
                with act.Fori(2, B - 1) as b:
                    iteration(b, True, True, True, True)
                iteration(B - 1, True, True, True, False)
                iteration(B, False, True, True, False)
                iteration(B + 1, False, False, True, False)

            def stage_outputs(X):
                with act.Fori(0, NT // G) as i:
                    for g in range(G):
                        j = i * G + g
                        wait(act, dve_ot, X * B + B - 1)
                        wait(act, pe_y, (1 if X == 0 else 5) * NT + j - G)
                        act.copy(OTs[:, g, :, 0:S], Qall[:, 2 * j].rearrange("p m (h s) -> p (m h) s", h=HM))\
                           .then_inc(act_ots.sem, 1)

            act.wait_ge(sp_wx0, 8 * 16)
            act.copy(w_hi[:, :], wk_x0).then_inc(act_whi, 1)
            act.wait_ge(dve_wlo, 1)
            value_output(0)

            def tiles(i, more):
                js = [i * G + g for g in range(G)]

                def between():
                    if more:
                        norm_T([j + G for j in js], NT)

                for u in range(4 * G + 2):
                    if u < 4 * G:
                        n, k4 = u % 4, 4 * js[0] + u
                        wait(act, pe_qx, k4)
                        wait(act, dve_ssa, k4 - 4)
                        act.activation(sq_a[0:R, n * 512:(n + 1) * 512], PS[0:R, 1 + n, :], ACT.Square)\
                           .then_inc(act_sqa.sem, 1)
                    if u == 4 * G:
                        between()
                    if u >= 2:
                        n, k4 = (u - 2) % 4, 4 * js[0] + u - 2
                        wait(act, pe_qhT, k4)
                        wait(act, pe_qt, k4 - 4)
                        act.copy(qhT[:, 4 * n:4 * n + 4, :], PS[:, 5 + n % 2, 0:4 * R].rearrange("p (h r) -> p h r", h=4))\
                           .then_inc(act_qhT.sem, 1)

            norm_T(range(G), NT)
            with act.Fori(0, NT // G - 1) as i:
                tiles(i, True)
            tiles(NT // G - 1, False)
            wait(act, pe_qt, 4 * NT - 1)
            cross_attention(0)
            stage_outputs(0)


            def tiles(i, more):
                js = [i * G + g for g in range(G)]

                def between():
                    if more:
                        norm_T([j + G for j in js], 2 * NT)

                wait(act, pe_y, 2 * NT + js[-1])
                between()

            norm_T(range(G), 2 * NT)
            with act.Fori(0, NT // G - 1) as i:
                tiles(i, True)
            tiles(NT // G - 1, False)

            act.wait_ge(pool_init, 6)

            def tiles(i, more):
                js = [i * G + g for g in range(G)]

                def between():
                    if more:
                        norm_T([j + G for j in js], 3 * NT)

                attention(js, NT, SA, D ** -0.5, between)

            norm_T(range(G), 3 * NT)
            with act.Fori(0, NT // G - 1) as i:
                tiles(i, True)
            tiles(NT // G - 1, False)

            act.wait_ge(sp_wx1, 10 * 16)
            value_output(H // 2)
            act.wait_ge(dve_setup, 13)
            act.copy(w_hi[:, 0:D], wk_x1).then_inc(act_whi, 1)
            act.wait_ge(dve_setup, 22)
            act.copy(b_hi, bk_x1[0:1, :]).then_inc(act_whi, 1)
            act.copy(ones_r, ones[0:1, :]).then_inc(act_whi, 1)
            for n in range(2):
                act.wait_ge(dve_kd, 2 * n + 1 if n == 0 else 3)
                act.activation(sq1a[:, n, :], kd[:, n, :], ACT.Square).then_inc(act_kd, 1)
            for n in range(2):
                act.wait_ge(pe_kdT, n + 1)
                act.activation(kTd[:, :, n * P:(n + 1) * P], PS[:, 5, 0:KC * P].rearrange("p (m r) -> p m r", m=KC),
                               ACT.Identity, scale=lncol[:, 4:5], bias=lncol[:, 5:6]).then_inc(act_kd, 1)
            act.wait_ge(pool_init, 8)

            def tiles(i, more):
                js = [i * G + g for g in range(G)]

                def between():
                    if more:
                        norm_T([j + G for j in js], 4 * NT)

                for g, j in enumerate(js):
                    wait(act, dve_qs, j)
                    act.activation(sq1a[0:R, g, :], qs[0:R, g, :], ACT.Square).then_inc(act_q1s.sem, 1)
                for g, j in enumerate(js):
                    wait(act, pe_q1T, j)
                    act.activation(DCA.qT[:, g, :, 0:R], PS[:, 5, 0:KC * R].rearrange("p (m r) -> p m r", m=KC),
                                   ACT.Identity, scale=lncol[:, 0:1], bias=lncol[:, 1:2]).then_inc(act_q1.sem, 1)
                attention(js, 2 * NT, DCA, HD ** -0.5, between)

            norm_T(range(G), 4 * NT)
            with act.Fori(0, NT // G - 1) as i:
                tiles(i, True)
            tiles(NT // G - 1, False)
            wait(act, dve_x, 5 * NT - 1)

            cross_attention(1)
            stage_outputs(1)


            def tiles(i, more):
                js = [i * G + g for g in range(G)]

                def between():
                    if more:
                        norm_T([j + G for j in js], 5 * NT)

                for g, j in enumerate(js):
                    wait(act, dve_le, j)
                    act.activation(le[0:R, g, :], le[0:R, g, :], ACT.Exp).then_inc(act_le.sem, 1)
                    act.activation(lg[0:R, g, E:E + 1], lg[0:R, g, E:E + 1], ACT.Tanh, scale=0.5).then_inc(act_le.sem, 1)
                for g, j in enumerate(js):
                    wait(act, pe_h, j)
                    act.activation(th[0:R, g, :], PS[0:R, 1:4, :].rearrange("p a n -> p (a n)")[:, 0:FA], ACT.Tanh,
                                   scale=0.5).then_inc(act_th.sem, 1)
                for g, j in enumerate(js):
                    for n in (0, 2):
                        wait(act, pe_hT, j * 3 + n)
                        c = min(4, FA // P - 4 * n)
                        act.copy(hT[:, g, 4 * n:4 * n + c, :], PS[:, 0, 0:c * R].rearrange("p (c r) -> p c r", c=c))\
                           .then_inc(act_hT.sem, 1)
                between()

            norm_T(range(G), 5 * NT)
            with act.Fori(0, NT // G - 1) as i:
                tiles(i, True)
            tiles(NT // G - 1, False)

        @block.vector
        def _(dve):
            for s in by_engine["dve"]:
                s.credit(dve)

            def norm(js, L, J):
                for g, j in enumerate(js):
                    if J > 0:
                        wait(dve, dve_x, J - NT + j)
                    dve.bn_stats(lnst[0:R, g, :], x[0:R, j, :]).then_inc(dve_stats.sem, 1)
                for g, j in enumerate(js):
                    wait(dve, dve_stats, L + j)
                    dve.sem_inc(dve_beat, 1)
                    dve.bn_aggr(lnmv[0:R, g, :], lnst[0:R, g, :]).then_inc(dve_aggr.sem, 1)
                for g, j in enumerate(js):
                    wait(dve, pool_rs, L + j)
                    wait(dve, pe_xT, L + j - G)
                    dve.tensor_scalar(xn[0:R, g, :], x[0:R, j, :], lnmv[0:R, g, 0:1], lnrs[0:R, g:g + 1],
                                      ALU.subtract, ALU.mult).then_inc(dve_xn.sem, 1)

            def head_sel(T):
                return hmask[:, :].unsqueeze(2).broadcast_to([P, HM, T])

            def attention(js, U, V, values, between):
                T = V.T
                for g, j in enumerate(js):
                    wait(dve, pe_s, U + j)
                    s = PS[:, 3:5, 0:HM * T]
                    z = V.Z[:, g, :].rearrange("p (m z) -> p m z", m=KC)
                    if U == 0:
                        dve.tensor_tensor(z, s, abias[:, :, :].rearrange("p (m h) t -> p m (h t)", m=KC), ALU.add)\
                           .then_inc(dve_z.sem, 1)
                    else:
                        s = s.rearrange("p m (h t) -> p m h t", h=HM)
                        z = z.rearrange("p m (h t) -> p m h t", h=HM)
                        largest = V.mx[:, g, :].rearrange("p (m h) -> p m h", m=KC)
                        dve.tensor_reduce(largest, s, AX.X, ALU.max).then_inc(dve_mx.sem, 1)
                        wait(dve, dve_mx, U - NT + j)
                        dve.tensor_tensor(z, s, largest.unsqueeze(3).broadcast_to([P, KC, HM, T]), ALU.subtract)\
                           .then_inc(dve_z.sem, 1)
                for g, j in enumerate(js):
                    if U == 0:
                        wait(dve, act_e, j)
                        z = V.Z[:, g, :].rearrange("p (h t) -> p h t", h=H)
                        dve.tensor_tensor(z, z, causal[:, :].unsqueeze(1).broadcast_to([P, H, S]), ALU.mult)\
                           .then_inc(dve_p.sem, 1)
                values()
                for g, j in enumerate(js):
                    for n in (1, 3):
                        wait(dve, pe_pT, (U + j) * 4 + n)
                        dve.tensor_copy(V.PT[0:T, g, 4 * n:4 * n + 4, :], PS[0:T, PT_BANKS[n], :].rearrange("p (h q) -> p h q", h=4))\
                           .then_inc(dve_pT.sem, 1)
                between()
                for g, j in enumerate(js):
                    wait(dve, pe_o, U + j)
                    o = PS[:, 7, 0:H * (HD + 1)].rearrange("p (h d) -> p h d", h=H)
                    dve.reciprocal(V.rc[:, g, :], o[:, :, HD]).then_inc(dve_rc.sem, 1)
                    wait(dve, dve_rc, U + j)
                    if U == NT:
                        dve.tensor_tensor(V.cx[:, g, :].rearrange("p (h m d) -> p m h d", h=HM, m=KC),
                                          o[:, :, 0:HD].rearrange("p (m h) d -> p m h d", m=KC),
                                          V.rc[:, g, :].rearrange("p (m h) -> p m h", m=KC).unsqueeze(3)
                                          .broadcast_to([P, KC, HM, HD]), ALU.mult).then_inc(dve_cx.sem, 1)
                    else:
                        dve.tensor_tensor(V.cx[:, g, :].rearrange("p (h d) -> p h d", h=H), o[:, :, 0:HD],
                                          V.rc[:, g, :].unsqueeze(2).broadcast_to([P, H, HD]), ALU.mult)\
                           .then_inc(dve_cx.sem, 1)

            def add_rows(js, J, banks=(2, 2)):
                for g, j in enumerate(js):
                    wait(dve, pe_y, J + j)
                    dve.tensor_tensor(x[0:R, j, :], x[0:R, j, :], PS[0:R, banks[g], 0:D], ALU.add).then_inc(dve_x.sem, 1)

            dve.wait_ge(sp_w0, 15 * 16)
            dve.wait_ge(sp_x, 16)
            dve.wait_ge(pool_init, 4)
            dve.tensor_tensor(abias[:, :, :], rel[:, :].unsqueeze(1).broadcast_to([P, H, S]),
                              slopes[:, :].unsqueeze(2).broadcast_to([P, H, S]), ALU.mult).then_inc(dve_setup, 1)
            dve.wait_ge(dve_setup, 1)

            def tiles(i, more):
                js = [i * G + g for g in range(G)]

                def between():
                    if more:
                        norm([j + G for j in js], 0, 0)

                def values():
                    for g, j in enumerate(js):
                        wait(dve, pe_v, j)
                        dve.tensor_tensor(SA.va[0:S, g, :, :, 0:HD],
                                          PS[0:S, V_BANKS[g], :].rearrange("p (b h d) -> p b h d", b=2, h=H),
                                          bv0[0:S, :].rearrange("p (h d) -> p h d", h=H).unsqueeze(1)
                                          .broadcast_to([S, 2, H, HD]), ALU.add).then_inc(dve_va.sem, 1)

                for g, j in enumerate(js):
                    wait(dve, pe_k, j)
                    for b in range(2):
                        for m in range(KC):
                            kb = PS[:, K_BANKS[g], m * R + b * S:m * R + b * S + S]
                            dve.scalar_tensor_tensor(SA.Km[:, g, b, m].rearrange("p (h t) -> p h t", h=HM), kb.unsqueeze(1).broadcast_to([P, HM, S]),
                                                     bqk0[:, 1, m:m + 1], head_sel(S), ALU.add, ALU.mult)\
                               .then_inc(dve_km0.sem, 1)
                attention(js, 0, SA, values, between)
                add_rows(js, 0, banks=Y_BANKS)

            norm(range(G), 0, 0)
            with dve.Fori(0, NT // G - 1) as i:
                tiles(i, True)
            tiles(NT // G - 1, False)

            def by_head(row):
                return row.rearrange("p (m h) -> p m h", m=2).unsqueeze(3).broadcast_to([row.shape[0], 2, HM, S])

            def key_norms(b, t):
                K = b * CT + t
                wait(dve, pool_vek, K - 2)
                for n in range(ACC[t] // 4, 4):
                    wait(dve, act_sq, K * 4 + n)
                    dve.tensor_reduce(ssr[0:CR, t % 2, 4 * n:4 * n + 4],
                                      sqr[0:CR, (sum(SUMS[:t]) + n - ACC[t] // 4) % 2, :].rearrange("p (h d) -> p h d", h=4), AX.X, ALU.add)\
                       .then_inc(dve_ss.sem, 1)

            def scores(b, t):
                K = b * CT + t
                wait(dve, pool_rk, K)
                wait(dve, pe_sx, K)
                if not at_first(b):
                    wait(dve, pe_pv, K - CT)
                    wait(dve, dve_sum, K - CT)
                dve.tensor_tensor(Sall[0:CR, t, :].rearrange("p (m h s) -> p m h s", m=2, h=HM),
                                  PS[0:CR, 2:4, 0:W].rearrange("p m (h s) -> p m h s", h=HM),
                                  by_head(rkr[0:CR, t % 6, :]), ALU.mult).then_inc(dve_t.sem, 1)

            def running_maximum(X, b, t):
                K = (X * B + b) * CT + t
                n_rows = rows_in(X, t)
                if X == 0:
                    wait(dve, dve_t, K)
                else:
                    wait(dve, act_t, b * CT + t)
                if t == 0:
                    wait(dve, pe_mT, X * B + b - 1)
                    dve.tensor_copy(Mx[0:CR, :], Sall[0:CR, 0, :]).then_inc(dve_mxr.sem, 1)
                else:
                    wait(dve, dve_mxr, K - 1)
                    dve.tensor_tensor(Mx[0:n_rows, :], Mx[0:n_rows, :], Sall[0:n_rows, t, :], ALU.max)\
                       .then_inc(dve_mxr.sem, 1)

            def sum_probabilities(X, b, t):
                K = (X * B + b) * CT + t
                n_rows = rows_in(X, t)
                wait(dve, act_p, K)
                if t == 0:
                    wait(dve, pe_zc, X * B + b - 1)
                    dve.tensor_copy(Zs[0:CR, :], Sall[0:CR, 0, :]).then_inc(dve_sum.sem, 1)
                else:
                    wait(dve, dve_sum, K - 1)
                    dve.tensor_tensor(Zs[0:n_rows, :], Zs[0:n_rows, :], Sall[0:n_rows, t, :], ALU.add)\
                       .then_inc(dve_sum.sem, 1)

            def spread(v, rows, T):
                return v.unsqueeze(2).broadcast_to([rows, H, T])

            def diagonal(col, after, n, done):
                wait(dve, after, n)
                for q in (slice(0, 4), slice(4, 7)):
                    size = q.stop - q.start
                    dve.tensor_tensor(mdiag[:, q, :], ident[:, :].unsqueeze(1).broadcast_to([P, size, P]),
                                      col[:, q].unsqueeze(2).broadcast_to([P, size, P]), ALU.mult).then_inc(done.sem, 1)

            def maxima(u):
                wait(dve, pe_mT, u)
                for bank, n in ((6, 4), (7, 3)):
                    dve.tensor_reduce(mcol[:, 4 * (bank - 6):4 * (bank - 6) + n],
                                      PS[:, bank, 0:n * CR].rearrange("p (a r) -> p a r", a=n), AX.X, ALU.max)\
                       .then_inc(dve_mcol.sem, 1)
                wait(dve, dve_mcol, u)

            def reciprocal_sums(u):
                wait(dve, pe_zc, u)
                dve.reciprocal(zcol[:, 0:7], PS[:, 7, 4 * CR:4 * CR + 7]).then_inc(dve_zcol.sem, 1)

            def outputs(X, b):
                wait(dve, act_rz, X * B + b)
                wait(dve, act_un, X * B + b)
                o = Qall[:, b].rearrange("p m w -> p (m w)")
                dve.tensor_tensor(o, o, rz[:, :], ALU.mult).then_inc(dve_ot.sem, 1)

            def split_context(X, b, c):
                span = slice(c * CHUNK * CR, (c + 1) * CHUNK * CR)
                wait(dve, act_chi, (X * B + b) * (CT // CHUNK) + c)
                dve.tensor_tensor(c_lo[:, span], cxT[:, span], c_hi[:, span].bitcast(F32), ALU.subtract)\
                   .then_inc(dve_clo.sem, 1)

            def split_queries(b):
                wait(dve, act_qhi, b)
                dve.tensor_tensor(q_lo[:, :, :], Qall[:, b], q_hi[:, :, :].bitcast(F32), ALU.subtract)\
                   .then_inc(dve_qlo.sem, 1)

            def key_sums(b, t):
                n_rows = rows_in(1, t)
                wait(dve, act_k1s, b * CT + t)
                wait(dve, pool_k1v, b * CT + t - 2)
                dve.tensor_reduce(ssr[0:n_rows, t % 2, :], squared[0:n_rows, :].rearrange("p (h d) -> p h d", h=H),
                                  AX.X, ALU.add).then_inc(dve_k1ss.sem, 1)

            def normal_keys(b, t):
                n_rows = rows_in(1, t)
                wait(dve, pool_k1r, b * CT + t)
                wait(dve, act_k1c, b * CT + t)
                k = centred(t)[0:n_rows, :].rearrange("p (h d) -> p h d", h=H)
                dve.tensor_tensor(k, k, spread(rkr[0:n_rows, t % 6, :], n_rows, HD), ALU.mult).then_inc(dve_k1n.sem, 1)

            def less_maximum(X, b, t):
                K = (X * B + b) * CT + t
                n_rows = rows_in(X, t)
                if t == 0:
                    wait(dve, act_mb, X * B + b)
                wait(dve, dve_mxr, K)
                s = Sall[0:n_rows, t, 0:DIFF[X]]
                dve.tensor_tensor(s, s, Mb[0:n_rows, 0:DIFF[X]], ALU.subtract).then_inc(dve_d.sem, 1)

            def cross_attention(X):
                def iteration(b, stage, before, sums, ahead):
                    u0 = X * B + b
                    for u in range(CT + LAG):
                        if stage and X == 1 and u == 0:
                            key_sums(b, 0)
                        if u == 0 and before:
                            maxima(u0 - 1)
                        if u == 0 and sums:
                            reciprocal_sums(u0 - 2)
                        if u == 0 and before:
                            diagonal(mcol, pe_zb, u0 - 3, dve_diag)
                        if stage and X == 0 and u == 2:
                            split_queries(b)
                        if stage and X == 0 and u < CT:
                            key_norms(b, u)
                        if stage and X == 1 and 2 <= u < CT + 2:
                            normal_keys(b, u - 2)
                        if stage and X == 1 and 1 <= u < CT:
                            key_sums(b, u)
                        for c in split_now(X, b, u, stage, ahead):
                            split_context(X, *c)
                        if before and 0 <= u - LESS < CT:
                            less_maximum(X, b - 1, u - LESS)
                        if before and PV <= u < CT + PV:
                            sum_probabilities(X, b - 1, u - PV)
                        if stage and X == 0 and u >= LAG:
                            scores(b, u - LAG)
                            running_maximum(X, b, u - LAG)
                        if stage and X == 1 and u > LAG:
                            running_maximum(X, b, u - LAG - 1)
                        if stage and X == 1 and u == CT + LAG - 1:
                            running_maximum(X, b, u - LAG)
                        if u == LAG + 1 and sums:
                            wait(dve, dve_zcol, u0 - 2)
                            diagonal(zcol, pe_mb, u0 - 1 if before else u0 - 2, dve_zdiag)
                        if u == LAG + 3 and sums:
                            outputs(X, b - 2)

                for c in range(CT // CHUNK):
                    split_context(X, 0, c)
                iteration(0, True, False, False, True)
                iteration(1, True, True, False, True)
                with dve.Fori(2, B - 1) as b:
                    iteration(b, True, True, True, True)
                iteration(B - 1, True, True, True, False)
                iteration(B, False, True, True, False)
                iteration(B + 1, False, False, True, False)

            dve.wait_ge(sp_wx0, 8 * 16)
            dve.tensor_scalar(wkT_x0, wkT_x0, gqk[:, 0:1], gqk[:, 1:2], ALU.mult, ALU.mult).then_inc(dve_setup, 1)
            dve.wait_ge(act_whi, 1)
            dve.tensor_tensor(w_lo[:, :], wk_x0, w_hi[:, :].bitcast(F32), ALU.subtract).then_inc(dve_wlo, 1)

            def tiles(i, more):
                js = [i * G + g for g in range(G)]

                def between():
                    if more:
                        norm([j + G for j in js], NT, NT)

                for u in range(4 * G + 3):
                    if u < 4 * G:
                        g, n, k4 = u // 4, u % 4, 4 * js[0] + u
                        wait(dve, act_sqa, k4)
                        dve.tensor_reduce(ss_a[0:R, g, 4 * n:4 * n + 4],
                                          sq_a[0:R, n * 512:(n + 1) * 512].rearrange("p (h d) -> p h d", h=4),
                                          AX.X, ALU.add).then_inc(dve_ssa.sem, 1)
                    if u == 4 * G - 1:
                        between()
                    if 1 <= u <= 4 * G:
                        g, n, k4 = (u - 1) // 4, (u - 1) % 4, 4 * js[0] + u - 1
                        wait(dve, pool_rqa, k4)
                        wait(dve, pe_qhT, k4 - 4)
                        dve.tensor_tensor(qn_a[0:R, 4 * n:4 * n + 4, :], PS[0:R, 1 + n, :].rearrange("p (h d) -> p h d", h=4),
                                          rq_a[0:R, g, 4 * n:4 * n + 4].unsqueeze(2).broadcast_to([R, 4, XD]), ALU.mult)\
                           .then_inc(dve_qh.sem, 1)
                    if u >= 3:
                        g, n, k4 = (u - 3) // 4, (u - 3) % 4, 4 * js[0] + u - 3
                        wait(dve, pe_qt, k4)
                        q = Qall[:, bass.ds(2 * js[g], 2)].rearrange("p b m (h s) -> p (m h) b s", h=HM)
                        dve.tensor_copy(q[:, 4 * n:4 * n + 4],
                                        PS[:, 7, 0:4 * R].rearrange("p (h b s) -> p h b s", h=4, b=2))\
                           .then_inc(dve_qt.sem, 1)

            norm(range(G), NT, NT)
            with dve.Fori(0, NT // G - 1) as i:
                tiles(i, True)
            tiles(NT // G - 1, False)
            cross_attention(0)
            with dve.Fori(0, NT // G) as i:
                add_rows([i * G + g for g in range(G)], NT, banks=(2, 3))

            dve.wait_ge(sp_fac, 16)
            mixed = fmix[:, :, :].rearrange("p k n -> p (k n)")
            dve.tensor_reduce(mixed, factors, AX.X, ALU.add).then_inc(dve_setup, 1)
            dve.wait_ge(dve_setup, 3)
            dve.tensor_scalar(mixed, mixed, 8 ** -0.5, None, ALU.mult).then_inc(dve_setup, 1)

            def tiles(i, more):
                js = [i * G + g for g in range(G)]

                def between():
                    if more:
                        norm([j + G for j in js], 2 * NT, 2 * NT)

                between()
                add_rows(js, 2 * NT, banks=(2, 3))

            norm(range(G), 2 * NT, 2 * NT)
            with dve.Fori(0, NT // G - 1) as i:
                tiles(i, True)
            tiles(NT // G - 1, False)

            dve.wait_ge(pool_init, 6)

            def tiles(i, more):
                js = [i * G + g for g in range(G)]

                def between():
                    if more:
                        norm([j + G for j in js], 3 * NT, 3 * NT)

                def values():
                    for g, j in enumerate(js):
                        wait(dve, pe_v, NT + j)
                        dve.tensor_copy(SA.va[0:S, g, :, 0:HM, 0:HD],
                                        PS[0:S, V_BANKS[g], 0:2 * P].rearrange("p (b h d) -> p b h d", b=2, h=HM)).then_inc(dve_va.sem, 1)

                for g, j in enumerate(js):
                    wait(dve, pe_q, NT + j)
                    q = PS[:, Q_BANKS[g], 0:2 * KC * R].rearrange("p (z r) -> p z r", z=2 * KC)
                    along = lambda tab: tab[:, :].unsqueeze(1).broadcast_to([P, KC, R])
                    dve.tensor_tensor(rope[:, 0], q[:, 0:KC], along(cosT), ALU.mult).then_inc(dve_rope.sem, 1)
                    dve.tensor_tensor(rope[:, 1], q[:, KC:2 * KC], along(sinT), ALU.mult).then_inc(dve_rope.sem, 1)
                    wait(dve, pe_k, NT + j)
                    dve.tensor_tensor(rope[:, 2, 0], PS[:, K_BANKS[g], 0:R], cosT[:, :], ALU.mult).then_inc(dve_rope.sem, 1)
                    dve.tensor_tensor(rope[:, 2, 1], PS[:, K_BANKS[g], R:2 * R], sinT[:, :], ALU.mult).then_inc(dve_rope.sem, 1)
                    wait(dve, dve_rope, j)
                    dve.tensor_tensor(SA.qT[:, g, :, 0:R], rope[:, 0], rope[:, 1], ALU.add).then_inc(dve_qk1.sem, 1)
                    dve.tensor_tensor(rope[:, 2, 0], rope[:, 2, 0], rope[:, 2, 1], ALU.add).then_inc(dve_qk1.sem, 1)
                    wait(dve, dve_qk1, j)
                    for b in range(2):
                        dve.tensor_tensor(SA.Km[:, g, b, 0].rearrange("p (h t) -> p h t", h=HM),
                                          rope[:, 2, 0, b * S:(b + 1) * S].unsqueeze(1).broadcast_to([P, HM, S]),
                                          head_sel(S), ALU.mult).then_inc(dve_km1.sem, 1)
                    wait(dve, dve_km1, j)
                attention(js, NT, SA, values, between)
                add_rows(js, 3 * NT, banks=Y_BANKS)

            norm(range(G), 3 * NT, 3 * NT)
            with dve.Fori(0, NT // G - 1) as i:
                tiles(i, True)
            tiles(NT // G - 1, False)

            def centre(v, n, at):
                v = v.rearrange("p (n d) -> p n d", d=HD)
                dve.wait_ge(dve_setup, at)
                dve.tensor_reduce(mean[:, 0:n], v, AX.X, ALU.add).then_inc(dve_setup, 1)
                dve.wait_ge(dve_setup, at + 1)
                dve.tensor_scalar(mean[:, 0:n], mean[:, 0:n], 1.0 / HD, None, ALU.mult).then_inc(dve_setup, 1)
                dve.wait_ge(dve_setup, at + 2)
                dve.tensor_tensor(v, v, mean[:, 0:n].unsqueeze(2).broadcast_to([P, n, HD]), ALU.subtract)\
                   .then_inc(dve_setup, 1)

            dve.wait_ge(sp_wx1, 10 * 16)
            centre(wq_x1.rearrange("p k n -> p (k n)"), KC * H, 4)
            centre(wkv_d[:, 0:D], H, 7)
            centre(wk_x1, H, 10)
            centre(bq_x1, H, 13)
            centre(bkv_d[:, 0:D], H, 16)
            centre(bk_x1, H, 19)
            dve.wait_ge(dve_setup, 22)
            dve.wait_ge(act_whi, 4)
            dve.tensor_tensor(b_lo, bk_x1[0:1, :], b_hi.bitcast(F32), ALU.subtract).then_inc(dve_wlo, 1)
            dve.tensor_tensor(w_lo[:, 0:D], wk_x1, w_hi[:, 0:D].bitcast(F32), ALU.subtract).then_inc(dve_wlo, 1)
            for n in range(2):
                dve.wait_ge(pe_kd, n + 1)
                dve.tensor_tensor(kd[:, n, :], PS[:, 1, 0:D], bkv_d[:, 0:D], ALU.add).then_inc(dve_kd, 1)
                dve.wait_ge(act_kd, n + 1)
                dve.tensor_reduce(ss1a[:, n, :], sq1a[:, n, :].rearrange("p (h d) -> p h d", h=H), AX.X, ALU.add)\
                   .then_inc(dve_kd, 1)
            for n in range(2):
                dve.wait_ge(pool_kd, 2 * n + 2)
                dve.tensor_tensor(kd[:, n, :].rearrange("p (h d) -> p h d", h=H), kd[:, n, :].rearrange("p (h d) -> p h d", h=H),
                                  spread(rs1a[:, n, :], P, HD), ALU.mult).then_inc(dve_kd, 1)
            dve.wait_ge(pool_init, 8)
            dve.wait_ge(act_kd, 4)

            def tiles(i, more):
                js = [i * G + g for g in range(G)]

                def between():
                    if more:
                        norm([j + G for j in js], 4 * NT, 4 * NT)

                def values():
                    for g, j in enumerate(js):
                        wait(dve, pe_v, 2 * NT + j)
                        dve.tensor_tensor(DCA.va[0:NDCA, g, :, :, 0:HD],
                                          PS[0:NDCA, V_BANKS[g], :].rearrange("p (b h d) -> p b h d", b=2, h=H),
                                          bkv_d[0:NDCA, D:2 * D].rearrange("p (h d) -> p h d", h=H).unsqueeze(1)
                                          .broadcast_to([NDCA, 2, H, HD]), ALU.add).then_inc(dve_va.sem, 1)
                    for g, j in enumerate(js):
                        wait(dve, act_q1, j)
                        for b in range(2):
                            for m in range(KC):
                                dve.tensor_tensor(Qall[:, 2 * j + b, m].rearrange("p (h s) -> p h s", h=HM),
                                                  DCA.qT[:, g, m, b * S:(b + 1) * S].unsqueeze(1).broadcast_to([P, HM, S]),
                                                  head_sel(S), ALU.mult).then_inc(dve_q1m.sem, 1)

                for g, j in enumerate(js):
                    wait(dve, pe_q1, j)
                    dve.tensor_tensor(qs[0:R, g, :], PS[0:R, 1, 0:D], bq_x1[0:R, :], ALU.add).then_inc(dve_qs.sem, 1)
                for g, j in enumerate(js):
                    wait(dve, act_q1s, j)
                    dve.tensor_reduce(ss1a[0:R, g, :], sq1a[0:R, g, :].rearrange("p (h d) -> p h d", h=H), AX.X, ALU.add)\
                       .then_inc(dve_q1ss.sem, 1)
                for g, j in enumerate(js):
                    wait(dve, pool_q1r, j)
                    q = qs[0:R, g, :].rearrange("p (h d) -> p h d", h=H)
                    dve.tensor_tensor(q, q, spread(rs1a[0:R, g, :], R, HD), ALU.mult).then_inc(dve_q1n.sem, 1)
                    for b in range(2):
                        for m in range(KC):
                            dve.tensor_tensor(DCA.Km[:, g, b, m].rearrange("p (h t) -> p h t", h=HM),
                                              kTd[:, m, bass.ds((2 * j + b) * NDCA, NDCA)].unsqueeze(1)
                                              .broadcast_to([P, HM, NDCA]), head_sel(NDCA), ALU.mult)\
                               .then_inc(dve_kmd.sem, 1)
                attention(js, 2 * NT, DCA, values, between)
                add_rows(js, 4 * NT, banks=Y_BANKS)

            norm(range(G), 4 * NT, 4 * NT)
            with dve.Fori(0, NT // G - 1) as i:
                tiles(i, True)
            tiles(NT // G - 1, False)

            cross_attention(1)
            with dve.Fori(0, NT // G) as i:
                add_rows([i * G + g for g in range(G)], 5 * NT, banks=(2, 3))


            def tiles(i, more):
                js = [i * G + g for g in range(G)]

                def between():
                    if more:
                        norm([j + G for j in js], 5 * NT, 6 * NT)

                for g, j in enumerate(js):
                    wait(dve, pe_lg, j)
                    dve.tensor_copy(lg[0:R, g, :], PS[0:R, 7, 0:E + 1]).then_inc(dve_lg.sem, 1)
                for g, j in enumerate(js):
                    wait(dve, dve_lg, j)
                    dve.tensor_reduce(lm[0:R, g, :], lg[0:R, g, 0:E], AX.X, ALU.max).then_inc(dve_lm.sem, 1)
                for g, j in enumerate(js):
                    wait(dve, dve_lm, j)
                    dve.tensor_scalar(le[0:R, g, :], lg[0:R, g, 0:E], lm[0:R, g, :], None, ALU.subtract)\
                       .then_inc(dve_le.sem, 1)
                for g, j in enumerate(js):
                    wait(dve, act_le, j)
                    dve.sem_inc(dve_beat, 1)
                    dve.max(top[0:R, g, :], le[0:R, g, :]).then_inc(dve_top.sem, 1)
                    wait(dve, dve_top, j)
                    dve.sem_inc(dve_beat, 1)
                    dve.max_index(topi[0:R, g, :], top[0:R, g, :], le[0:R, g, :]).then_inc(dve_topi.sem, 1)
                    wait(dve, dve_topi, j)
                    dve.tensor_copy(topf[0:R, g, :], topi[0:R, g, :]).then_inc(dve_topf.sem, 1)
                    dve.tensor_tensor(tw[0:R, g, 0:1], top[0:R, g, 0:1], top[0:R, g, 1:2], ALU.add).then_inc(dve_tw.sem, 1)
                    dve.wait_ge(dve_tw.sem, dve_tw.done(j) - 2)
                    dve.reciprocal(tw[0:R, g, 1:2], tw[0:R, g, 0:1]).then_inc(dve_tw.sem, 1)
                    dve.wait_ge(dve_tw.sem, dve_tw.done(j) - 1)
                    dve.tensor_scalar(tw[0:R, g, 2:4], top[0:R, g, 0:2], tw[0:R, g, 1:2], 0.5, ALU.mult, ALU.mult)\
                       .then_inc(dve_tw.sem, 1)
                    wait(dve, dve_tw, j)
                    wait(dve, dve_topf, j)
                    for n in range(2):
                        dve.tensor_scalar(hot[0:R, g, n, :], eidx[0:R, :], topf[0:R, g, n:n + 1], tw[0:R, g, 2 + n:3 + n],
                                          ALU.is_equal, ALU.mult).then_inc(dve_hot.sem, 1)
                    wait(dve, dve_hot, j)
                    dve.tensor_tensor(comb[0:R, g, 0:E], hot[0:R, g, 0, :], hot[0:R, g, 1, :], ALU.add).then_inc(dve_comb.sem, 1)
                    dve.tensor_scalar(comb[0:R, g, E:EW], lg[0:R, g, E:E + 1].broadcast_to([R, EW - E]), 1.0, 0.25,
                                      ALU.add, ALU.mult).then_inc(dve_comb.sem, 1)
                for g, j in enumerate(js):
                    wait(dve, act_th, j)
                    wait(dve, pe_h, j)
                    flat_h = hm[0:R, g, :]
                    h1, h3 = (PS[0:R, 1:6, :].rearrange("p a n -> p (a n)")[:, c:c + FA] for c in (0, FA))
                    dve.scalar_tensor_tensor(flat_h, th[0:R, g, :], 1.0, h1, ALU.add, ALU.mult).then_inc(dve_h.sem, 1)
                    dve.wait_ge(dve_h.sem, dve_h.done(j) - 2)
                    dve.tensor_tensor(flat_h, flat_h, h3, ALU.mult).then_inc(dve_h.sem, 1)
                    dve.wait_ge(dve_h.sem, dve_h.done(j) - 1)
                    wait(dve, dve_comb, j)
                    blocks = flat_h.rearrange("p (e i) -> p e i", i=FI)
                    dve.tensor_tensor(blocks, blocks, comb[0:R, g, :].unsqueeze(2).broadcast_to([R, EW, FI]), ALU.mult)\
                       .then_inc(dve_h.sem, 1)
                    if g == G - 1:
                        between()
                    wait(dve, pe_hT, j * 3 + 1)
                    dve.tensor_copy(hT[:, g, 4:8, :], PS[:, 7, 0:4 * R].rearrange("p (c r) -> p c r", c=4)).then_inc(dve_hT.sem, 1)
                add_rows(js, 6 * NT, banks=(6, 6))

            norm(range(G), 5 * NT, 6 * NT)
            with dve.Fori(0, NT // G - 1) as i:
                tiles(i, True)
            tiles(NT // G - 1, False)

        @block.gpsimd
        def _(pool):
            for s in by_engine["pool"]:
                s.credit(pool)
            pool.memset(nhalf[:, :], -0.5).then_inc(pool_init, 1)
            pool.memset(ones[:, :], 1.0).then_inc(pool_init, 1)
            pool.memset(SA.qT, 0.0).then_inc(pool_init, 1)
            pool.memset(SA.va, 1.0).then_inc(pool_init, 1)
            pool.wait_ge(pool_init, 4)

            def norm(js, L, eps):
                for g, j in enumerate(js):
                    wait(pool, dve_aggr, L + j)
                    pool.sem_inc(pool_beat, 1)
                    pool.tensor_scalar(lnve[0:R, g:g + 1], lnmv[0:R, g, 1:2], eps, None, ALU.add).then_inc(pool_ve.sem, 1)
                    wait(pool, pool_ve, L + j)
                    pool.tensor_tensor(lnrs[0:R, g:g + 1], lnve[0:R, g:g + 1], nhalf[0:R, 0:1], ALU.pow)\
                        .then_inc(pool_rs.sem, 1)

            with pool.Fori(0, NT // G) as i:
                norm([i * G + g for g in range(G)], 0, 1e-5)

            def key_norms(b, t):
                K = b * CT + t
                wait(pool, dve_ss, b * sum(SUMS) + sum(SUMS[:t + 1]) - 1)
                wait(pool, act_scrap, b * sum(ACC) + sum(ACC[:t + 1]) - 1)
                wait(pool, dve_t, K - 6)
                pool.sem_inc(pool_beat, 1)
                pool.tensor_scalar(vek[0:CR, t % 2, :], ssr[0:CR, t % 2, :], 1.0 / XD, 1e-5, ALU.mult, ALU.add)\
                    .then_inc(pool_vek.sem, 1)
                wait(pool, pool_vek, K)
                pool.tensor_tensor(rkr[0:CR, t % 6, :], vek[0:CR, t % 2, :], nhalf[0:CR, 0:H], ALU.pow)\
                    .then_inc(pool_rk.sem, 1)

            def less_maximum(X, b, t):
                K = (X * B + b) * CT + t
                n_rows = rows_in(X, t)
                if t == 0:
                    wait(pool, act_mb, X * B + b)
                if X == 0:
                    wait(pool, dve_t, K)
                else:
                    wait(pool, act_t, b * CT + t)
                wait(pool, dve_mxr, K)
                s = Sall[0:n_rows, t, DIFF[X]:]
                pool.tensor_tensor(s, s, Mb[0:n_rows, DIFF[X]:], ALU.subtract).then_inc(pool_d.sem, 1)

            def key_norms_1(b, t):
                n_rows = rows_in(1, t)
                wait(pool, dve_k1ss, b * CT + t)
                wait(pool, dve_k1n, b * CT + t - 2)
                pool.sem_inc(pool_beat, 1)
                pool.tensor_scalar(vek[0:n_rows, t % 2, :], ssr[0:n_rows, t % 2, :], 1.0 / HD, 1e-6, ALU.mult, ALU.add)\
                    .then_inc(pool_k1v.sem, 1)
                wait(pool, pool_k1v, b * CT + t)
                pool.tensor_tensor(rkr[0:n_rows, t % 6, :], vek[0:n_rows, t % 2, :], nhalf[0:n_rows, 0:H], ALU.pow)\
                    .then_inc(pool_k1r.sem, 1)

            def cross_attention(X):
                def iteration(b, stage, before):
                    for u in range(CT + LAG):
                        if X == 1 and stage and u < CT:
                            key_norms_1(b, u)
                        if before and 0 <= u - LESS < CT:
                            less_maximum(X, b - 1, u - LESS)
                        if X == 0 and stage and u < CT:
                            key_norms(b, u)

                iteration(0, True, False)
                with pool.Fori(1, B) as b:
                    iteration(b, True, True)
                iteration(B, False, True)

            def stage_outputs(X):
                with pool.Fori(0, NT // G) as i:
                    for g in range(G):
                        j = i * G + g
                        wait(pool, dve_ot, X * B + B - 1)
                        wait(pool, pe_y, (1 if X == 0 else 5) * NT + j - G)
                        pool.sem_inc(pool_beat, 1)
                        pool.tensor_copy(OTs[:, g, :, S:R], Qall[:, 2 * j + 1].rearrange("p m (h s) -> p (m h) s", h=HM))\
                            .then_inc(pool_ots.sem, 1)

            with pool.Fori(0, NT // G) as i:
                js = [i * G + g for g in range(G)]
                norm(js, NT, 1e-5)
                for u in range(4 * G):
                    g, n, k4 = u // 4, u % 4, 4 * js[0] + u
                    heads = slice(4 * n, 4 * n + 4)
                    wait(pool, dve_ssa, k4)
                    pool.sem_inc(pool_beat, 1)
                    pool.tensor_scalar(ss_a[0:R, g, heads], ss_a[0:R, g, heads], 1.0 / XD, 1e-5, ALU.mult, ALU.add)\
                        .then_inc(pool_vea.sem, 1)
                    wait(pool, pool_vea, k4)
                    pool.tensor_tensor(rq_a[0:R, g, heads], ss_a[0:R, g, heads], nhalf[0:R, 0:4], ALU.pow)\
                        .then_inc(pool_rqa.sem, 1)
            wait(pool, pe_qt, 4 * NT - 1)
            cross_attention(0)
            stage_outputs(0)

            with pool.Fori(0, NT // G) as i:
                norm([i * G + g for g in range(G)], 2 * NT, 1e-5)

            wait(pool, act_ots, NT - 1)
            pool.memset(SA.qT, 0.0).then_inc(pool_init, 1)
            pool.memset(SA.va, 1.0).then_inc(pool_init, 1)
            with pool.Fori(0, NT // G) as i:
                norm([i * G + g for g in range(G)], 3 * NT, 1e-5)

            def rsqrt_rows(to, v, rows, n, ready_v, ready_r, index):
                pool.sem_inc(pool_beat, 1)
                pool.tensor_scalar(v, v, 1.0 / HD, 1e-6, ALU.mult, ALU.add).then_inc(ready_v.sem, 1)
                wait(pool, ready_v, index)
                pool.tensor_tensor(to, v, nhalf[0:rows, 0:n], ALU.pow).then_inc(ready_r.sem, 1)

            wait(pool, pe_y, 4 * NT - 1)
            pool.memset(DCA.qT, 0.0).then_inc(pool_init, 1)
            pool.memset(DCA.va, 1.0).then_inc(pool_init, 1)
            for n in range(2):
                pool.wait_ge(dve_kd, 2 * n + 2)
                pool.tensor_scalar(ss1a[:, n, :], ss1a[:, n, :], 1.0 / HD, 1e-6, ALU.mult, ALU.add).then_inc(pool_kd, 1)
                pool.wait_ge(pool_kd, 2 * n + 1)
                pool.tensor_tensor(rs1a[:, n, :], ss1a[:, n, :], nhalf[:, 0:H], ALU.pow).then_inc(pool_kd, 1)
            pool.wait_ge(sp_wx1, 10 * 16)
            with pool.Fori(0, NT // G) as i:
                js = [i * G + g for g in range(G)]
                for g, j in enumerate(js):
                    wait(pool, pe_v, 2 * NT + i * G - 1)
                    pool.sem_inc(pool_beat, 1)
                    pool.tensor_copy(yds[:, g, :], ydT[:, bass.ds(2 * NDCA * j, 2 * NDCA)]).then_inc(pool_yd.sem, 1)
                norm(js, 4 * NT, 1e-5)
                for g, j in enumerate(js):
                    wait(pool, dve_q1ss, j)
                    rsqrt_rows(rs1a[0:R, g, :], ss1a[0:R, g, :], R, H, pool_q1v, pool_q1r, j)
            wait(pool, dve_x, 5 * NT - 1)

            cross_attention(1)
            stage_outputs(1)

            with pool.Fori(0, NT // G) as i:
                norm([i * G + g for g in range(G)], 5 * NT, 1e-5)


def layout(v):
    f = {n: np.asarray(t) for n, t in v.items()}

    def chunks(w):
        return np.ascontiguousarray(w.reshape(-1, P, w.shape[1]).transpose(1, 0, 2))

    def column(b):
        return np.ascontiguousarray(b.reshape(-1, P).T)

    out = {
        "x": f["x"].reshape(B * S, D),
        "wq0": chunks(f["L0_attn_Wq"].T), "wk0": chunks(f["L0_attn_Wk"].T), "wv0": chunks(f["L0_attn_Wv"].T),
        "wo0": chunks(f["L0_attn_Wo"].T),
        "bqk0": np.stack([column(f["L0_attn_bq"]), column(f["L0_attn_bk"])], axis=1),
        "bv0": f["L0_attn_bv"], "slopes": f["L0_attn_alibi_slopes"],
        "rows": np.stack([f["L0_attn_bo"], f["L0_ffn_bias"], f["L1_xattn_bo"], f["L1_xattn_bo"]]),
        "wq_x0": chunks(f["L0_xattn_Wq"]),
        "wkT_x0": f["L0_xattn_Wk"].reshape(CD, H, XD).transpose(2, 1, 0),
        "wvT_x0": f["L0_xattn_Wv"].reshape(CD, H, XD).transpose(2, 1, 0),
        "wo_x0": f["L0_xattn_Wo"].reshape(H, XD, D).transpose(1, 0, 2),
        "wk_x0": f["L0_xattn_Wk"],
        "ctx": f["ctx_1024"], "ctxT": f["ctx_1024"].transpose(0, 2, 1),
        "gqk": np.stack([f["L0_xattn_gq"], f["L0_xattn_gk"]], axis=1),
    }
    heads = f["L1_attn_W_Q"].reshape(HD, HM, KC, D).transpose(2, 1, 0, 3)
    keys = f["L1_attn_W_K"].reshape(HD, HM, D).transpose(1, 0, 2)
    swap = (np.arange(HD) + HD // 2) % HD
    out.update(
        factors=f["L0_ffn_factors"].reshape(8, KC, P, D).transpose(2, 1, 3, 0).reshape(P, KC * D, 8),
        wq1=chunks(np.concatenate([heads.reshape(D, D), heads[:, :, swap].reshape(D, D)]).T),
        wk1=chunks(np.concatenate([keys.reshape(P, D), keys[:, swap].reshape(P, D)]).T),
        wv1=chunks(f["L1_attn_W_V"].reshape(HD, HM, D).transpose(1, 0, 2).reshape(P, D).T),
        wo1=chunks(f["L1_attn_W_O"].T),
        wq_x1=chunks(f["L1_xattn_Wq"]), wk_x1=f["L1_xattn_Wk"], wkv_d=f["L1_xattn_Wkv_dca"],
        bq_x1=f["L1_xattn_bq"], bk_x1=f["L1_xattn_bk"], bkv_d=f["L1_xattn_bkv_dca"],
        wo_x1=chunks(f["L1_xattn_Wo"]), woh_x1=f["L1_xattn_Wo"].reshape(H, HD, D).transpose(1, 0, 2),
        ydT=f["ctx_1024"][:, C - NDCA:].reshape(B * NDCA, CD).T,
    )
    kv = np.concatenate([f["L1_xattn_Wk"], f["L1_xattn_Wv"]], axis=1).reshape(CD, H, 2, HD)
    bkv = np.concatenate([f["L1_xattn_bk"], f["L1_xattn_bv"]]).reshape(H, 2, HD)
    out.update(
        wk_x1=kv[:, :, 0].reshape(CD, D), bk_x1=bkv[:, 0].reshape(D),
        wvT_x1=kv[:, :, 1].transpose(2, 1, 0), bvcol=column(bkv[:, 1].reshape(D)),
        lncol=np.stack([np.concatenate([f[n]] * HM) for n in (
            "L1_xattn_qn_w", "L1_xattn_qn_b", "L1_xattn_kn_w", "L1_xattn_kn_b", "L1_xattn_kn_dca_w", "L1_xattn_kn_dca_b")], axis=1),
        w13=np.stack([chunks(np.concatenate([f[e].reshape(E * FI, D), f[w]]).T)
                      for e, w in (("L1_ffn_w1", "L1_ffn_ws_gate"), ("L1_ffn_w3", "L1_ffn_ws_up"))], axis=2),
        w2=chunks(np.concatenate([f["L1_ffn_w2"].transpose(0, 2, 1).reshape(E * FI, D), f["L1_ffn_ws_down"].T])),
        wr=chunks(np.concatenate([f["L1_ffn_gate_w"], f["L1_ffn_shared_gate_w"]]).T),
    )
    row = np.arange(P)
    q = (row % SL).astype(np.float32)
    key = np.arange(S, dtype=np.float32)
    d = row % HD
    half = HD // 2
    inv = (1.0 / 10000.0 ** (np.arange(half, dtype=np.float32) * 2.0 / HD)).astype(np.float32)
    pos = (np.arange(R) % S).astype(np.float32)
    ang = (pos[None, :] * inv[d % half][:, None]).astype(np.float32)
    sign = np.where(d < half, -1.0, 1.0).astype(np.float32)
    out.update(
        ident=np.eye(P, dtype=np.float32),
        hmask=(row[:, None] // HD == np.arange(HM)[None, :]).astype(np.float32),
        rel=(key[None, :] - q[:, None]).astype(np.float32),
        causal=(key[None, :] <= q[:, None]).astype(np.float32),
        eidx=np.broadcast_to(np.arange(E, dtype=np.float32), (P, E)),
        cosT=np.cos(ang), sinT=np.sin(ang) * sign[:, None],
    )
    return {n: np.ascontiguousarray(t) for n, t in out.items()}


def kernel(**inputs):
    import concourse.bacc as bacc
    from concourse.bass_utils import run_bass_kernel_spmd

    nc = bacc.Bacc("TRN2", target_bir_lowering=False, num_devices=1)
    arrays, aps = {}, {}
    for name, v in layout(inputs).items():
        arrays[f"in_{name}_dram"] = v
        aps[name] = nc.dram_tensor(f"in_{name}_dram", v.shape, mybir.dt.from_np(v.dtype), kind="ExternalInput").ap()
    result = nc.dram_tensor("out_dram", (B * S, D), F32, kind="ExternalOutput").ap()
    build(nc, aps, result)
    r = run_bass_kernel_spmd(nc, [arrays], core_ids=[0])
    return r.results[0]["out_dram"].reshape(B, S, D)
```
